# Optimizing a Trainium2 kernel written in Bass

```python
import numpy as np
import jax
import jax.numpy as jnp

def _softmax(x, axis=-1):
    return jax.nn.softmax(x, axis=axis)

def _gelu(x):
    return jax.nn.gelu(x, approximate=True)

def _silu(x):
    return jax.nn.silu(x)

def _sigmoid(x):
    return jax.nn.sigmoid(x)

def _layernorm(x, axis=-1, eps=1e-05):
    m = jnp.mean(x, axis=axis, keepdims=True)
    v = jnp.var(x, axis=axis, keepdims=True)
    return (x - m) / jnp.sqrt(v + eps)

def _scatter_add(tgt, idx, src, axis=0):
    return tgt.at[idx].add(src)

def _segment_sum(src, seg, n):
    return jax.ops.segment_sum(src, seg, n)
kernel_name = 'mk_xattn_ffn_d2_seqx_r4_5add20'

def setup_inputs(seed: int=0):
    np.random.seed(seed)
    _w = jnp.asarray

    def _rec_inputs():
        import jax
        import jax.numpy as jnp
        _rk = jax.random.key(seed)
        x = -0.0003929 + 0.9999 * jax.random.normal(jax.random.fold_in(_rk, 1), (4, 512, 256), jnp.float32)
        _lenS = 512 - jax.random.randint(jax.random.fold_in(_rk, 7), (4,), 0, max(1, 512 // 4) + 1, jnp.int32)
        _lenS2 = 512 - jax.random.randint(jax.random.fold_in(_rk, 8), (4,), 0, max(1, 512 // 4) + 1, jnp.int32)
        _ctx_1024P = jax.random.normal(jax.random.fold_in(_rk, 11), (4, 16, 256), jnp.float32)
        _ctx_1024c = jax.random.dirichlet(jax.random.fold_in(_rk, 511), 0.3 * jnp.ones((16,), jnp.float32), (4, 512))
        _ctx_1024t = jnp.einsum('bsk,bkd->bsd', _ctx_1024c, _ctx_1024P)
        _ctx_1024t = _ctx_1024t * jax.lax.rsqrt(jnp.mean(jnp.square(_ctx_1024t)) + 1e-12) * 0.953939
        ctx_1024 = 2.81802e-05 + 1.00001 * (_ctx_1024t + 0.3 * jax.random.normal(jax.random.fold_in(_rk, 611), (4, 512, 256), jnp.float32))
        return (x, ctx_1024)
    x, ctx_1024 = _rec_inputs()

    def _L0_xattn_setup():
        import jax, jax.numpy as jnp
        import numpy as np
        EPS = 1e-08
        LN_EPS = 1e-05

        def _layernorm(x, g, b):
            mu = jnp.mean(x, axis=-1, keepdims=True)
            var = jnp.var(x, axis=-1, keepdims=True)
            return (x - mu) * jax.lax.rsqrt(var + LN_EPS) * g + b

        def _prob(x):
            x = jnp.tanh(x) * 0.499 + 0.5
            return jnp.clip(x / (jnp.sum(x, axis=-1, keepdims=True) + EPS), EPS)
        key = jax.random.key(seed)
        ks = jax.random.split(key, 8)
        B, N, D = (8, 512, 256)
        H = 4 * D
        s = 0.02
        return {'q': jax.random.normal(ks[0], (B, N, D), jnp.float32), 'k': jax.random.normal(ks[1], (B, N, D), jnp.float32), 'v': jax.random.normal(ks[2], (B, N, D), jnp.float32), 'W_diff': jax.random.normal(ks[3], (D, D), jnp.float32) * s, 'b_diff': jnp.zeros((D,), jnp.float32), 'ln_g': jnp.ones((D,), jnp.float32), 'ln_b': jnp.zeros((D,), jnp.float32), 'W1': jax.random.normal(ks[4], (H, D), jnp.float32) * s, 'b1': jnp.zeros((H,), jnp.float32), 'W2': jax.random.normal(ks[5], (D, H), jnp.float32) * s, 'b2': jnp.zeros((D,), jnp.float32)}
    _L0_xattn_all = _L0_xattn_setup()
    _L0_xattn_in = {k: v for k, v in _L0_xattn_all.items() if k in ('W_diff', 'b_diff', 'ln_g', 'ln_b', 'W1', 'b1', 'W2', 'b2')}
    del _L0_xattn_all

    def _L0_ffn_setup():
        import jax, jax.numpy as jnp
        import numpy as np
        D_IN, D_H, D_OUT = (256, 256, 256)
        D_MOE = 1024
        N_EXPERTS = 8
        TOP_K = 2
        key = jax.random.key(seed)
        ks = jax.random.split(key, 10)
        s = lambda d: 1.0 / np.sqrt(d)
        x = jax.random.normal(ks[0], (2, 512, D_IN), dtype=jnp.float32)
        W_in = jax.random.normal(ks[1], (D_IN, D_H), dtype=jnp.float32) * s(D_IN)
        b_in = jnp.zeros((D_H,), jnp.float32)
        W_gate = jax.random.normal(ks[2], (D_H, N_EXPERTS), dtype=jnp.float32) * s(D_H)
        b_gate = jnp.zeros((N_EXPERTS,), jnp.float32)
        W1 = jax.random.normal(ks[3], (N_EXPERTS, D_H, D_MOE), dtype=jnp.float32) * s(D_H)
        b1 = jnp.zeros((N_EXPERTS, D_MOE), jnp.float32)
        W2 = jax.random.normal(ks[4], (N_EXPERTS, D_MOE, D_H), dtype=jnp.float32) * s(D_MOE)
        b2 = jnp.zeros((N_EXPERTS, D_H), jnp.float32)
        W_out = jax.random.normal(ks[5], (D_H, D_OUT), dtype=jnp.float32) * s(D_H)
        b_out = jnp.zeros((D_OUT,), jnp.float32)
        return {'x': x, 'W_in': W_in, 'b_in': b_in, 'W_gate': W_gate, 'b_gate': b_gate, 'W1': W1, 'b1': b1, 'W2': W2, 'b2': b2, 'W_out': W_out, 'b_out': b_out}
    _L0_ffn_all = _L0_ffn_setup()
    _L0_ffn_in = {k: v for k, v in _L0_ffn_all.items() if k in ('W_in', 'b_in', 'W_gate', 'b_gate', 'W1', 'b1', 'W2', 'b2', 'W_out', 'b_out')}
    del _L0_ffn_all

    def _L1_xattn_setup():
        import jax, jax.numpy as jnp
        import numpy as np
        D_MODEL = 256
        HEADS = 16
        HEAD_DIM = D_MODEL // HEADS
        key = jax.random.key(seed)
        ks = jax.random.split(key, 11)
        B, S = (2, 512)
        scale = 1.0 / np.sqrt(D_MODEL)
        inp = {'q': jax.random.normal(ks[0], (B, S, D_MODEL), jnp.float32), 'k': jax.random.normal(ks[1], (B, S, D_MODEL), jnp.float32), 'v': jax.random.normal(ks[2], (B, S, D_MODEL), jnp.float32), 'Wq': jax.random.normal(ks[3], (D_MODEL, D_MODEL), jnp.float32) * scale, 'bq': jax.random.normal(ks[4], (D_MODEL,), jnp.float32) * scale, 'Wk': jax.random.normal(ks[5], (D_MODEL, D_MODEL), jnp.float32) * scale, 'bk': jax.random.normal(ks[6], (D_MODEL,), jnp.float32) * scale, 'Wv': jax.random.normal(ks[7], (D_MODEL, D_MODEL), jnp.float32) * scale, 'bv': jax.random.normal(ks[8], (D_MODEL,), jnp.float32) * scale, 'Wo': jax.random.normal(ks[9], (D_MODEL, D_MODEL), jnp.float32) * scale, 'bo': jax.random.normal(ks[10], (D_MODEL,), jnp.float32) * scale}
        return inp
    _L1_xattn_all = _L1_xattn_setup()
    _L1_xattn_in = {k: v for k, v in _L1_xattn_all.items() if k in ('Wq', 'bq', 'Wk', 'bk', 'Wv', 'bv', 'Wo', 'bo')}
    del _L1_xattn_all

    def _L1_ffn_setup():
        import jax, jax.numpy as jnp
        import numpy as np
        B, T, E, C, H, G = (2, 512, 8, 256, 512, 16)
        key = jax.random.key(seed)
        ks = jax.random.split(key, 7)
        return {'hidden_states': jax.random.normal(ks[0], (B, T, C), jnp.float32), 'w_red': jax.random.normal(ks[1], (C, G), jnp.float32) * 0.02, 'wg': jax.random.normal(ks[2], (E, G), jnp.float32), 'W1': jax.random.normal(ks[3], (E, C, H), jnp.float32) * 0.02, 'b1': jax.random.normal(ks[4], (E, H), jnp.float32) * 0.02, 'W2': jax.random.normal(ks[5], (E, H, C), jnp.float32) * 0.02, 'b2': jax.random.normal(ks[6], (E, C), jnp.float32) * 0.02}
    _L1_ffn_all = _L1_ffn_setup()
    _L1_ffn_in = {k: v for k, v in _L1_ffn_all.items() if k in ('w_red', 'wg', 'W1', 'b1', 'W2', 'b2')}
    del _L1_ffn_all
    return {'x': x, 'ctx_1024': ctx_1024, 'L0_xattn_W_diff': _L0_xattn_in['W_diff'], 'L0_xattn_b_diff': _L0_xattn_in['b_diff'], 'L0_xattn_ln_g': _L0_xattn_in['ln_g'], 'L0_xattn_ln_b': _L0_xattn_in['ln_b'], 'L0_xattn_W1': _L0_xattn_in['W1'], 'L0_xattn_b1': _L0_xattn_in['b1'], 'L0_xattn_W2': _L0_xattn_in['W2'], 'L0_xattn_b2': _L0_xattn_in['b2'], 'L0_ffn_W_in': _L0_ffn_in['W_in'], 'L0_ffn_b_in': _L0_ffn_in['b_in'], 'L0_ffn_W_gate': _L0_ffn_in['W_gate'], 'L0_ffn_b_gate': _L0_ffn_in['b_gate'], 'L0_ffn_W1': _L0_ffn_in['W1'], 'L0_ffn_b1': _L0_ffn_in['b1'], 'L0_ffn_W2': _L0_ffn_in['W2'], 'L0_ffn_b2': _L0_ffn_in['b2'], 'L0_ffn_W_out': _L0_ffn_in['W_out'], 'L0_ffn_b_out': _L0_ffn_in['b_out'], 'L1_xattn_Wq': _L1_xattn_in['Wq'], 'L1_xattn_bq': _L1_xattn_in['bq'], 'L1_xattn_Wk': _L1_xattn_in['Wk'], 'L1_xattn_bk': _L1_xattn_in['bk'], 'L1_xattn_Wv': _L1_xattn_in['Wv'], 'L1_xattn_bv': _L1_xattn_in['bv'], 'L1_xattn_Wo': _L1_xattn_in['Wo'], 'L1_xattn_bo': _L1_xattn_in['bo'], 'L1_ffn_w_red': _L1_ffn_in['w_red'], 'L1_ffn_wg': _L1_ffn_in['wg'], 'L1_ffn_W1': _L1_ffn_in['W1'], 'L1_ffn_b1': _L1_ffn_in['b1'], 'L1_ffn_W2': _L1_ffn_in['W2'], 'L1_ffn_b2': _L1_ffn_in['b2']}

def reference(x, ctx_1024, L0_xattn_W_diff, L0_xattn_b_diff, L0_xattn_ln_g, L0_xattn_ln_b, L0_xattn_W1, L0_xattn_b1, L0_xattn_W2, L0_xattn_b2, L0_ffn_W_in, L0_ffn_b_in, L0_ffn_W_gate, L0_ffn_b_gate, L0_ffn_W1, L0_ffn_b1, L0_ffn_W2, L0_ffn_b2, L0_ffn_W_out, L0_ffn_b_out, L1_xattn_Wq, L1_xattn_bq, L1_xattn_Wk, L1_xattn_bk, L1_xattn_Wv, L1_xattn_bv, L1_xattn_Wo, L1_xattn_bo, L1_ffn_w_red, L1_ffn_wg, L1_ffn_W1, L1_ffn_b1, L1_ffn_W2, L1_ffn_b2):
    import jax
    import jax.numpy as jnp

    def _L0_xattn_ref(q, k, v, W_diff, b_diff, ln_g, ln_b, W1, b1, W2, b2):
        import jax, jax.numpy as jnp
        import numpy as np
        EPS = 1e-08
        LN_EPS = 1e-05

        def _layernorm(x, g, b):
            mu = jnp.mean(x, axis=-1, keepdims=True)
            var = jnp.var(x, axis=-1, keepdims=True)
            return (x - mu) * jax.lax.rsqrt(var + LN_EPS) * g + b

        def _prob(x):
            x = jnp.tanh(x) * 0.499 + 0.5
            return jnp.clip(x / (jnp.sum(x, axis=-1, keepdims=True) + EPS), EPS)
        D = q.shape[-1]
        q_prob = _prob(q)
        k_prob = _prob(k)
        log_ratio = jnp.log(q_prob) - jnp.log(k_prob)
        sid = jnp.einsum('bnd,bmd->bnm', q_prob - k_prob, log_ratio)
        sid_sim = -sid
        attn = jax.nn.softmax(sid_sim / D ** 0.5, axis=-1)
        attn_feat = jnp.einsum('bnm,bmd->bnd', attn, v)
        f_diff = (v - attn_feat) @ W_diff.T + b_diff + q
        h = _layernorm(f_diff, ln_g, ln_b)
        mlp = jax.nn.gelu(h @ W1.T + b1, approximate=False) @ W2.T + b2
        out = mlp + f_diff
        return _layernorm(out, ln_g, ln_b)

    def _L0_ffn_ref(x, W_in, b_in, W_gate, b_gate, W1, b1, W2, b2, W_out, b_out):
        import jax, jax.numpy as jnp
        import numpy as np
        D_IN, D_H, D_OUT = (256, 256, 256)
        D_MOE = 1024
        N_EXPERTS = 8
        TOP_K = 2
        B, S, _ = x.shape
        h = x @ W_in + b_in
        t = h.reshape(B * S, -1)
        logits = t @ W_gate + b_gate
        probs = jax.nn.softmax(logits, axis=-1)
        topv, topi = jax.lax.top_k(probs, TOP_K)
        topv = topv / jnp.sum(topv, axis=-1, keepdims=True)
        route = jnp.zeros_like(probs).at[jnp.arange(t.shape[0])[:, None], topi].set(topv)
        mid = jax.nn.relu(jnp.einsum('nd,edh->neh', t, W1) + b1)
        eout = jnp.einsum('neh,ehd->ned', mid, W2) + b2
        moe_out = jnp.einsum('ne,ned->nd', route, eout)
        out = moe_out.reshape(B, S, -1) @ W_out + b_out
        return out

    def _L1_xattn_ref(q, k, v, Wq, bq, Wk, bk, Wv, bv, Wo, bo):
        import jax, jax.numpy as jnp
        import numpy as np
        D_MODEL = 256
        HEADS = 16
        HEAD_DIM = D_MODEL // HEADS
        B, S, _ = q.shape
        inv_sqrt_d = 1.0 / np.sqrt(HEAD_DIM).astype(np.float32)

        def split_heads(x):
            return x.reshape(B, S, HEADS, HEAD_DIM).transpose(0, 2, 1, 3)
        qw = split_heads(q @ Wq + bq)
        kw = split_heads(k @ Wk + bk)
        vw = split_heads(v @ Wv + bv)
        scores = jnp.einsum('bhqd,bhkd->bhqk', qw, kw) * inv_sqrt_d
        weights = jax.nn.softmax(scores, axis=-1)
        ctx = jnp.einsum('bhqk,bhkd->bhqd', weights, vw)
        ctx = ctx.transpose(0, 2, 1, 3).reshape(B, S, D_MODEL)
        return ctx @ Wo + bo

    def _L1_ffn_ref(hidden_states, w_red, wg, W1, b1, W2, b2):
        import jax, jax.numpy as jnp
        import numpy as np
        B, T, E, C, H, G = (2, 512, 8, 256, 512, 16)
        b, t, c = hidden_states.shape
        x = hidden_states.reshape(-1, c)
        x_red = x @ w_red
        wg_n = wg / jnp.maximum(jnp.linalg.norm(wg, axis=1, keepdims=True), 0.0001)
        logits = x_red @ wg_n.T
        gates = jax.nn.softmax(logits, axis=1)
        scores = jnp.max(gates, axis=1)
        idx = jnp.argmax(gates, axis=1)
        h = jnp.einsum('nc,ech->neh', x, W1) + b1[None]
        h = jnp.take_along_axis(h, idx[:, None, None], axis=1)[:, 0, :]
        h = jax.nn.gelu(h, approximate=False)
        o = jnp.einsum('nh,ehc->nec', h, W2) + b2[None]
        o = jnp.take_along_axis(o, idx[:, None, None], axis=1)[:, 0, :]
        o = o * scores[:, None]
        return o.reshape(b, t, c)
    x = x + _L0_xattn_ref(_layernorm(x, axis=-1), ctx_1024, ctx_1024, L0_xattn_W_diff, L0_xattn_b_diff, L0_xattn_ln_g, L0_xattn_ln_b, L0_xattn_W1, L0_xattn_b1, L0_xattn_W2, L0_xattn_b2)
    x = x + _L0_ffn_ref(_layernorm(x, axis=-1), L0_ffn_W_in, L0_ffn_b_in, L0_ffn_W_gate, L0_ffn_b_gate, L0_ffn_W1, L0_ffn_b1, L0_ffn_W2, L0_ffn_b2, L0_ffn_W_out, L0_ffn_b_out)
    x = x + _L1_xattn_ref(_layernorm(x, axis=-1), ctx_1024, ctx_1024, L1_xattn_Wq, L1_xattn_bq, L1_xattn_Wk, L1_xattn_bk, L1_xattn_Wv, L1_xattn_bv, L1_xattn_Wo, L1_xattn_bo)
    x = x + _L1_ffn_ref(_layernorm(x, axis=-1), L1_ffn_w_red, L1_ffn_wg, L1_ffn_W1, L1_ffn_b1, L1_ffn_W2, L1_ffn_b2)
    return x

_drawn_inputs = setup_inputs


def setup_inputs(seed=0):
    import zlib

    import numpy as np

    out = dict(_drawn_inputs(seed))
    spreads = {'L0_xattn_b_diff': (0.0, 0.1),
     'L0_xattn_ln_g': (1.0, 0.2),
     'L0_xattn_ln_b': (0.0, 0.1),
     'L0_xattn_b1': (0.0, 0.27),
     'L0_xattn_b2': (0.0, 0.1),
     'L0_ffn_b_in': (0.0, 0.1),
     'L0_ffn_b_gate': (0.0, 0.1),
     'L0_ffn_b1': (0.0, 0.333),
     'L0_ffn_b2': (0.0, 0.1),
     'L0_ffn_b_out': (0.0, 0.1)}
    factors = {'L1_xattn_bq': 8.0,
     'L1_xattn_bk': 8.0,
     'L1_ffn_w_red': 8.0,
     'L1_ffn_wg': 8.0,
     'L1_ffn_W1': 8.0,
     'L1_ffn_b1': 8.0,
     'L1_ffn_W2': 8.0,
     'L1_ffn_b2': 8.0}
    for name, (base, spread) in spreads.items():
        noise = np.random.default_rng([zlib.crc32(name.encode()), seed]).standard_normal(out[name].shape)
        drawn = base * np.exp(spread * noise) if base else spread * noise
        out[name] = jnp.asarray(drawn.astype(out[name].dtype))
    for name, factor in factors.items():
        out[name] = (out[name] * factor).astype(out[name].dtype)
    return out
```

```python
import numpy as np
import concourse.bass as bass
from concourse import mybir
from contextlib import ExitStack

F32 = mybir.dt.float32
F32R = mybir.dt.float32r
F16 = mybir.dt.float16
I32 = mybir.dt.int32
U32 = mybir.dt.uint32
ALU = mybir.AluOpType
ACT = mybir.ActivationFunctionType
AX = mybir.AxisListType

NB, TB, P, D = 4, 4, 128, 256
NT = NB * TB
S = 512
E = 8
TOK = 256
SUB = TOK // P
N0 = (2 * NT * P + E * (TOK - 1)) // TOK
N1 = (NT * P + E * (TOK - 1)) // TOK
H0, H1 = 1024, 512
NH, HD = 16, 16
WS = 64.0


class Queue:

    def __init__(self, sem):
        self.sem, self.n, self.items = sem, 0, []

    def __call__(self, fn, *waits, inc=True):
        self.items.append((fn, flat(waits), inc))
        if inc:
            self.n += 1
            return (self.sem, self.n)
        return None

    def last(self):
        return (self.sem, self.n)

    def play(self, eng):
        seen = {}
        for fn, waits, inc in self.items:
            for sem, value in waits:
                if value > seen.get(sem.name, 0):
                    eng.wait_ge(sem, value)
                    seen[sem.name] = value
            made = fn(eng)
            if inc:
                made.then_inc(self.sem, 1)


def flat(waits):
    out = []
    for w in waits:
        if w is None:
            continue
        if isinstance(w, list):
            out += flat(w)
        else:
            out.append(w)
    return out


class Buf:

    def __init__(self, ap, rel=None):
        self.ap, self.rel = ap[(slice(None),) * len(ap.shape)], rel or []


class Ring:
    def __init__(self, aps):
        self.bufs, self.at = [Buf(a) for a in aps], 0

    def take(self):
        b = self.bufs[self.at % len(self.bufs)]
        self.at += 1
        return b


def build(nc, a, out, stop=4):
    ctx = ExitStack()
    with ctx:
        base = [nc.sbuf_base + (-nc.sbuf_base) % 64]
        names = [0]

        def at(off, shape, dt=F32):
            names[0] += 1
            return nc.alloc_sbuf_tensor_at(f"t{names[0]}", shape, dt, offset=off)

        def size(shape, dt):
            n = 2 if dt == F16 else 4
            for s in shape[1:]:
                n *= s
            return n + (-n) % 32

        class Zone:
            def __init__(self, start, length):
                self.start, self.end, self.at = start, start + length, start

            def __call__(self, *shape, dt=F32):
                t = at(self.at, list(shape), dt)
                self.at += size(shape, dt)
                assert self.at <= self.end, (shape, self.at - self.end)
                return t

            def reset(self):
                self.at = self.start

        class Zones:

            def __init__(self, *zones):
                self.zones = zones

            def __call__(self, *shape, dt=F32):
                n = size(shape, dt)
                for z in self.zones:
                    if z.at + n <= z.end:
                        return z(*shape, dt=dt)
                raise AssertionError(("no room", shape, [z.end - z.at for z in self.zones]))

        def sem(name):
            return ctx.enter_context(nc.semaphore(name))

        K = 1024
        b0 = base[0]
        PZ = Zone(b0, 40 * K)
        WA = Zone(PZ.end, 20 * K)
        SZ = Zone(WA.end, 19 * K)
        MZ = Zone(SZ.end, 128 * K)
        assert MZ.end <= nc.sbuf_usable_end, (MZ.end, nc.sbuf_usable_end)

        T = Queue(sem("s_pe"))
        V = Queue(sem("s_dve"))
        A = Queue(sem("s_act"))
        G = Queue(sem("s_pool"))
        Y = Queue(None)
        chans = {}

        def dma(q, name, o, i, *waits):
            if name not in chans:
                chans[name] = [sem("d_" + name), 0]
            c = chans[name]
            c[1] += 16
            s, v = c[0], c[1]
            q(lambda e: e.dma_start(o, i).then_inc(s, 16), *waits, inc=False)
            return (s, v)

        def everyone():
            return [T.last(), V.last(), A.last(), G.last()] + [(c[0], c[1]) for c in chans.values()]

        PB = [ctx.enter_context(nc.psum_tensor(f"pb{i}", [128, 1024], F32)) for i in range(4)]

        def banks(ids):
            return Ring([PB[i // 2][:, i % 2 * 512:i % 2 * 512 + 512] for i in ids])

        def pairs(ids):
            return Ring([PB[i][:, :] for i in ids])

        def held(rings, toks):
            for r in rings:
                for b in r.bufs:
                    b.rel = toks

        X = PZ(128, NT, D)
        ident = PZ(128, 128)
        identh = PZ(128, 128, dt=F16)
        bc = PZ(128, 7, D)
        bgate = PZ(128, E)
        Win = PZ(128, 2, D)
        bin_ = PZ(128, D)
        Wg = PZ(128, 2, E)
        Wout = PZ(128, 2, D)
        Wqkv = PZ(128, 4, 2, D)
        wred = PZ(128, 2, 16)
        wg8 = PZ(8, 16)
        pp = PZ(128, 16)
        b1m = PZ(128, 64)
        U = PZ(128, 128)
        ones = PZ(128, 128)
        io8 = PZ(128, E)
        ioj = PZ(128, 32)
        W1T = WA(128, 2, H0)
        W2T = WA(128, 8, D)
        WdT = WA(128, 2, D)
        lng, lnb, bdiff, b2a, bout, bo, bv = (bc[:, i, :] for i in range(7))

        ld = {}
        ld["ident"] = dma(Y, "ident", ident[:, :], a["ident"])
        xv = a["x"].rearrange("b (t p) d -> b p t d", p=128)
        cv = a["ctx_1024"].rearrange("b (t p) d -> b p t d", p=128)
        tx = [dma(Y, f"x{b}", X[:, 4 * b:4 * b + 4, :], xv[b]) for b in range(NB)]

        def bcast(n):
            return a[n].partition_broadcast(128)

        def loads_a():
            dma(Y, "wa", WdT[:, :, :], a["WdT"])
            dma(Y, "wa", W1T[:, :, :], a["W1T"])
            dma(Y, "wa", W2T[:, :, :], a["W2T"])
            dma(Y, "wa", pp[:, :], a["pp"])
            for i, n in enumerate(["L0_xattn_ln_g", "L0_xattn_ln_b", "L0_xattn_b_diff", "L0_xattn_b2", "L0_ffn_b_out",
                                   "L1_xattn_bo", "L1_xattn_bv"]):
                t = dma(Y, "wa", bc[:, i, :], bcast(n))
            return t

        def loads_b():
            dma(Y, "wb", Win[:, :, :], a["Win"])
            dma(Y, "wb", bin_[:, :], bcast("L0_ffn_b_in"))
            dma(Y, "wb", Wg[:, :, :], a["Wg"])
            dma(Y, "wb", bgate[:, :], bcast("L0_ffn_b_gate"))
            dma(Y, "wb", U[:, :], a["U"])
            dma(Y, "wb", io8[:, :], a["io8"])
            dma(Y, "wb", ioj[:, :], a["ioj"])
            dma(Y, "wb", Wout[:, :, :], a["Wout"])
            return dma(Y, "wb", b1m[:, :], a["b1m0"])

        t_oneset = V(lambda e: e.memset(ones[:, :], 1.0))
        t_idh = V(lambda e: e.tensor_copy(identh[:, :], ident[:, :]), ld["ident"])

        def vts(o, i, s1, s2, o0, o1, *w):
            return V(lambda e: e.tensor_scalar(o, i, s1, s2, o0, o1), *w)

        def vtt(o, x, y, op, *w, q=None):
            return (q or V)(lambda e: e.tensor_tensor(o, x, y, op), *w)

        def vstt(o, x, s, y, o0, o1, *w):
            return V(lambda e: e.scalar_tensor_tensor(out=o, in0=x, scalar=s, in1=y, op0=o0, op1=o1), *w)

        def vcopy(o, i, *w):
            return V(lambda e: e.tensor_copy(o, i), *w)

        def act(o, i, f, *w, bias=0.0, scale=1.0, accum=None):
            if accum is None:
                return A(lambda e: e.activation(o, i, f, bias=bias, scale=scale), *w)
            return A(lambda e: e.activation(o, i, f, bias=bias, scale=scale, accum_out=accum), *w)

        def acopy(o, i, *w):
            return act(o, i, ACT.Copy, *w)

        def mm(o, l, r, st, sp, *w, inc=False, skip=False):
            return T(lambda e: e.matmul(o, l, r, start=st, stop=sp, skip_group_check=skip), *w, inc=inc)

        def tr(o, i, idn, *w, inc=False):
            return T(lambda e: e.transpose(o, i, idn), *w, inc=inc)

        smalls = []

        def rsqrt(v, n, tmp, *w, parts=128):
            y, i1, t1, hv = (tmp[0:parts, k * n:(k + 1) * n] for k in range(4))
            c = V(lambda e: e.tensor_single_scalar(i1.bitcast(I32), v.bitcast(I32), 1, ALU.logical_shift_right), *w)
            vts(hv, v, -0.5, None, ALU.mult, ALU.bypass)
            c = V(lambda e: e.tensor_scalar(y.bitcast(I32), i1.bitcast(I32), -1.0, float(0x5f3759df), ALU.mult, ALU.add), c)
            for _ in range(4):
                c = vtt(t1, y, hv, ALU.mult, c)
                c = vtt(t1, t1, y, ALU.mult, c)
                c = vstt(y, t1, 1.5, y, ALU.add, ALU.mult, c)
            return y, c

        def ln_stats(tiles, zone, *w):
            n = len(tiles)
            st, mv, ve, tmp = zone(128, n, 6), zone(128, n, 2), zone(128, n), zone(128, 4 * n)
            for i, t in enumerate(tiles):
                wi = w[0][i] if isinstance(w[0], list) and len(w[0]) == n and len(w) == 1 else list(w)
                s = V(lambda e, i=i, t=t: e.bn_stats(st[:, i, :], t), wi)
            for i in range(n):
                g = V(lambda e, i=i: e.bn_aggr(mv[:, i, :], st[:, i, :]), s)
            c = vts(ve[:, :], mv[:, :, 1], 1e-5, None, ALU.add, ALU.bypass, g)
            y, c = rsqrt(ve[:, :], n, tmp[:, :], c)
            return [(mv[:, i, 0:1], y[:, i:i + 1]) for i in range(n)], c

        t_wa = loads_a()
        t_wb = loads_b()

        LNZ = Zone(SZ.start, 8 * K)
        CT = [Buf(MZ(128, 4, D + 1)) for _ in range(2)]
        Q = [Buf(MZ(128, 4, D)) for _ in range(2)]
        TQ, TC, LQ, LC = (Buf(MZ(128, 4, D)) for _ in range(4))
        DT = [Buf(MZ(128, 2, S)) for _ in range(2)]
        LT = [Buf(MZ(128, 2, S)) for _ in range(2)]
        ET = [Buf(MZ(128, 4, S)) for _ in range(2)]
        UB = Ring([MZ(128, D)[:, :] for _ in range(2)])
        UT = Ring([MZ(128, 2, 128)[:, :, :] for _ in range(2)])
        HT = [Buf(MZ(128, 2, S)) for _ in range(2)]
        GT = Ring([MZ(128, S)[:, :] for _ in range(16)])
        XB = [Buf(MZ(128, 4, D))]
        bT, bS, bY = banks([0, 1]), banks([2, 3, 4]), banks([5, 6, 7])
        t_neg = [V(lambda e, c=c: e.memset(c.ap[:, :, D:D + 1], -1.0)) for c in CT]
        st = {}

        def transpose4(ring, tiles, evac, *w):
            k = ring.take()
            for i, t in enumerate(tiles):
                tok = tr(k.ap[:, i * 128:(i + 1) * 128], t, ident[:, :], k.rel, ld["ident"], *w, inc=i == len(tiles) - 1)
            tok = evac(k.ap, tok)
            k.rel = [tok]
            return tok

        def pre(b):
            ct, q = CT[b % 2], Q[b % 2]
            tc = dma(Y, f"c{b % 2}", ct.ap[:, :, 0:D], cv[b], ct.rel)
            sc, tk = ln_stats([X[:, 4 * b + t, :] for t in range(4)], LNZ, tx[b])
            for t in range(4):
                tq = vts(q.ap[:, t, :], X[:, 4 * b + t, :], *sc[t], ALU.subtract, ALU.mult, tk, q.rel)
            sums, r = LNZ(128, 8), LNZ(128, 24)
            for t in range(4):
                act(TQ.ap[:, t, :], q.ap[:, t, :], ACT.Tanh, tq, TQ.rel, accum=sums[:, t:t + 1])
            for t in range(4):
                th = act(TC.ap[:, t, :], ct.ap[:, t, 0:D], ACT.Tanh, tc, TC.rel, accum=sums[:, 4 + t:5 + t])
            c = vts(r[:, 0:8], sums[:, :], 0.499, 128.0 + 1e-8, ALU.mult, ALU.add, th)
            c = V(lambda e: e.reciprocal(r[:, 0:8], r[:, 0:8]), c)
            vts(r[:, 8:16], r[:, 0:8], 0.499, None, ALU.mult, ALU.bypass, c)
            c = vts(r[:, 16:24], r[:, 0:8], 0.5, None, ALU.mult, ALU.bypass, c)
            for src, dst, o in ((TQ, LQ, 0), (TC, LC, 4)):
                for t in range(4):
                    tl = act(dst.ap[:, t, :], src.ap[:, t, :], ACT.Ln, c, dst.rel,
                             scale=r[:, 8 + o + t:9 + o + t], bias=r[:, 16 + o + t:17 + o + t])
            for src, o in ((TQ, 0), (TC, 4)):
                for t in range(4):
                    tp = vts(src.ap[:, t, :], src.ap[:, t, :], r[:, 8 + o + t:9 + o + t], r[:, 16 + o + t:17 + o + t],
                             ALU.mult, ALU.add, tl)
            tr_ = vtt(LQ.ap[:, :, :], LQ.ap[:, :, :], LC.ap[:, :, :], ALU.subtract, tl, q=G)
            td = vtt(TQ.ap[:, :, :], TQ.ap[:, :, :], TC.ap[:, :, :], ALU.subtract, tp)
            TC.rel, LC.rel = [td], [tr_]
            for c in range(2):
                e1 = transpose4(bT, [TQ.ap[:, t, c * 128:(c + 1) * 128] for t in range(4)],
                                lambda k, tok, c=c: vcopy(DT[b % 2].ap[:, c, :], k, tok, DT[b % 2].rel), td)
                e2 = transpose4(bT, [LQ.ap[:, t, c * 128:(c + 1) * 128] for t in range(4)],
                                lambda k, tok, c=c: acopy(LT[b % 2].ap[:, c, :], k, tok, LT[b % 2].rel), tr_)
            TQ.rel, LQ.rel = [T.last()], [T.last()]
            tqb = vtt(q.ap[:, :, :], q.ap[:, :, :], bdiff.unsqueeze(1).to_broadcast([128, 4, D]), ALU.add, t_wa, th, tq, q=G)
            txb = vtt(X[:, 4 * b:4 * b + 4, :], X[:, 4 * b:4 * b + 4, :], lnb.unsqueeze(1).to_broadcast([128, 4, D]),
                      ALU.add, t_wa, tq, q=G)
            st[b] = dict(tc=tc, e=[e1, e2], tqb=tqb, txb=txb)

        def s_exp(b):
            s = st[b]
            for mc in range(4):
                k = bS.take()
                for c in range(2):
                    tok = mm(k.ap, LT[b % 2].ap[:, c, mc * 128:(mc + 1) * 128], DT[b % 2].ap[:, c, :], c == 0, c == 1,
                             s["e"], k.rel, inc=c == 1)
                te = act(ET[b % 2].ap[:, mc, :], k.ap, ACT.Exp, tok, ET[b % 2].rel, scale=-1.0 / 16)
                k.rel = [te]
            DT[b % 2].rel = LT[b % 2].rel = [tok]
            s["te"] = te

        def rest(b):
            s, ct, q = st[b], CT[b % 2], Q[b % 2]
            rinv = LNZ(128, 4)
            tf, us = [], []
            for t in range(4):
                k = bY.take()
                for mc in range(4):
                    tok = mm(k.ap[:, 0:D + 1], ET[b % 2].ap[:, mc, t * 128:(t + 1) * 128], ct.ap[:, mc, :], mc == 0, mc == 3,
                             s["te"], s["tc"], t_neg, k.rel, inc=mc == 3)
                u = UB.take()
                c = V(lambda e, k=k, t=t: e.reciprocal(rinv[:, t:t + 1], k.ap[:, D:D + 1]), tok)
                c = vstt(u.ap, k.ap[:, 0:D], rinv[:, t:t + 1], ct.ap[:, t, 0:D], ALU.mult, ALU.add, c, u.rel)
                k.rel = [c]
                us.append((u, c))
                if t % 2 == 1:
                    yield
                    for tt in (t - 1, t):
                        u, c = us[tt]
                        kt = bT.take()
                        for cc in range(2):
                            tok = tr(kt.ap[:, cc * 128:(cc + 1) * 128], u.ap[:, cc * 128:(cc + 1) * 128], ident[:, :], c,
                                     kt.rel, inc=cc == 1)
                        u.rel = [tok]
                        ut = UT.take()
                        ev = acopy(ut.ap, kt.ap[:, 0:256].rearrange("p (c n) -> p c n", c=2), tok, ut.rel)
                        kt.rel = [ev]
                        ky = bY.take()
                        for cc in range(2):
                            tok = mm(ky.ap[:, 0:D], ut.ap[:, cc, :], WdT[:, cc, :], cc == 0, cc == 1, ev, t_wa, ky.rel,
                                     inc=cc == 1)
                        ut.rel = [tok]
                        f = vtt(q.ap[:, tt, :], ky.ap[:, 0:D], q.ap[:, tt, :], ALU.add, tok, s["tqb"])
                        ky.rel = [f]
                        tf.append(f)
                        yield
            ET[b % 2].rel = [tok]
            ct.rel = [T.last(), V.last()]
            sc, tk = ln_stats([q.ap[:, t, :] for t in range(4)], LNZ, tf)
            z = UZ[b % 2]
            for t in range(4):
                tz = vts(z.ap[:, t, :], q.ap[:, t, :], *sc[t], ALU.subtract, ALU.mult, tk, z.rel)
            tfb = vtt(q.ap[:, :, :], q.ap[:, :, :], b2a.unsqueeze(1).to_broadcast([128, 4, D]), ALU.add, tz, q=G)
            yield
            for c in range(2):
                eh = transpose4(bT, [z.ap[:, t, c * 128:(c + 1) * 128] for t in range(4)],
                                lambda k, tok, c=c: vts(HT[b % 2].ap[:, c, :], k, pp[:, c:c + 1], pp[:, 2 + c:3 + c],
                                                        ALU.mult, ALU.add, tok, HT[b % 2].rel), tz)
            z.rel = [T.last()]
            s["eh"], s["tfb"] = eh, tfb
            yield

        def mlp(b):
            s, q = st[b], Q[b % 2]
            gts = []
            for hc in range(8):
                k, g = bS.take(), GT.take()
                for c in range(2):
                    tok = mm(k.ap, W1T[:, c, hc * 128:(hc + 1) * 128], HT[b % 2].ap[:, c, :], c == 0, c == 1, s["eh"],
                             k.rel, inc=c == 1)
                tg = act(g.ap, k.ap, ACT.Gelu, tok, g.rel, bias=pp[:, 4 + hc:5 + hc])
                k.rel = [tg]
                gts.append((g, tg))
                yield
            HT[b % 2].rel = [tok]
            to = []
            for t in range(4):
                k = bY.take()
                for hc in range(8):
                    g, tg = gts[hc]
                    tok = mm(k.ap[:, 0:D], g.ap[:, t * 128:(t + 1) * 128], W2T[:, hc, :], hc == 0, hc == 7, tg, k.rel,
                             inc=hc == 7)
                    if t == 3:
                        g.rel = [(T.sem, T.n + (hc < 7))]
                o = vtt(q.ap[:, t, :], k.ap[:, 0:D], q.ap[:, t, :], ALU.add, tok, s["tfb"])
                k.rel = [o]
                to.append(o)
                yield
            sc, tk = ln_stats([q.ap[:, t, :] for t in range(4)], LNZ, to)
            z = XB[0]
            for t in range(4):
                tz = vts(z.ap[:, t, :], q.ap[:, t, :], *sc[t], ALU.subtract, ALU.mult, tk, z.rel)
            q.rel = [tz]
            tm = vtt(z.ap[:, :, :], z.ap[:, :, :], lng.unsqueeze(1).to_broadcast([128, 4, D]), ALU.mult, tz)
            s["x1"] = vtt(X[:, 4 * b:4 * b + 4, :], X[:, 4 * b:4 * b + 4, :], z.ap[:, :, :], ALU.add, tm, s["txb"])
            z.rel = [s["x1"]]
            yield

        UZ = [Buf(MZ(128, 4, D)) for _ in range(1)] * 2

        def weave(*gens):
            gens = [g for g in gens if g is not None]
            while gens:
                for g in list(gens):
                    if next(g, gens) is gens:
                        gens.remove(g)

        for b in range(NB):
            pre(b)
            s_exp(b)
            weave(rest(b), mlp(b - 1) if b else None)
        weave(mlp(NB - 1))

        def finish():
            ov = out.rearrange("b (t p) d -> p (b t) d", p=128)
            t = dma(Y, "out", ov, X[:, :, :], everyone())
            Y(lambda e: e.wait_ge(*t), inc=False)

        def emit():
            block = ctx.enter_context(nc.Block())

            @block.sync
            def _(eng):
                Y.play(eng)

            @block.gpsimd
            def _(eng):
                G.play(eng)

            @block.scalar
            def _(eng):
                A.play(eng)

            @block.vector
            def _(eng):
                V.play(eng)

            @block.tensor
            def _(eng):
                T.play(eng)

        if stop == 1:
            finish()
            emit()
            return


        bar = everyone()
        buf0 = nc.dram_tensor("buf0", (N0 * TOK, 2 * D), F16, kind="Internal").ap()
        obuf0 = nc.dram_tensor("obuf0", (N0 * TOK, D), F32, kind="Internal").ap()

        def zero_rows(buf, n, zone, *w):
            zt = zone(128, 2 * D, dt=F16)
            tz = V(lambda e: e.memset(zt[:, :], 0.0), *w)
            return dma(Y, buf.tensor.name, buf.rearrange("(j p) d -> p j d", p=128),
                       zt[:, :].unsqueeze(1).to_broadcast([128, n * SUB, 2 * D]), tz)

        class Weights:

            def __init__(self, zone, e1, e2):
                self.w1h, self.w1l = zone(128, e1, dt=F16), zone(128, e1, dt=F16)
                self.w2h, self.w2l = zone(128, e2, dt=F16), zone(128, e2, dt=F16)
                self.t1, self.t2 = [], []

        CH = 1024

        def split_weights(src, hi, lo, n, ring, tag, *w):
            toks = []
            for i in range(n // CH):
                s = ring.take()
                r = slice(i * CH, (i + 1) * CH)
                td = dma(Y, f"{tag}{ring.at % len(ring.bufs)}", s.ap, src[:, r], s.rel, *w)
                th = act(hi[:, r], s.ap, ACT.Copy, td, *w, scale=WS)
                tl = vstt(lo[:, r], s.ap, WS, hi[:, r], ALU.mult, ALU.subtract, th, td)
                s.rel = [tl]
                toks = [tl]
                yield
            return toks

        def routing(ns, idx, nt_max, zone, *w):
            O = [zone(128, NT, E) for _ in range(ns)]
            M = O[0] if ns == 1 else zone(128, NT, E)
            C = [zone(128, NT, E) for _ in range(2)]
            tot, tmp = zone(128, NT, E), zone(128, NT, E)
            sm, smi, cmp, tef = zone(128, 6, E), zone(128, E), zone(1, nt_max, E), zone(1, nt_max)
            tei = [zone(1, nt_max) for _ in range(3)]
            pf, pi = zone(128, ns, NT), zone(128, ns, NT)
            io = io8[:, :].unsqueeze(1).to_broadcast([128, NT, E])
            for s in range(ns):
                c = vtt(O[s][:, :, :], io, idx[:, s, :].unsqueeze(2).to_broadcast([128, NT, E]), ALU.is_equal, *w)
            if ns == 2:
                c = vtt(M[:, :, :], O[0][:, :, :], O[1][:, :, :], ALU.add, c)
            m2 = M[:, :, :].rearrange("p t e -> p (t e)")
            k1, k2 = bY.take(), bY.take()
            mm(k1.ap[:, 0:128], U[:, :], m2, True, True, c, k1.rel, *w)
            tp = mm(k2.ap[:, 0:128], ones[:, :], m2, True, True, k2.rel, t_oneset, inc=True)
            c = vcopy(tot[:, :, :], k2.ap[:, 0:128].rearrange("p (t e) -> p t e", e=E), tp)
            k2.rel = [c]
            cur = tot
            for i, sh in enumerate((1, 2, 4, 8)):
                nx = C[i % 2]
                vcopy(nx[:, 0:sh, :], cur[:, 0:sh, :], c)
                c = vtt(nx[:, sh:, :], cur[:, sh:, :], cur[:, 0:NT - sh, :], ALU.add, c)
                cur = nx
            V(lambda e: e.tensor_scalar(smi[:, :].bitcast(I32), cur[:, NT - 1, :], float(TOK - 1), None, ALU.add, ALU.bypass), c)
            c = V.last()
            c = V(lambda e: e.tensor_single_scalar(smi[:, :].bitcast(I32), smi[:, :].bitcast(I32), 8, ALU.logical_shift_right), c)
            c = vcopy(sm[:, 0, :], smi[:, :].bitcast(I32), c)
            p = 0
            for i, sh in enumerate((1, 2, 4)):
                vcopy(sm[:, i + 1, 0:sh], sm[:, p, 0:sh], c)
                c = vtt(sm[:, i + 1, sh:], sm[:, p, sh:], sm[:, p, 0:E - sh], ALU.add, c)
                p = i + 1
            vtt(sm[:, 4, :], sm[:, 3, :], sm[:, 0, :], ALU.subtract, c)
            ce = vtt(cmp[:, :, :], sm[0:1, 3, :].unsqueeze(1).to_broadcast([1, nt_max, E]),
                     ioj[0:1, 0:nt_max].unsqueeze(2).to_broadcast([1, nt_max, E]), ALU.is_le, c)
            ce = V(lambda e: e.tensor_reduce(tef[:, :], cmp[:, :, :], AX.X, ALU.add), ce)
            return O, M, C, cur, tot, tmp, sm, k1, ce, tef, tei, pf, pi, c

        def positions(ns, r, hc):
            O, M, C, cur, tot, tmp, sm, k1, ce, tef, tei, pf, pi, c = r
            n2 = 2 * hc * 128
            vts(tei[0][:, :].bitcast(I32), tef[:, :], float(E - 1), float(n2), ALU.min, ALU.mult, ce)
            vts(tei[1][:, :].bitcast(I32), tef[:, :], float(E - 1), float(hc), ALU.min, ALU.mult, ce)
            te = vts(tei[2][:, :].bitcast(I32), tef[:, :], float(E - 1), float(D), ALU.min, ALU.mult, ce)
            c = vtt(tmp[:, :, :], cur[:, :, :], tot[:, :, :], ALU.subtract, c)
            c = vtt(tmp[:, :, :], k1.ap[:, 0:128].rearrange("p (t e) -> p t e", e=E), tmp[:, :, :], ALU.add, c)
            k1.rel = [c]
            c = vstt(tmp[:, :, :], sm[:, 4, :].unsqueeze(1).to_broadcast([128, NT, E]), float(TOK), tmp[:, :, :],
                     ALU.mult, ALU.add, c)
            for s in range(ns):
                o = C[s % 2]
                c2 = vtt(o[:, :, :], O[s][:, :, :], tmp[:, :, :], ALU.mult, c)
                c2 = V(lambda e, s=s, o=o: e.tensor_reduce(pf[:, s, :], o[:, :, :], AX.X, ALU.add), c2)
                c2 = vcopy(pi[:, s, :].bitcast(U32), pf[:, s, :], c2)
            return pi, tei, te, c2

        def scatter(buf, rows, pi, ns, tag, *w):
            for t in range(NT):
                for s in range(ns):
                    name = tag
                    chans.setdefault(name, [sem("d_" + name) if name not in chans else chans[name][0], 0])
                    ch = chans[name]
                    ch[1] += 16
                    G(lambda e, t=t, s=s, ch=ch: e.indirect_dma_start(
                        out=buf, out_offset=bass.IndirectOffsetOnAxis(ap=pi[:, s, t:t + 1].bitcast(U32), axis=0),
                        in_=rows[:, t, :], in_offset=None).then_inc(ch[0], 16), *w, inc=False)
            return (ch[0], ch[1])

        def experts(zone, buf, obuf, n, HC, W, func, b1m, b2m, tei, tag, *w):
            xr = Ring([zone(128, SUB, 2 * D, dt=F16) for _ in range(2)])
            xt = Ring([zone(128, 4, TOK, dt=F16) for _ in range(2)])
            m32 = Ring([zone(128, 2, TOK) for _ in range(2)])
            mh = Ring([zone(128, 2, TOK, dt=F16) for _ in range(HC // 2 + 2)])
            ml = Ring([zone(128, 2, TOK, dt=F16) for _ in range(HC // 2 + 2)])
            ob = Ring([zone(128, SUB, D) for _ in range(2)])
            bX, bU, bD = banks([0, 1]), banks([2, 3, 4]), banks([5, 6, 7])
            for r_ in (bX, bU, bD):
                for bb in r_.bufs:
                    bb.rel = flat(w)
            bv_ = buf.rearrange("(j s p) d -> j p s d", p=128, s=SUB)
            ov_ = obuf.rearrange("(j s p) d -> j p s d", p=128, s=SUB)
            regs = {}

            def reg(q, key, src, top):
                def go(e):
                    regs[key] = e.value_load(src, min_val=0, max_val=top)
                q(go, *w, inc=False)

            def load(j):
                x = xr.take()
                td = dma(Y, f"{tag}x{xr.at % 2}", x.ap, bv_[j], x.rel, *w)
                k = bX.take()
                kh = k.ap.bitcast(F16).rearrange("p (c n) -> p c n", c=4)
                for s in range(SUB):
                    for c in range(4):
                        tok = tr(kh[:, c, s * 128:(s + 1) * 128], x.ap[:, s, c * 128:(c + 1) * 128], identh[:, :], td,
                                 t_idh, k.rel, inc=s == SUB - 1 and c == 3)
                x.rel = [tok]
                xx = xt.take()
                ev = vcopy(xx.ap, kh, tok, xx.rel)
                k.rel = [ev]
                return xx, ev

            nxt = load(0)
            tout = None
            for j in range(n):
                xx, ev = nxt
                reg(T, ("t", j), tei[0][0:1, j:j + 1].bitcast(I32), (E - 1) * 2 * HC * 128)
                reg(A, ("a", j), tei[1][0:1, j:j + 1].bitcast(I32), (E - 1) * HC)
                reg(V, ("v", j), tei[2][0:1, j:j + 1].bitcast(I32), (E - 1) * D)
                mids = []
                for g in range(HC // 2):
                    k = bU.take()
                    for h2 in range(2):
                        hc = 2 * g + h2
                        o = k.ap[:, h2 * TOK:(h2 + 1) * TOK]
                        seq = [(W.w1h, c, c) for c in range(2)] + [(W.w1h, c, 2 + c) for c in range(2)] + \
                              [(W.w1l, c, c) for c in range(2)]
                        for i, (ww, c, xc) in enumerate(seq):
                            off = c * HC * 128 + hc * 128
                            tok = T(lambda e, o=o, ww=ww, off=off, xx=xx, xc=xc, i=i, j=j: e.matmul(
                                o, ww[:, bass.ds(regs["t", j] + off, 128)], xx.ap[:, xc, :], start=i == 0, stop=i == 5),
                                ev, k.rel, W.t1, inc=i == 5)
                    m = m32.take()
                    for h2 in range(2):
                        hc = 2 * g + h2
                        ta = A(lambda e, m=m, k=k, h2=h2, hc=hc, j=j: e.activation(
                            m.ap[:, h2, :], k.ap[:, h2 * TOK:(h2 + 1) * TOK], func,
                            bias=b1m[:, bass.ds(regs["a", j] + hc, 1)], scale=1.0 / WS), tok, m.rel)
                    k.rel = [ta]
                    h, l = mh.take(), ml.take()
                    th = vcopy(h.ap, m.ap, ta, h.rel)
                    tl = vtt(l.ap, m.ap, h.ap, ALU.subtract, th, l.rel)
                    m.rel = [tl]
                    mids.append((h, l, tl))
                xx.rel = [tok]
                if j + 1 < n:
                    nxt = load(j + 1)
                o2 = ob.take()
                for s in range(SUB):
                    k = bD.take()
                    i, last = 0, HC * 3 - 1
                    for hc in range(HC):
                        h, l, tl = mids[hc // 2]
                        for src, ww in ((h, W.w2h), (l, W.w2h), (h, W.w2l)):
                            tok = T(lambda e, k=k, src=src, hc=hc, s=s, ww=ww, i=i, j=j, last=last: e.matmul(
                                k.ap[:, 0:D], src.ap[:, hc % 2, s * 128:(s + 1) * 128],
                                ww[:, bass.ds(regs["t", j] + hc * D, D)], start=i == 0, stop=i == last),
                                tl, k.rel, W.t2, inc=i == last)
                            i += 1
                    tv = V(lambda e, o2=o2, k=k, s=s, j=j: e.scalar_tensor_tensor(
                        out=o2.ap[:, s, :], in0=k.ap[:, 0:D], scalar=1.0 / WS,
                        in1=b2m[:, bass.ds(regs["v", j], D)], op0=ALU.mult, op1=ALU.add), tok, o2.rel)
                    k.rel = [tv]
                for h, l, tl in mids:
                    h.rel = l.rel = [tok]
                to = dma(Y, f"{tag}o{ob.at % 2}", ov_[j], o2.ap, tv)
                o2.rel = [to]
                tout = ([tout] if tout else []) + [to] if j >= n - 2 else None
            return [t for t in flat(tout)]

        def gather(obuf, pi, s, t, dst, name, *w):
            chans.setdefault(name, [sem("d_" + name) if name not in chans else chans[name][0], 0])
            ch = chans[name]
            ch[1] += 16
            G(lambda e: e.indirect_dma_start(
                out=dst, out_offset=None, in_=obuf,
                in_offset=bass.IndirectOffsetOnAxis(ap=pi[:, s, t:t + 1].bitcast(U32), axis=0)).then_inc(ch[0], 16),
                *w, inc=False)
            return (ch[0], ch[1])

        MZ.reset()
        SZ.reset()
        W0 = Weights(MZ, E * 2 * H0, E * 2 * H0)
        LNZ = Zone(SZ.start, 19 * K)
        HLz = Zone(WA.start, 20 * K)
        HL = HLz(128, NT, 2 * D, dt=F16)
        b2m0 = LNZ(128, E * D)
        SRZ = Zone(LNZ.at, 8 * K)
        SR = Ring([LNZ(128, CH)[:, :] for _ in range(2)])
        tr0 = Zone(MZ.start + 96 * K, 32 * K)
        XN, XT_, HF, HT_ = (Buf(tr0(128, 4, D), bar) for _ in range(4))
        lgz = tr0(128, NT, E)
        rz = Zone(tr0.at, tr0.end - tr0.at)
        tb2 = dma(Y, "b2m0", b2m0[:, :], a["L0_ffn_b2"].rearrange("e d -> (e d)").partition_broadcast(128), bar)
        tzero0 = zero_rows(buf0, N0, rz, bar)
        bT, bS, bY = banks([0, 1]), banks([2, 3, 4]), banks([5, 6, 7])
        for r_ in (bT, bS, bY):
            for bb in r_.bufs:
                bb.rel = bar
        top, idxu = rz(128, NT, 8), rz(128, NT, 8)
        idxf, ww = rz(128, 2, NT), LNZ(128, 3, NT)
        lnz2 = Zone(rz.at, 2 * K)
        rz = Zone(lnz2.end, tr0.end - lnz2.end)

        def moe_pre(b):
            sc, tk = ln_stats([X[:, 4 * b + t, :] for t in range(4)], lnz2, bar)
            for t in range(4):
                c = vts(XN.ap[:, t, :], X[:, 4 * b + t, :], *sc[t], ALU.subtract, ALU.mult, tk, XN.rel)
            yield
            xt4 = XT_.ap[:, :, :].rearrange("p a n -> p (a n)").rearrange("p (c n) -> p c n", c=2)
            for c2 in range(2):
                ev = transpose4(bT, [XN.ap[:, t, c2 * 128:(c2 + 1) * 128] for t in range(4)],
                                lambda k, tok: acopy(xt4[:, c2, :], k, tok, XT_.rel), c)
            XN.rel = [T.last()]
            yield
            for t in range(4):
                k = bY.take()
                for c2 in range(2):
                    tok = mm(k.ap[:, 0:D], xt4[:, c2, t * 128:(t + 1) * 128], Win[:, c2, :], c2 == 0, c2 == 1, ev, t_wb,
                             k.rel, inc=c2 == 1)
                th = vtt(HF.ap[:, t, :], k.ap[:, 0:D], bin_[:, :], ALU.add, tok, HF.rel)
                k.rel = [th]
            XT_.rel = [tok]
            yield
            hs = HL[:, 4 * b:4 * b + 4, :]
            tc_ = acopy(hs[:, :, 0:D], HF.ap[:, :, :], th)
            tl = vtt(hs[:, :, D:2 * D], HF.ap[:, :, :], hs[:, :, 0:D], ALU.subtract, tc_)
            ht4 = HT_.ap[:, :, :].rearrange("p a n -> p (a n)").rearrange("p (c n) -> p c n", c=2)
            for c2 in range(2):
                ev = transpose4(bT, [HF.ap[:, t, c2 * 128:(c2 + 1) * 128] for t in range(4)],
                                lambda k, tok: acopy(ht4[:, c2, :], k, tok, HT_.rel), th)
            HF.rel = [T.last(), tl]
            yield
            k = bY.take()
            for t in range(4):
                for c2 in range(2):
                    tok = mm(k.ap[:, t * E:(t + 1) * E], ht4[:, c2, t * 128:(t + 1) * 128], Wg[:, c2, :], c2 == 0, c2 == 1,
                             ev, t_wb, k.rel, inc=c2 == 1)
            HT_.rel = [tok]
            lg = lgz[:, 4 * b:4 * b + 4, :]
            c = vtt(lg, k.ap[:, 0:4 * E].rearrange("p (t e) -> p t e", e=E), bgate[:, :].unsqueeze(1).to_broadcast([128, 4, E]),
                    ALU.add, tok)
            k.rel = [c]
            for t in range(4):
                tt = 4 * b + t
                cm = V(lambda e, tt=tt: e.max(top[:, tt, :], lgz[:, tt, :]), c)
            for t in range(4):
                tt = 4 * b + t
                ci = V(lambda e, tt=tt: e.max_index(idxu[:, tt, :].bitcast(U32), top[:, tt, :], lgz[:, tt, :]), cm)
            st[b]["i"], st[b]["hl"] = ci, tl
            yield

        def chain(*gens):
            for g in gens:
                yield from g

        def keep(g, box):
            box += (yield from g)

        sp1 = keep(split_weights(a["w1m0"], W0.w1h, W0.w1l, E * 2 * H0, SR, "wm", bar), W0.t1)
        weave(chain(*[moe_pre(b) for b in range(NB)]), sp1)
        cis, hls = [st[b]["i"] for b in range(NB)], [st[b]["hl"] for b in range(NB)]
        c = vcopy(idxf[:, :, :], idxu[:, :, 0:2].bitcast(U32).rearrange("p t s -> p s t"), cis)
        d01 = LNZ(128, NT)
        c1 = vtt(d01[:, :], top[:, :, 1], top[:, :, 0], ALU.subtract, cis)
        c1 = act(d01[:, :], d01[:, :], ACT.Exp, c1)
        c1 = vts(ww[:, 2, :], d01[:, :], 1.0, None, ALU.add, ALU.bypass, c1)
        c1 = V(lambda e: e.reciprocal(ww[:, 0, :], ww[:, 2, :]), c1)
        tw = vtt(ww[:, 1, :], d01[:, :], ww[:, 0, :], ALU.mult, c1)
        r = routing(2, idxf, N0, rz, c, t_wb)
        pi0z = Zone(PZ.at, PZ.end - PZ.at)
        rr = list(r)
        pi_keep = LNZ(128, 2, NT)
        tei_keep = [LNZ(1, N0) for _ in range(3)]
        rr[10], rr[12] = tei_keep, pi_keep
        pi0, tei0, te0, tpos = positions(2, rr, 8)
        tsc = scatter(buf0, HL, pi0, 2, "sc0", tpos, hls, tzero0)
        weave(keep(split_weights(a["w2m0"], W0.w2h, W0.w2l, E * 2 * H0, SR, "wm", [tpos, te0, tw, tzero0]), W0.t2))
        SRZ.reset()
        ez = Zones(Zone(WA.start, 20 * K), Zone(LNZ.at, LNZ.end - LNZ.at), SRZ)
        te0 = experts(ez, buf0, obuf0, N0, 8, W0, ACT.Relu, b1m, b2m0, tei0, "e0", tsc, te0, tb2, t_wb, W0.t2)

        bar = everyone()
        MZ.reset()
        cz = Zone(MZ.start, 128 * K)
        GB = Ring([cz(128, 2, D)[:, :, :] for _ in range(4)])
        MO = [cz(128, 4, D) for _ in range(2)]
        MT = [Buf(cz(128, 2, S)) for _ in range(2)]
        bT, bY = banks([0, 1, 2]), banks([3, 4, 5, 6, 7])
        for r_ in (bT, bY):
            for bb in r_.bufs:
                bb.rel = bar

        def combine(b):
            mo, mt = MO[b % 2], MT[b % 2]
            txo = vtt(X[:, 4 * b:4 * b + 4, :], X[:, 4 * b:4 * b + 4, :], bout.unsqueeze(1).to_broadcast([128, 4, D]),
                      ALU.add, bar, q=G)
            gs = []
            for t in range(4):
                tt = 4 * b + t
                g = GB.take()
                for s in range(2):
                    tg = gather(obuf0, pi0, s, tt, g.ap[:, s, :], f"g0{GB.at % 4}", te0, g.rel)
                gs.append((g, tg))
            for t in range(4):
                tt = 4 * b + t
                g, tg = gs[t]
                c = vts(mo[:, t, :], g.ap[:, 0, :], ww[:, 0, tt:tt + 1], None, ALU.mult, ALU.bypass, tg, tw, bar, st[b].get("mo"))
                c = vstt(mo[:, t, :], g.ap[:, 1, :], ww[:, 1, tt:tt + 1], mo[:, t, :], ALU.mult, ALU.add, c)
                g.rel = [c]
            for c2 in range(2):
                ev = transpose4(bT, [mo[:, t, c2 * 128:(c2 + 1) * 128] for t in range(4)],
                                lambda k, tok: acopy(mt.ap[:, c2, :], k, tok, mt.rel), c)
            st[(b + 2)] = dict(st.get(b + 2, {}), mo=T.last())
            for t in range(4):
                k = bY.take()
                for c2 in range(2):
                    tok = mm(k.ap[:, 0:D], mt.ap[:, c2, t * 128:(t + 1) * 128], Wout[:, c2, :], c2 == 0, c2 == 1, ev, k.rel,
                             t_wb, inc=c2 == 1)
                tx2 = vtt(X[:, 4 * b + t, :], k.ap[:, 0:D], X[:, 4 * b + t, :], ALU.add, tok, txo)
                k.rel = [tx2]
            mt.rel = [tok]
            return tx2

        x2 = [combine(b) for b in range(NB)]
        if stop == 2:
            finish()
            emit()
            return

        bar = everyone()
        MZ.reset()
        QS = [MZ(128, 8, S, dt=F32R) for _ in range(2)]
        KS = [MZ(128, NH, S, dt=F32R) for _ in range(2)]
        VA = [Buf(MZ(128, 4, NH, 32)) for _ in range(2)]
        AZ = Zones(Zone(WA.start, 20 * K), Zone(SZ.start, 19 * K), MZ)
        ET = Ring([AZ(128, 2, S) for _ in range(2)])
        HLR = Ring([AZ(128, 2, 2, S, dt=F32R) for _ in range(2)])
        XT_, CTT, CX, CXT = (Buf(AZ(128, 2, S)) for _ in range(4))
        OS = Ring([AZ(128, S) for _ in range(1)])
        MT_ = Buf(AZ(16, S, dt=F32R))
        zrow = AZ(1, S)
        LNZ = AZ
        qkrel = {("q", 0): bar, ("q", 1): bar, ("k", 0): bar, ("k", 1): bar}
        tz = V(lambda e: e.memset(zrow[:, :], 0.0), bar)
        t1row = V(lambda e: e.memset(MT_.ap[0:1, :].bitcast(F32), 1.0), bar)
        tms = []
        for i in range(2):
            tms.append(G(lambda e, i=i: e.memset(QS[i][:, :, :].bitcast(F32), 0.0), bar))
            t0 = G(lambda e, i=i: e.memset(KS[i][:, :, :].bitcast(F32), 0.0), bar)
            for j in range(2):
                t0_ = (dma(Y, f"one{i}", KS[i][64 * j + 48:64 * j + 49, :, :].bitcast(F32).rearrange(
                    "o (p j) n -> o p j n", j=2)[:, :, j, :],
                    MT_.ap[0:1, :].bitcast(F32).unsqueeze(1).to_broadcast([1, 8, S]), t0, t1row))
            tms.append(t0_)
            MT_.rel = [*MT_.rel, t0_]
            t0 = V(lambda e, i=i: e.memset(VA[i].ap[:, :, :, 16:32], 0.0), bar)
            tms.append(V(lambda e, i=i: e.memset(VA[i].ap[:, :, :, 16:17], 1.0), t0))
        bX, bM, bS, bO = banks([0]), pairs([1]), pairs([2, 3]), banks([1])
        held((bX, bM, bS, bO), bar)
        ctv = a["ctxT"].rearrange("b p c n -> b p c n")
        st = {b: {} for b in range(NB)}

        def spread(b, which, src, toks):
            dst = (QS if which == "q" else KS)[b % 2]
            n = 4 if which == "q" else 8
            dv = dst[:, :, :].bitcast(F32).rearrange("p (c b) n -> p c b n", c=2)
            order = (0, 0, 1) if which == "q" else (0, 1, 0)
            for g, part in enumerate(order):
                for b8 in range(8):
                    r0 = 64 * (b8 % 2) + 16 * g
                    t = dma(Y, f"{which}s{b % 2}", dv[r0:r0 + 16, :, b8 // 2 if which == "q" else b8, :],
                            src[16 * b8:16 * b8 + 16, part, :, :].bitcast(F32), toks, tms, qkrel[which, b % 2])
            if which == "q":
                for j in range(2):
                    t = dma(Y, f"qs{b % 2}", dst[64 * j + 48:64 * j + 49, :, :].bitcast(F32),
                            zrow[:, :].unsqueeze(1).to_broadcast([1, 8, S]), tz, qkrel[which, b % 2])
            return t

        def prep(b):
            s = st[b]
            tct = dma(Y, "ctt", CTT.ap, ctv[b], CTT.rel, bar)
            sc, tk = ln_stats([X[:, 4 * b + t, :] for t in range(4)], LNZ, bar)
            cxv = CX.ap.rearrange("p a n -> p (a n)").rearrange("p (t d) -> p t d", t=4)
            for which in ("k", "q"):
                hl = HLR.take()
                if which == "q":
                    xn = XN_.ap
                    for t in range(4):
                        c = vts(xn[:, t, :], X[:, 4 * b + t, :], *sc[t], ALU.subtract, ALU.mult, tk, XN_.rel)
                    for c2 in range(2):
                        ev = transpose4(bX, [xn[:, t, c2 * 128:(c2 + 1) * 128] for t in range(4)],
                                        lambda k, tok: vcopy(XT_.ap[:, c2, :], k, tok, XT_.rel), c)
                    XN_.rel = [T.last()]
                    txb = vtt(X[:, 4 * b:4 * b + 4, :], X[:, 4 * b:4 * b + 4, :], bo.unsqueeze(1).to_broadcast([128, 4, D]),
                              ALU.add, c, q=G)
                    s["txb"] = txb
                    yield
                src, ts_, wi, bi = (CTT, tct, 1, 14) if which == "k" else (XT_, ev, 0, 12)
                for c in range(2):
                    k = bX.take()
                    for kk in range(2):
                        tok = mm(k.ap, Wqkv[:, wi, kk, c * 128:(c + 1) * 128], src.ap[:, kk, :], kk == 0, kk == 1, ts_, k.rel,
                                 t_wc, inc=kk == 1)
                    hi = hl.ap[:, 0, c, :]
                    th = act(hi, k.ap, ACT.Identity, tok, hl.rel, bias=pp[:, bi + c:bi + c + 1])
                    tl = vstt(hl.ap[:, 1, c, :], k.ap, pp[:, bi + c:bi + c + 1], hi.bitcast(F32), ALU.add, ALU.subtract, th)
                    k.rel = [tl]
                    yield
                src.rel = [tok]
                sp = spread(b, which, hl.ap, [th, tl])
                hl.rel = [sp]
                s[which] = sp
                yield
                if which == "k":
                    va = VA[b % 2]
                    for t in range(4):
                        k = bX.take()
                        for kk in range(2):
                            tok = mm(k.ap[:, 0:D], CTT.ap[:, kk, t * 128:(t + 1) * 128], Wqkv[:, 2, kk, :], kk == 0, kk == 1,
                                     tct, k.rel, t_wc, inc=kk == 1)
                        tv = vtt(va.ap[:, t, :, 0:16], k.ap[:, 0:D].rearrange("p (h d) -> p h d", d=16),
                                 bv.rearrange("p (h d) -> p h d", d=16), ALU.add, tok, va.rel, tms)
                        k.rel = [tv]
                        yield
                    CTT.rel = [tok]
                    s["v"] = tv

        def maxima(b):
            s = st[b]
            mx = MXB[b % 2]
            for t in range(4):
                for p in range(8):
                    k = bM.take()
                    for j in range(2):
                        tok = mm(k.ap[:, j * S:(j + 1) * S], QS[b % 2][:, p, t * 128:(t + 1) * 128], KS[b % 2][:, 2 * p + j, :],
                                 True, True, s["q"], s["k"], k.rel, inc=j == 1)
                    tm = V(lambda e, t=t, p=p, k=k: e.tensor_reduce(
                        mx[:, t, 2 * p:2 * p + 2], k.ap.rearrange("p (j n) -> p j n", j=2), AX.X, ALU.max), tok)
                    k.rel = [tm]
                    yield
            k = bX.take()
            for t in range(4):
                tt = tr(k.ap[0:16, t * 128:(t + 1) * 128], mx[:, t, :], ident[:, :], tm, k.rel, inc=t == 3)
            te = vts(MT_.ap, k.ap[0:16, :], -1.0, None, ALU.mult, ALU.bypass, tt, MT_.rel)
            k.rel = [te]
            for h in range(NH):
                r0 = 64 * (h % 2) + 48
                tq = dma(Y, f"qs{b % 2}", QS[b % 2][r0:r0 + 1, h // 2, :].bitcast(F32), MT_.ap[h:h + 1, :].bitcast(F32), te, tok)
            MT_.rel = [tq]
            s["m"] = tq
            yield

        def attend(b):
            s, va = st[b], VA[b % 2]
            for g in range(4):
                ko = bO.take()
                for j in range(4):
                    h = 4 * g + j
                    for kp in range(2):
                        k = bS.take()
                        for i in range(2):
                            kc = 2 * kp + i
                            tok = mm(k.ap[:, i * S:(i + 1) * S], KS[b % 2][:, h, kc * 128:(kc + 1) * 128],
                                     QS[b % 2][:, h // 2, :], True, True, s["m"], s["k"], k.rel, inc=i == 1)
                        et = ET.take()
                        te = act(et.ap, k.ap.rearrange("p (i n) -> p i n", i=2), ACT.Exp, tok, et.rel, scale=0.25)
                        k.rel = [te]
                        s.setdefault("pend", []).append((ko, j, h, kp, et, te))
                        if len(s["pend"]) > 1:
                            av(s, va, s["pend"].pop(0))
                        yield
                while s["pend"]:
                    av(s, va, s["pend"].pop(0))
                o = OS.take()
                ev = vcopy(o.ap, ko.ap, s["av"], o.rel)
                ko.rel = [ev]
                k = bX.take()
                for t in range(4):
                    tok = tr(k.ap[:, t * 128:(t + 1) * 128], o.ap[:, t * 128:(t + 1) * 128], ident[:, :], ev, k.rel, inc=t == 3)
                o.rel = [tok]
                kv = k.ap.rearrange("p (t j d) -> p t j d", t=4, j=4)
                rc = RC.take()
                c = V(lambda e, kv=kv, rc=rc: e.reciprocal(rc.ap, kv[:, :, :, 16]), tok)
                cxv = CX.ap.rearrange("p a n -> p (a n)").rearrange("p (t h d) -> p t h d", t=4, h=NH)
                for t in range(4):
                    tx_ = vtt(cxv[:, t, 4 * g:4 * g + 4, :], kv[:, t, :, 0:16], rc.ap[:, t, :].unsqueeze(2).to_broadcast([128, 4, 16]),
                              ALU.mult, c, CX.rel)
                k.rel = [tx_]
                yield
            va.rel = [s["av"]]
            qkrel["q", b % 2] = qkrel["k", b % 2] = [T.last()]
            cx = CX.ap.rearrange("p a n -> p (a n)").rearrange("p (t d) -> p t d", t=4)
            for c2 in range(2):
                ev = transpose4(bX, [cx[:, t, c2 * 128:(c2 + 1) * 128] for t in range(4)],
                                lambda k, tok: vcopy(CXT.ap[:, c2, :], k, tok, CXT.rel), tx_)
            CX.rel = [T.last()]
            yield
            for t in range(4):
                k = bX.take()
                for c2 in range(2):
                    tok = mm(k.ap[:, 0:D], CXT.ap[:, c2, t * 128:(t + 1) * 128], Wqkv[:, 3, c2, :], c2 == 0, c2 == 1, ev, t_wc,
                             k.rel, inc=c2 == 1)
                tx2 = vtt(X[:, 4 * b + t, :], k.ap[:, 0:D], X[:, 4 * b + t, :], ALU.add, tok, s["txb"])
                k.rel = [tx2]
                yield
            CXT.rel = [tok]

        def av(s, va, item):
            ko, j, h, kp, et, te = item
            for i in range(2):
                kc = 2 * kp + i
                s["av"] = mm(ko.ap[32 * j:32 * j + 32, :], va.ap[:, kc, h, :], et.ap[:, i, :], kc == 0, kc == 3, te, s["v"], ko.rel,
                             inc=i == 1)
            et.rel = [s["av"]]

        XN_ = Buf(AZ(128, 4, D))
        MXB = [AZ(128, 4, NH) for _ in range(2)]
        RC = Ring([AZ(128, 4, 4) for _ in range(2)])
        t_wc = dma(Y, "wc", Wqkv[:, :, :, :], a["Wqkv"], bar)
        weave(prep(0))
        weave(maxima(0))
        for b in range(NB):
            weave(attend(b), chain(prep(b + 1), maxima(b + 1)) if b + 1 < NB else None)
        if stop == 3:
            finish()
            emit()
            return

        bar = everyone()
        MZ.reset()
        buf1 = nc.dram_tensor("buf1", (N1 * TOK, 2 * D), F16, kind="Internal").ap()
        obuf1 = nc.dram_tensor("obuf1", (N1 * TOK, D), F32, kind="Internal").ap()
        W1 = Weights(MZ, E * 2 * H1, E * 2 * H1)
        HL = MZ(128, NT, 2 * D, dt=F16)
        XN = [Buf(MZ(128, 4, D), bar) for _ in range(2)]
        XT_ = [Buf(MZ(128, 2, S), bar) for _ in range(2)]
        rz = Zone(MZ.at, MZ.end - MZ.at)
        SRZ = Zone(WA.start, 20 * K)
        SR = Ring([SRZ(128, CH) for _ in range(4)])
        LNZ = Zone(SZ.start, 19 * K)
        b2m1 = LNZ(128, E * D)
        b1m1 = LNZ(128, 32)
        wgT, xrT, wgt = LNZ(16, E), [Buf(rz(16, S), bar) for _ in range(2)], LNZ(E, 64)
        lgz1, top1, idxu1, idxf1, exz, scr = rz(128, NT, E), rz(128, NT, 8), rz(128, NT, 8), rz(128, 1, NT), rz(128, NT, E), LNZ(128, NT)
        dma(Y, "wd", b2m1[:, :], a["L1_ffn_b2"].rearrange("e d -> (e d)").partition_broadcast(128), bar)
        dma(Y, "wd", b1m1[:, :], a["b1m1"], bar)
        dma(Y, "wd", wred[:, :, :], a["wred"], bar)
        t_wd = dma(Y, "wd", wg8[:, :], a["L1_ffn_wg"], bar)
        tzero1 = zero_rows(buf1, N1, rz, bar)
        bT, bS, bY = banks([0, 1]), banks([2, 3, 4]), banks([5, 6, 7])
        held((bT, bS, bY), bar)
        c = V(lambda e: e.tensor_tensor(wgt[:, 0:16], wg8[:, :], wg8[:, :], ALU.mult), t_wd, bar)
        c = V(lambda e: e.tensor_reduce(wgt[:, 16:17], wgt[:, 0:16], AX.X, ALU.add), c)
        y, c = rsqrt(wgt[:, 16:17], 1, wgt[:, 20:24], c, parts=E)
        c = vtt(wgt[:, 17:18], wgt[:, 16:17], y, ALU.mult, c)
        c = vts(wgt[:, 17:18], wgt[:, 17:18], 1e-4, None, ALU.max, ALU.bypass, c)
        c = V(lambda e: e.reciprocal(wgt[:, 18:19], wgt[:, 17:18]), c)
        c = vts(wgt[:, 32:48], wg8[:, :], wgt[:, 18:19], None, ALU.mult, ALU.bypass, c)
        k = bY.take()
        tok = tr(k.ap[0:16, 0:E], wgt[:, 32:48], ident[0:E, 0:E], c, k.rel, inc=True)
        t_wg = vcopy(wgT[:, :], k.ap[0:16, 0:E], tok)
        k.rel = [t_wg]

        def gate(b):
            xn, xt, xr = XN[b % 2], XT_[b % 2], xrT[b % 2]
            sc, tk = ln_stats([X[:, 4 * b + t, :] for t in range(4)], LNZ, bar)
            for t in range(4):
                c = vts(xn.ap[:, t, :], X[:, 4 * b + t, :], *sc[t], ALU.subtract, ALU.mult, tk, xn.rel)
            yield
            hs = HL[:, 4 * b:4 * b + 4, :]
            tc_ = acopy(hs[:, :, 0:D], xn.ap, c)
            tl = vtt(hs[:, :, D:2 * D], xn.ap, hs[:, :, 0:D], ALU.subtract, tc_)
            for c2 in range(2):
                ev = transpose4(bT, [xn.ap[:, t, c2 * 128:(c2 + 1) * 128] for t in range(4)],
                                lambda k, tok: acopy(xt.ap[:, c2, :], k, tok, xt.rel), c)
            xn.rel = [T.last(), tl]
            yield
            k = bY.take()
            for c2 in range(2):
                tok = mm(k.ap[0:16, :], wred[:, c2, :], xt.ap[:, c2, :], c2 == 0, c2 == 1, ev, t_wd, k.rel, inc=c2 == 1)
            xt.rel = [tok]
            ex = acopy(xr.ap, k.ap[0:16, :], tok, xr.rel)
            k.rel = [ex]
            k = bY.take()
            for t in range(4):
                tok = mm(k.ap[:, t * E:(t + 1) * E], xr.ap[:, t * 128:(t + 1) * 128], wgT[:, :], True, True, ex, t_wg, k.rel, inc=t == 3)
            xr.rel = [tok]
            c = vcopy(lgz1[:, 4 * b:4 * b + 4, :], k.ap[:, 0:4 * E].rearrange("p (t e) -> p t e", e=E), tok)
            k.rel = [c]
            for t in range(4):
                tt = 4 * b + t
                cm = V(lambda e, tt=tt: e.max(top1[:, tt, :], lgz1[:, tt, :]), c)
            for t in range(4):
                tt = 4 * b + t
                ci = V(lambda e, tt=tt: e.max_index(idxu1[:, tt, :].bitcast(U32), top1[:, tt, :], lgz1[:, tt, :]), cm)
            st[b]["i"], st[b]["hl"] = ci, tl
            yield

        weave(chain(*[gate(b) for b in range(NB)]),
              chain(keep(split_weights(a["w1m1"], W1.w1h, W1.w1l, E * 2 * H1, SR, "wn", bar), W1.t1),
                    keep(split_weights(a["w2m1"], W1.w2h, W1.w2l, E * 2 * H1, SR, "wn", bar), W1.t2)))
        cis, hls = [st[b]["i"] for b in range(NB)], [st[b]["hl"] for b in range(NB)]
        c = vcopy(idxf1[:, :, :], idxu1[:, :, 0:1].bitcast(U32).rearrange("p t s -> p s t"), cis)
        c1 = vtt(exz[:, :, :], lgz1[:, :, :], top1[:, :, 0:1].to_broadcast([128, NT, E]), ALU.subtract, cis)
        c1 = act(exz[:, :, :], exz[:, :, :], ACT.Exp, c1)
        c1 = V(lambda e: e.tensor_reduce(scr[:, :], exz[:, :, :], AX.X, ALU.add), c1)
        tsc1 = V(lambda e: e.reciprocal(scr[:, :], scr[:, :]), c1)
        rr = list(routing(1, idxf1, N1, rz, c, t_wb))
        rr[10], rr[12] = [LNZ(1, N1) for _ in range(3)], LNZ(128, 1, NT)
        pi1, tei1, te1, tpos = positions(1, rr, 4)
        tsc = scatter(buf1, HL, pi1, 1, "sc1", tpos, hls, tzero1)
        ez = Zones(Zone(MZ.start + 64 * K, 64 * K))
        tout = experts(ez, buf1, obuf1, N1, 4, W1, ACT.Gelu, b1m1, b2m1, tei1, "e1", tsc, te1, tpos, tsc1, t_wd, W1.t1, W1.t2)
        GB = Ring([SRZ0(128, D) for SRZ0 in [Zone(WA.start, 20 * K)] for _ in range(8)])
        ov = out.rearrange("b (t p) d -> p (b t) d", p=128)
        for t in range(NT):
            g = GB.take()
            tg = gather(obuf1, pi1, 0, t, g.ap, f"g1{GB.at % 8}", tout, g.rel)
            c = vstt(X[:, t, :], g.ap, scr[:, t:t + 1], X[:, t, :], ALU.mult, ALU.add, tg, tsc1)
            g.rel = [c]
            if t % 4 == 3:
                to = dma(Y, "out", ov[:, t - 3:t + 1, :], X[:, t - 3:t + 1, :], c)
        Y(lambda e: e.wait_ge(*to), inc=False)
        emit()


def layouts(v):
    f = np.float32
    c = np.ascontiguousarray

    def kmaj(w, k):
        return c(w.reshape(k, 128, w.shape[-1]).transpose(1, 0, 2))

    d = {}
    for n in ("x", "ctx_1024", "L0_xattn_ln_g", "L0_xattn_ln_b", "L0_xattn_b_diff", "L0_xattn_b2", "L0_ffn_b_out",
              "L1_xattn_bo", "L1_xattn_bv", "L0_ffn_b_in", "L0_ffn_b_gate"):
        d[n] = c(v[n])
    d["ident"] = np.eye(128, dtype=f)
    d["U"] = np.triu(np.ones((128, 128), f), 1)
    d["io8"] = np.broadcast_to(np.arange(8, dtype=f), (128, 8)).copy()
    d["ioj"] = np.broadcast_to(np.arange(32, dtype=f), (128, 32)).copy()
    d["WdT"] = kmaj(v["L0_xattn_W_diff"].T, 2)
    d["W1T"] = kmaj(v["L0_xattn_W1"].T, 2)
    d["W2T"] = kmaj(v["L0_xattn_W2"].T, 8)
    pp = np.zeros((128, 16), f)
    pp[:, 0:2] = v["L0_xattn_ln_g"].reshape(2, 128).T
    pp[:, 2:4] = v["L0_xattn_ln_b"].reshape(2, 128).T
    pp[:, 4:12] = v["L0_xattn_b1"].reshape(8, 128).T
    pp[:, 12:14] = v["L1_xattn_bq"].reshape(2, 128).T
    pp[:, 14:16] = v["L1_xattn_bk"].reshape(2, 128).T
    d["pp"] = pp
    d["Win"] = kmaj(v["L0_ffn_W_in"], 2)
    d["Wg"] = kmaj(v["L0_ffn_W_gate"], 2)
    d["Wout"] = kmaj(v["L0_ffn_W_out"], 2)
    d["L0_ffn_b2"] = c(v["L0_ffn_b2"])
    d["w1m0"] = c(v["L0_ffn_W1"].reshape(8, 2, 128, H0).transpose(2, 0, 1, 3).reshape(128, -1))
    d["w2m0"] = c(v["L0_ffn_W2"].reshape(8, 8, 128, D).transpose(2, 0, 1, 3).reshape(128, -1))
    d["ctxT"] = c(v["ctx_1024"].reshape(NB, S, 2, 128).transpose(0, 3, 2, 1))
    d["Wqkv"] = c(np.stack([kmaj(v["L1_xattn_" + n], 2) for n in ("Wq", "Wk", "Wv", "Wo")], 1))
    d["wred"] = kmaj(v["L1_ffn_w_red"], 2)
    d["L1_ffn_wg"], d["L1_ffn_b2"] = c(v["L1_ffn_wg"]), c(v["L1_ffn_b2"])
    d["w1m1"] = c(v["L1_ffn_W1"].reshape(8, 2, 128, H1).transpose(2, 0, 1, 3).reshape(128, -1))
    d["w2m1"] = c(v["L1_ffn_W2"].reshape(8, 4, 128, D).transpose(2, 0, 1, 3).reshape(128, -1))
    d["b1m1"] = c(v["L1_ffn_b1"].reshape(32, 128).T)
    d["b1m0"] = c(v["L0_ffn_b1"].reshape(64, 128).T)
    return d


def kernel(**inputs):
    import concourse.bacc as bacc
    from concourse.bass_utils import run_bass_kernel_spmd

    arrays = layouts({n: np.asarray(x) for n, x in inputs.items()})
    nc = bacc.Bacc("TRN2", target_bir_lowering=False, num_devices=1)
    aps = {n: nc.dram_tensor("in_" + n, x.shape, mybir.dt.from_np(x.dtype), kind="ExternalInput").ap()
           for n, x in arrays.items()}
    out = nc.dram_tensor("out_0", (NB, S, D), F32, kind="ExternalOutput").ap()
    build(nc, aps, out)
    r = run_bass_kernel_spmd(nc, [{"in_" + n: x for n, x in arrays.items()}], core_ids=[0])
    return r.results[0]["out_0"]
```

```python
import numpy as np
import concourse.bass as bass
from concourse import mybir
from contextlib import ExitStack

F32 = mybir.dt.float32
F32R = mybir.dt.float32r
F16 = mybir.dt.float16
I32 = mybir.dt.int32
U32 = mybir.dt.uint32
ALU = mybir.AluOpType
ACT = mybir.ActivationFunctionType
AX = mybir.AxisListType

NB, TB, P, D = 4, 4, 128, 256
NT = NB * TB
S = 512
E = 8
TOK = 256
SUB = TOK // P
N0 = (2 * NT * P + E * (TOK - 1)) // TOK
N1 = (NT * P + E * (TOK - 1)) // TOK
H0, H1 = 1024, 512
NH, HD = 16, 16
WS = 64.0
VS = 64.0
LNES = float(np.log(1024.0))


class Queue:

    def __init__(self, sem):
        self.sem, self.n, self.items = sem, 0, []

    def __call__(self, fn, *waits, inc=True):
        self.items.append((fn, flat(waits), inc))
        if inc:
            self.n += 1
            return (self.sem, self.n)
        return None

    def last(self):
        return (self.sem, self.n)

    def play(self, eng):
        seen = {}
        for fn, waits, inc in self.items:
            for sem, value in waits:
                if value > seen.get(sem.name, 0):
                    eng.wait_ge(sem, value)
                    seen[sem.name] = value
            made = fn(eng)
            if inc:
                made.then_inc(self.sem, 1)


def flat(waits):
    out = []
    for w in waits:
        if w is None:
            continue
        if isinstance(w, list):
            out += flat(w)
        else:
            out.append(w)
    return out


class Buf:

    def __init__(self, ap, rel=None):
        self.ap, self.rel = ap[(slice(None),) * len(ap.shape)], rel or []


class Ring:
    def __init__(self, aps):
        self.bufs, self.at = [Buf(a) for a in aps], 0

    def take(self):
        b = self.bufs[self.at % len(self.bufs)]
        self.at += 1
        return b


def build(nc, a, out, stop=4):
    ctx = ExitStack()
    with ctx:
        base = [nc.sbuf_base + (-nc.sbuf_base) % 64]
        names = [0]

        def at(off, shape, dt=F32):
            names[0] += 1
            return nc.alloc_sbuf_tensor_at(f"t{names[0]}", shape, dt, offset=off)

        def size(shape, dt):
            n = 2 if dt == F16 else 4
            for s in shape[1:]:
                n *= s
            return n + (-n) % 32

        class Zone:
            def __init__(self, start, length):
                self.start, self.end, self.at = start, start + length, start

            def __call__(self, *shape, dt=F32):
                t = at(self.at, list(shape), dt)
                self.at += size(shape, dt)
                assert self.at <= self.end, (shape, self.at - self.end)
                return t

            def reset(self):
                self.at = self.start

        class Zones:

            def __init__(self, *zones):
                self.zones = zones

            def __call__(self, *shape, dt=F32):
                n = size(shape, dt)
                for z in self.zones:
                    if z.at + n <= z.end:
                        return z(*shape, dt=dt)
                raise AssertionError(("no room", shape, [z.end - z.at for z in self.zones]))

        def sem(name):
            return ctx.enter_context(nc.semaphore(name))

        K = 1024
        b0 = base[0]
        PZ = Zone(b0, 40 * K)
        WA = Zone(PZ.end, 20 * K)
        SZ = Zone(WA.end, 19 * K)
        MZ = Zone(SZ.end, 128 * K)
        assert MZ.end <= nc.sbuf_usable_end, (MZ.end, nc.sbuf_usable_end)

        T = Queue(sem("s_pe"))
        V = Queue(sem("s_dve"))
        A = Queue(sem("s_act"))
        G = Queue(sem("s_pool"))
        Y = Queue(None)
        chans = {}

        def dma(q, name, o, i, *waits):
            if name not in chans:
                chans[name] = [sem("d_" + name), 0]
            c = chans[name]
            c[1] += 16
            s, v = c[0], c[1]
            q(lambda e: e.dma_start(o, i).then_inc(s, 16), *waits, inc=False)
            return (s, v)

        def everyone():
            return [T.last(), V.last(), A.last(), G.last()] + [(c[0], c[1]) for c in chans.values()]

        PB = [ctx.enter_context(nc.psum_tensor(f"pb{i}", [128, 1024], F32)) for i in range(4)]

        def banks(ids):
            return Ring([PB[i // 2][:, i % 2 * 512:i % 2 * 512 + 512] for i in ids])

        def pairs(ids):
            return Ring([PB[i][:, :] for i in ids])

        def held(rings, toks):
            for r in rings:
                for b in r.bufs:
                    b.rel = toks

        X = PZ(128, NT, D)
        ident = PZ(128, 128)
        identh = PZ(128, 128, dt=F16)
        bc = PZ(128, 7, D)
        bgate = PZ(128, E)
        Win_off = PZ.at
        Win = PZ(128, 2, D)
        bin_ = PZ(128, D)
        Wg = PZ(128, 2, E)
        Wout_off = PZ.at
        Wout = PZ(128, 2, D)
        Wqkv = PZ(128, 4, 2, D)
        wred = PZ(128, 2, 16)
        wg8 = PZ(8, 16)
        pp = PZ(128, 16)
        b1m = PZ(128, 64)
        U = PZ(128, 128)
        ones = PZ(128, 128)
        io8 = PZ(128, E)
        ioj = PZ(128, 32)
        W1T = WA(128, 2, H0)
        W2T = WA(128, 8, D)
        WdT = WA(128, 2, D)
        lng, lnb, bdiff, b2a, bout, bo, bv = (bc[:, i, :] for i in range(7))

        ld = {}
        ld["ident"] = dma(Y, "ident", ident[:, :], a["ident"])
        xv = a["x"].rearrange("b (t p) d -> b p t d", p=128)
        cv = a["ctx_1024"].rearrange("b (t p) d -> b p t d", p=128)
        tx = {}

        def load_x(b):
            tx[b] = dma(Y, f"x{b}", X[:, 4 * b:4 * b + 4, :], xv[b])

        def bcast(n):
            return a[n].partition_broadcast(128)

        def loads_p():
            dma(Y, "wp", pp[:, :], a["pp"])
            for i, n in enumerate(["L0_xattn_ln_g", "L0_xattn_ln_b", "L0_xattn_b_diff", "L0_xattn_b2", "L0_ffn_b_out",
                                   "L1_xattn_bo", "L1_xattn_bv"]):
                t = dma(Y, "wp", bc[:, i, :], bcast(n))
            return t

        def loads_a():
            dma(Y, "wa", WdT[:, :, :], a["WdT"])
            dma(Y, "wa", W1T[:, :, :], a["W1T"])
            return dma(Y, "wa", W2T[:, :, :], a["W2T"])

        def loads_b():
            dma(Y, "wb", Win[:, :, :], a["Win"])
            dma(Y, "wb", bin_[:, :], bcast("L0_ffn_b_in"))
            dma(Y, "wb", Wg[:, :, :], a["Wg"])
            dma(Y, "wb", bgate[:, :], bcast("L0_ffn_b_gate"))
            dma(Y, "wb", U[:, :], a["U"])
            dma(Y, "wb", io8[:, :], a["io8"])
            dma(Y, "wb", ioj[:, :], a["ioj"])
            dma(Y, "wb", Wout[:, :, :], a["Wout"])
            return dma(Y, "wb", b1m[:, :], a["b1m0"])

        t_oneset = V(lambda e: e.memset(ones[:, :], 1.0))
        t_idh = V(lambda e: e.tensor_copy(identh[:, :], ident[:, :]), ld["ident"])

        def vts(o, i, s1, s2, o0, o1, *w):
            return V(lambda e: e.tensor_scalar(o, i, s1, s2, o0, o1), *w)

        def vtt(o, x, y, op, *w, q=None):
            return (q or V)(lambda e: e.tensor_tensor(o, x, y, op), *w)

        def vstt(o, x, s, y, o0, o1, *w):
            return V(lambda e: e.scalar_tensor_tensor(out=o, in0=x, scalar=s, in1=y, op0=o0, op1=o1), *w)

        def vcopy(o, i, *w):
            return V(lambda e: e.tensor_copy(o, i), *w)

        def act(o, i, f, *w, bias=0.0, scale=1.0, accum=None):
            if accum is None:
                return A(lambda e: e.activation(o, i, f, bias=bias, scale=scale), *w)
            return A(lambda e: e.activation(o, i, f, bias=bias, scale=scale, accum_out=accum), *w)

        def acopy(o, i, *w):
            return act(o, i, ACT.Copy, *w)

        def mm(o, l, r, st, sp, *w, inc=False, skip=False):
            return T(lambda e: e.matmul(o, l, r, start=st, stop=sp, skip_group_check=skip), *w, inc=inc)

        def tr(o, i, idn, *w, inc=False):
            return T(lambda e: e.transpose(o, i, idn), *w, inc=inc)

        smalls = []

        def rsqrt(v, n, tmp, *w, parts=128):
            y, i1, t1, hv = (tmp[0:parts, k * n:(k + 1) * n] for k in range(4))
            c = V(lambda e: e.tensor_single_scalar(i1.bitcast(I32), v.bitcast(I32), 1, ALU.logical_shift_right), *w)
            vts(hv, v, -0.5, None, ALU.mult, ALU.bypass)
            c = V(lambda e: e.tensor_scalar(y.bitcast(I32), i1.bitcast(I32), -1.0, float(0x5f3759df), ALU.mult, ALU.add), c)
            for _ in range(4):
                c = vtt(t1, y, hv, ALU.mult, c)
                c = vtt(t1, t1, y, ALU.mult, c)
                c = vstt(y, t1, 1.5, y, ALU.add, ALU.mult, c)
            return y, c

        def ln_stats(tiles, zone, *w):
            n = len(tiles)
            st, mv, ve, tmp = zone(128, n, 6), zone(128, n, 2), zone(128, n), zone(128, 4 * n)
            for i, t in enumerate(tiles):
                wi = w[0][i] if isinstance(w[0], list) and len(w[0]) == n and len(w) == 1 else list(w)
                s = V(lambda e, i=i, t=t: e.bn_stats(st[:, i, :], t), wi)
            for i in range(n):
                g = V(lambda e, i=i: e.bn_aggr(mv[:, i, :], st[:, i, :]), s)
            c = vts(ve[:, :], mv[:, :, 1], 1e-5, None, ALU.add, ALU.bypass, g)
            y, c = rsqrt(ve[:, :], n, tmp[:, :], c)
            return [(mv[:, i, 0:1], y[:, i:i + 1]) for i in range(n)], c

        def weave(*gens):
            gens = [g for g in gens if g is not None]
            while gens:
                for g in list(gens):
                    if next(g, gens) is gens:
                        gens.remove(g)

        def beside(main, *sides, drain=True):
            due = [0.0] * len(sides)
            for _ in main:
                for i, (side, rate) in enumerate(sides):
                    due[i] += rate
                    while due[i] >= 1:
                        due[i] -= 1
                        next(side, None)
            for side, _ in sides:
                weave(side if drain else None)

        def pause(n):
            for _ in range(n):
                yield

        def chain(*gens):
            for g in gens:
                yield from g

        def keep(g, box):
            box += (yield from g)

        load_x(0)
        t_wc = dma(Y, "wc", Wqkv[:, 1:3, :, :], a["Wqkv"][:, 1:3])

        LNZ = Zone(SZ.start, 8 * K)
        CT = [Buf(MZ(128, 4, D + 1)) for _ in range(2)]
        Q = [Buf(MZ(128, 4, D)) for _ in range(3)]
        TQ, TC, LQ, LC = (Buf(MZ(128, 4, D)) for _ in range(4))
        DT = [Buf(MZ(128, 2, S)) for _ in range(2)]
        LT = [Buf(MZ(128, 2, S)) for _ in range(2)]
        ET = [Buf(MZ(128, 4, S)) for _ in range(2)]
        UB = Ring([MZ(128, D)[:, :] for _ in range(2)])
        UT = Ring([MZ(128, 2, 128)[:, :, :] for _ in range(2)])
        HT = [Buf(MZ(128, 2, S)) for _ in range(2)]
        gt_at = MZ.at
        GT = Ring([MZ(128, S)[:, :] for _ in range(16)])
        XB = [Buf(MZ(128, 4, D))]
        bT, bS, bY = banks([0, 1]), banks([2, 3, 4]), banks([5, 6, 7])
        t_neg = [V(lambda e, c=c: e.memset(c.ap[:, :, D:D + 1], -1.0)) for c in CT]
        st = {}

        def transpose4(ring, tiles, evac, *w):
            k = ring.take()
            for i, t in enumerate(tiles):
                tok = tr(k.ap[:, i * 128:(i + 1) * 128], t, ident[:, :], k.rel, ld["ident"], *w, inc=i == len(tiles) - 1)
            tok = evac(k.ap, tok)
            k.rel = [tok]
            return tok

        def pre(b):
            ct, q = CT[b % 2], Q[b % 3]
            tc = dma(Y, f"c{b % 2}", ct.ap[:, :, 0:D], cv[b], ct.rel)
            sc, tk = ln_stats([X[:, 4 * b + t, :] for t in range(4)], LNZ, tx[b])
            for t in range(4):
                tq = vts(q.ap[:, t, :], X[:, 4 * b + t, :], *sc[t], ALU.subtract, ALU.mult, tk, q.rel)
            yield from pause(2)
            sums, r = LNZ(128, 8), LNZ(128, 24)
            for t in range(4):
                th = act(TC.ap[:, t, :], ct.ap[:, t, 0:D], ACT.Tanh, tc, TC.rel, accum=sums[:, 4 + t:5 + t])
            for t in range(4):
                th = act(TQ.ap[:, t, :], q.ap[:, t, :], ACT.Tanh, tq, TQ.rel, accum=sums[:, t:t + 1])
            yield from pause(3)
            c = vts(r[:, 0:8], sums[:, :], 0.499, 128.0 + 1e-8, ALU.mult, ALU.add, th)
            c = V(lambda e: e.reciprocal(r[:, 0:8], r[:, 0:8]), c)
            vts(r[:, 8:16], r[:, 0:8], 0.499, None, ALU.mult, ALU.bypass, c)
            c = vts(r[:, 16:24], r[:, 0:8], 0.5, None, ALU.mult, ALU.bypass, c)
            yield
            for src, dst, o in ((TQ, LQ, 0), (TC, LC, 4)):
                for t in range(4):
                    tl = act(dst.ap[:, t, :], src.ap[:, t, :], ACT.Ln, c, dst.rel,
                             scale=r[:, 8 + o + t:9 + o + t], bias=r[:, 16 + o + t:17 + o + t])
            yield from pause(3)
            for src, o in ((TQ, 0), (TC, 4)):
                for t in range(4):
                    tp = vts(src.ap[:, t, :], src.ap[:, t, :], r[:, 8 + o + t:9 + o + t], r[:, 16 + o + t:17 + o + t],
                             ALU.mult, ALU.add, tl)
            tr_ = vtt(LQ.ap[:, :, :], LQ.ap[:, :, :], LC.ap[:, :, :], ALU.subtract, tl, q=G)
            td = vtt(TQ.ap[:, :, :], TQ.ap[:, :, :], TC.ap[:, :, :], ALU.subtract, tp)
            TC.rel, LC.rel = [td], [tr_]
            yield from pause(3)
            for c in range(2):
                e1 = transpose4(bT, [TQ.ap[:, t, c * 128:(c + 1) * 128] for t in range(4)],
                                lambda k, tok, c=c: acopy(DT[b % 2].ap[:, c, :], k, tok, DT[b % 2].rel), td)
                yield
            TQ.rel = [T.last()]
            tqb = vtt(q.ap[:, :, :], q.ap[:, :, :], bdiff.unsqueeze(1).to_broadcast([128, 4, D]), ALU.add, t_wp, th, tq, q=G)
            txb = vtt(X[:, 4 * b:4 * b + 4, :], X[:, 4 * b:4 * b + 4, :], lnb.unsqueeze(1).to_broadcast([128, 4, D]),
                      ALU.add, t_wp, tq, q=G)
            for c in range(2):
                e2 = transpose4(bT, [LQ.ap[:, t, c * 128:(c + 1) * 128] for t in range(4)],
                                lambda k, tok, c=c: acopy(LT[b % 2].ap[:, c, :], k, tok, LT[b % 2].rel), tr_)
                yield
            LQ.rel = [T.last()]
            st[b] = dict(tc=tc, e=[e1, e2], tqb=tqb, txb=txb)

        def s_exp(b):
            s = st[b]
            for mc in range(4):
                k = bS.take()
                for c in range(2):
                    tok = mm(k.ap, LT[b % 2].ap[:, c, mc * 128:(mc + 1) * 128], DT[b % 2].ap[:, c, :], c == 0, c == 1,
                             s["e"], k.rel, inc=c == 1)
                te = act(ET[b % 2].ap[:, mc, :], k.ap, ACT.Exp, tok, ET[b % 2].rel, scale=-1.0 / 16)
                k.rel = [te]
                yield
            DT[b % 2].rel = LT[b % 2].rel = [tok]
            s["te"] = te

        def rest(b):
            s, ct, q = st[b], CT[b % 2], Q[b % 3]
            rinv = LNZ(128, 4)
            tf, us = [], []
            for t in range(4):
                k = bY.take()
                for mc in range(4):
                    tok = mm(k.ap[:, 0:D + 1], ET[b % 2].ap[:, mc, t * 128:(t + 1) * 128], ct.ap[:, mc, :], mc == 0, mc == 3,
                             s["te"], s["tc"], t_neg, k.rel, inc=mc == 3)
                u = UB.take()
                c = V(lambda e, k=k, t=t: e.reciprocal(rinv[:, t:t + 1], k.ap[:, D:D + 1]), tok)
                c = vstt(u.ap, k.ap[:, 0:D], rinv[:, t:t + 1], ct.ap[:, t, 0:D], ALU.mult, ALU.add, c, u.rel)
                k.rel = [c]
                us.append((u, c))
                if t % 2 == 1:
                    yield
                    for tt in (t - 1, t):
                        u, c = us[tt]
                        kt = bT.take()
                        for cc in range(2):
                            tok = tr(kt.ap[:, cc * 128:(cc + 1) * 128], u.ap[:, cc * 128:(cc + 1) * 128], ident[:, :], c,
                                     kt.rel, inc=cc == 1)
                        u.rel = [tok]
                        ut = UT.take()
                        ev = acopy(ut.ap, kt.ap[:, 0:256].rearrange("p (c n) -> p c n", c=2), tok, ut.rel)
                        kt.rel = [ev]
                        ky = bY.take()
                        for cc in range(2):
                            tok = mm(ky.ap[:, 0:D], ut.ap[:, cc, :], WdT[:, cc, :], cc == 0, cc == 1, ev, t_wa, ky.rel,
                                     inc=cc == 1)
                        ut.rel = [tok]
                        f = vtt(q.ap[:, tt, :], ky.ap[:, 0:D], q.ap[:, tt, :], ALU.add, tok, s["tqb"])
                        ky.rel = [f]
                        tf.append(f)
                        yield
            ET[b % 2].rel = [tok]
            ct.rel = [T.last(), V.last()]
            sc, tk = ln_stats([q.ap[:, t, :] for t in range(4)], LNZ, tf)
            z = UZ[b % 2]
            for t in range(4):
                tz = vts(z.ap[:, t, :], q.ap[:, t, :], *sc[t], ALU.subtract, ALU.mult, tk, z.rel)
            tfb = vtt(q.ap[:, :, :], q.ap[:, :, :], b2a.unsqueeze(1).to_broadcast([128, 4, D]), ALU.add, tz, q=G)
            yield
            for c in range(2):
                eh = transpose4(bT, [z.ap[:, t, c * 128:(c + 1) * 128] for t in range(4)],
                                lambda k, tok, c=c: vts(HT[b % 2].ap[:, c, :], k, pp[:, c:c + 1], pp[:, 2 + c:3 + c],
                                                        ALU.mult, ALU.add, tok, HT[b % 2].rel), tz)
            z.rel = [T.last()]
            s["eh"], s["tfb"] = eh, tfb
            yield

        def mlp(b):
            s, q = st[b], Q[b % 3]
            gts = []
            for hc in range(8):
                k, g = bS.take(), GT.take()
                for c in range(2):
                    tok = mm(k.ap, W1T[:, c, hc * 128:(hc + 1) * 128], HT[b % 2].ap[:, c, :], c == 0, c == 1, s["eh"],
                             k.rel, inc=c == 1)
                tg = act(g.ap, k.ap, ACT.Gelu, tok, g.rel, bias=pp[:, 4 + hc:5 + hc])
                k.rel = [tg]
                gts.append((g, tg))
                yield
            HT[b % 2].rel = [tok]
            to = []
            for t in range(4):
                k = bY.take()
                for hc in range(8):
                    g, tg = gts[hc]
                    tok = mm(k.ap[:, 0:D], g.ap[:, t * 128:(t + 1) * 128], W2T[:, hc, :], hc == 0, hc == 7, tg, k.rel,
                             inc=hc == 7)
                    if t == 3:
                        g.rel = [(T.sem, T.n + (hc < 7))]
                o = vtt(q.ap[:, t, :], k.ap[:, 0:D], q.ap[:, t, :], ALU.add, tok, s["tfb"])
                k.rel = [o]
                to.append(o)
                yield
            sc, tk = ln_stats([q.ap[:, t, :] for t in range(4)], LNZ, to)
            z = XB[0]
            for t in range(4):
                tz = vts(z.ap[:, t, :], q.ap[:, t, :], *sc[t], ALU.subtract, ALU.mult, tk, z.rel)
            q.rel = [tz]
            tm = vtt(z.ap[:, :, :], z.ap[:, :, :], lng.unsqueeze(1).to_broadcast([128, 4, D]), ALU.mult, tz)
            s["x1"] = vtt(X[:, 4 * b:4 * b + 4, :], X[:, 4 * b:4 * b + 4, :], z.ap[:, :, :], ALU.add, tm, s["txb"])
            z.rel = [s["x1"]]
            yield

        UZ = [Buf(MZ(128, 4, D)) for _ in range(1)] * 2

        kd = nc.dram_tensor("kd", (NB, 2, 128, 2, S), F32, kind="Internal").ap()
        qd = nc.dram_tensor("qd", (NB, 2, 128, 2, S), F32, kind="Internal").ap()
        md = nc.dram_tensor("md", (NB, NH, S), F32, kind="Internal").ap()
        vd = nc.dram_tensor("vd", (NB, 128, 4, NH, 64), F16, kind="Internal").ap()
        tkd, tvd = {}, {}

        def project(ring, hl, src, wi, bi, c, *w):
            k = ring.take()
            for kk in range(2):
                tok = mm(k.ap, Wqkv[:, wi, kk, c * 128:(c + 1) * 128], src[:, kk, :], kk == 0, kk == 1, *w, k.rel, t_wc if wi == 1 else t_wd,
                         inc=kk == 1)
            hi = hl.ap[:, 0, :]
            th = act(hi, k.ap, ACT.Identity, tok, hl.rel, t_wp, bias=pp[:, bi + c:bi + c + 1])
            tl = vstt(hl.ap[:, 1, :], k.ap, pp[:, bi + c:bi + c + 1], hi.bitcast(F32), ALU.add, ALU.subtract, th, hl.rel)
            k.rel = [tl]
            return th, tl

        ctts = {}

        def kv_load(b):
            ct = KVC.take()
            ctts[b] = ct, dma(Y, f"ctt{b % 2}", ct.ap, a["ctxT"][b], ct.rel)

        def kv(b):
            ct, tct = ctts[b]
            for c in range(2):
                hl = KHL.take()
                th, tl = project(bS, hl, ct.ap, 1, 14, c, tct)
                tw = dma(G, f"kw{c}", kd[b].rearrange("q p c n -> p q c n")[:, :, c, :], hl.ap.bitcast(F32), th, tl)
                tkd[b] = tkd.get(b, []) + [tw]
                hl.rel = [tw]
                yield
            for t in range(4):
                k, f = bY.take(), VF.take()
                for kk in range(2):
                    tok = mm(k.ap[:, 0:D], ct.ap[:, kk, t * 128:(t + 1) * 128], Wqkv[:, 2, kk, :], kk == 0, kk == 1,
                             tct, k.rel, t_wc, inc=kk == 1)
                c = vstt(f.ap, k.ap[:, 0:D], VS, bv64[:, :], ALU.mult, ALU.add, tok, t_bv, f.rel)
                k.rel = [c]
                fv = f.ap.rearrange("p (h d) -> p h d", d=16)
                th = acopy(VAB.ap[:, t, :, 0:16], fv, c, VAB.rel, t_va)
                tl = vtt(VAB.ap[:, t, :, 32:48], fv, VAB.ap[:, t, :, 0:16], ALU.subtract, th)
                f.rel = [tl]
                yield
            ct.rel = [tok]
            if b + 2 < NB:
                kv_load(b + 2)
            tvd[b] = dma(G, f"vw{b}", vd[b], VAB.ap, tl)
            VAB.rel = [tvd[b]]

        gz = Zone(gt_at, 32 * K)
        KVC = Ring([gz(128, 2, S) for _ in range(2)])
        KHL = Ring([gz(128, 2, S, dt=F32R) for _ in range(2)])
        VAB = Buf(gz(128, 4, NH, 64, dt=F16))
        VF = Ring([gz(128, D) for _ in range(2)])
        bv64 = gz(128, D)
        t_wp = loads_p()
        t_bv = vts(bv64[:, :], bv, VS, None, ALU.mult, ALU.bypass, t_wp)
        t0 = V(lambda e: e.memset(VAB.ap[:, :, :, 16:64], 0.0))
        t_va = V(lambda e: e.memset(VAB.ap[:, :, :, 16:17], VS), t0)
        kvs = chain(*[kv(b) for b in range(NB)])
        def head(b):
            yield from pre(b)
            yield from s_exp(b)

        h0 = head(0)
        kv_load(0)
        next(h0)
        kv_load(1)
        load_x(1)
        t_wa = loads_a()
        load_x(2)
        load_x(3)
        t_wd = dma(Y, "wd", Wqkv[:, ::3, :, :], a["Wqkv"][:, ::3])
        t_wb = loads_b()
        beside(h0, (kvs, 1.0), drain=False)
        for b in range(NB):
            weave(head(b + 1) if b + 1 < NB else None, rest(b), mlp(b - 1) if b else kvs)
            if b == 0:
                held((GT,), [*tkd[NB - 1], tvd[NB - 1], T.last(), V.last(), A.last()])
        weave(mlp(NB - 1))

        def finish():
            ov = out.rearrange("b (t p) d -> p (b t) d", p=128)
            t = dma(Y, "out", ov, X[:, :, :], everyone())
            Y(lambda e: e.wait_ge(*t), inc=False)

        def emit():
            block = ctx.enter_context(nc.Block())

            @block.sync
            def _(eng):
                Y.play(eng)

            @block.gpsimd
            def _(eng):
                G.play(eng)

            @block.scalar
            def _(eng):
                A.play(eng)

            @block.vector
            def _(eng):
                V.play(eng)

            @block.tensor
            def _(eng):
                T.play(eng)

        if stop == 1:
            finish()
            emit()
            return


        bar = everyone()
        buf0 = nc.dram_tensor("buf0", (N0 * TOK, 2 * D), F16, kind="Internal").ap()
        obuf0 = nc.dram_tensor("obuf0", (N0 * TOK, D), F32, kind="Internal").ap()

        def zero_rows(buf, n, zone, *w):
            zt = zone(128, 2 * D, dt=F16)
            tz = V(lambda e: e.memset(zt[:, :], 0.0), *w)
            return dma(Y, buf.tensor.name, buf.rearrange("(j p) d -> p j d", p=128),
                       zt[:, :].unsqueeze(1).to_broadcast([128, n * SUB, 2 * D]), tz)

        class Weights:

            def __init__(self, zone, e1, e2):
                self.w1h, self.w1l = zone(128, e1, dt=F16), zone(128, e1, dt=F16)
                self.w2h, self.w2l = zone(128, e2, dt=F16), zone(128, e2, dt=F16)
                self.t1, self.t2 = [], []

        CH = 1024

        def split_weights(src, hi, lo, n, ring, tag, *w):
            toks = []
            for i in range(n // CH):
                s = ring.take()
                r = slice(i * CH, (i + 1) * CH)
                td = dma(Y, f"{tag}{ring.at % len(ring.bufs)}", s.ap, src[:, r], s.rel, *w)
                th = act(hi[:, r], s.ap, ACT.Copy, td, *w, scale=WS)
                tl = vstt(lo[:, r], s.ap, WS, hi[:, r], ALU.mult, ALU.subtract, th, td)
                s.rel = [tl]
                toks = [tl]
                yield
            return toks

        def routing(ns, idx, nt_max, zone, *w):
            O = [zone(128, NT, E) for _ in range(ns)]
            M = O[0] if ns == 1 else zone(128, NT, E)
            C = [zone(128, NT, E) for _ in range(2)]
            tot, tmp = zone(128, NT, E), zone(128, NT, E)
            sm, smi, cmp, tef = zone(128, 6, E), zone(128, E), zone(1, nt_max, E), zone(1, nt_max)
            tei = [zone(1, nt_max) for _ in range(3)]
            pf, pi = zone(128, ns, NT), zone(128, ns, NT)
            io = io8[:, :].unsqueeze(1).to_broadcast([128, NT, E])
            for s in range(ns):
                c = vtt(O[s][:, :, :], io, idx[:, s, :].unsqueeze(2).to_broadcast([128, NT, E]), ALU.is_equal, *w)
            if ns == 2:
                c = vtt(M[:, :, :], O[0][:, :, :], O[1][:, :, :], ALU.add, c)
            m2 = M[:, :, :].rearrange("p t e -> p (t e)")
            k1, k2 = bY.take(), bY.take()
            mm(k1.ap[:, 0:128], U[:, :], m2, True, True, c, k1.rel, *w)
            tp = mm(k2.ap[:, 0:128], ones[:, :], m2, True, True, k2.rel, t_oneset, inc=True)
            c = vcopy(tot[:, :, :], k2.ap[:, 0:128].rearrange("p (t e) -> p t e", e=E), tp)
            k2.rel = [c]
            cur = tot
            for i, sh in enumerate((1, 2, 4, 8)):
                nx = C[i % 2]
                vcopy(nx[:, 0:sh, :], cur[:, 0:sh, :], c)
                c = vtt(nx[:, sh:, :], cur[:, sh:, :], cur[:, 0:NT - sh, :], ALU.add, c)
                cur = nx
            V(lambda e: e.tensor_scalar(smi[:, :].bitcast(I32), cur[:, NT - 1, :], float(TOK - 1), None, ALU.add, ALU.bypass), c)
            c = V.last()
            c = V(lambda e: e.tensor_single_scalar(smi[:, :].bitcast(I32), smi[:, :].bitcast(I32), 8, ALU.logical_shift_right), c)
            c = vcopy(sm[:, 0, :], smi[:, :].bitcast(I32), c)
            p = 0
            for i, sh in enumerate((1, 2, 4)):
                vcopy(sm[:, i + 1, 0:sh], sm[:, p, 0:sh], c)
                c = vtt(sm[:, i + 1, sh:], sm[:, p, sh:], sm[:, p, 0:E - sh], ALU.add, c)
                p = i + 1
            vtt(sm[:, 4, :], sm[:, 3, :], sm[:, 0, :], ALU.subtract, c)
            ce = vtt(cmp[:, :, :], sm[0:1, 3, :].unsqueeze(1).to_broadcast([1, nt_max, E]),
                     ioj[0:1, 0:nt_max].unsqueeze(2).to_broadcast([1, nt_max, E]), ALU.is_le, c)
            ce = V(lambda e: e.tensor_reduce(tef[:, :], cmp[:, :, :], AX.X, ALU.add), ce)
            return O, M, C, cur, tot, tmp, sm, k1, ce, tef, tei, pf, pi, c

        def positions(ns, r, hc):
            O, M, C, cur, tot, tmp, sm, k1, ce, tef, tei, pf, pi, c = r
            n2 = 2 * hc * 128
            vts(tei[0][:, :].bitcast(I32), tef[:, :], float(E - 1), float(n2), ALU.min, ALU.mult, ce)
            vts(tei[1][:, :].bitcast(I32), tef[:, :], float(E - 1), float(hc), ALU.min, ALU.mult, ce)
            te = vts(tei[2][:, :].bitcast(I32), tef[:, :], float(E - 1), float(D), ALU.min, ALU.mult, ce)
            c = vtt(tmp[:, :, :], cur[:, :, :], tot[:, :, :], ALU.subtract, c)
            c = vtt(tmp[:, :, :], k1.ap[:, 0:128].rearrange("p (t e) -> p t e", e=E), tmp[:, :, :], ALU.add, c)
            k1.rel = [c]
            c = vstt(tmp[:, :, :], sm[:, 4, :].unsqueeze(1).to_broadcast([128, NT, E]), float(TOK), tmp[:, :, :],
                     ALU.mult, ALU.add, c)
            for s in range(ns):
                o = C[s % 2]
                c2 = vtt(o[:, :, :], O[s][:, :, :], tmp[:, :, :], ALU.mult, c)
                c2 = V(lambda e, s=s, o=o: e.tensor_reduce(pf[:, s, :], o[:, :, :], AX.X, ALU.add), c2)
                c2 = vcopy(pi[:, s, :].bitcast(U32), pf[:, s, :], c2)
            return pi, tei, te, c2

        def scatter(buf, rows, pi, ns, tag, *w):
            for t in range(NT):
                for s in range(ns):
                    name = tag
                    chans.setdefault(name, [sem("d_" + name) if name not in chans else chans[name][0], 0])
                    ch = chans[name]
                    ch[1] += 16
                    G(lambda e, t=t, s=s, ch=ch: e.indirect_dma_start(
                        out=buf, out_offset=bass.IndirectOffsetOnAxis(ap=pi[:, s, t:t + 1].bitcast(U32), axis=0),
                        in_=rows[:, t, :], in_offset=None).then_inc(ch[0], 16), *w, inc=False)
            return (ch[0], ch[1])

        def experts(zone, buf, obuf, n, HC, W, func, b1m, b2m, tei, tag, *w):
            xr = Ring([zone(128, SUB, 2 * D, dt=F16) for _ in range(2)])
            xt = Ring([zone(128, 4, TOK, dt=F16) for _ in range(2)])
            m32 = Ring([zone(128, 2, TOK) for _ in range(2)])
            mh = Ring([zone(128, 2, TOK, dt=F16) for _ in range(HC // 2 + 2)])
            ml = Ring([zone(128, 2, TOK, dt=F16) for _ in range(HC // 2 + 2)])
            ob = Ring([zone(128, SUB, D) for _ in range(2)])
            bX, bU, bD = banks([0, 1]), banks([2, 3, 4]), banks([5, 6, 7])
            for r_ in (bX, bU, bD):
                for bb in r_.bufs:
                    bb.rel = flat(w)
            bv_ = buf.rearrange("(j s p) d -> j p s d", p=128, s=SUB)
            ov_ = obuf.rearrange("(j s p) d -> j p s d", p=128, s=SUB)
            regs = {}

            def reg(q, key, src, top):
                def go(e):
                    regs[key] = e.value_load(src, min_val=0, max_val=top)
                q(go, *w, inc=False)

            def load(j):
                x = xr.take()
                td = dma(Y, f"{tag}x{xr.at % 2}", x.ap, bv_[j], x.rel, *w)
                k = bX.take()
                kh = k.ap.bitcast(F16).rearrange("p (c n) -> p c n", c=4)
                for s in range(SUB):
                    for c in range(4):
                        tok = tr(kh[:, c, s * 128:(s + 1) * 128], x.ap[:, s, c * 128:(c + 1) * 128], identh[:, :], td,
                                 t_idh, k.rel, inc=s == SUB - 1 and c == 3)
                x.rel = [tok]
                xx = xt.take()
                ev = vcopy(xx.ap, kh, tok, xx.rel)
                k.rel = [ev]
                return xx, ev

            nxt = load(0)
            tout = None
            for j in range(n):
                xx, ev = nxt
                reg(T, ("t", j), tei[0][0:1, j:j + 1].bitcast(I32), (E - 1) * 2 * HC * 128)
                reg(A, ("a", j), tei[1][0:1, j:j + 1].bitcast(I32), (E - 1) * HC)
                reg(V, ("v", j), tei[2][0:1, j:j + 1].bitcast(I32), (E - 1) * D)
                mids = []
                for g in range(HC // 2):
                    k = bU.take()
                    for h2 in range(2):
                        hc = 2 * g + h2
                        o = k.ap[:, h2 * TOK:(h2 + 1) * TOK]
                        seq = [(W.w1h, c, c) for c in range(2)] + [(W.w1h, c, 2 + c) for c in range(2)] + \
                              [(W.w1l, c, c) for c in range(2)]
                        for i, (ww, c, xc) in enumerate(seq):
                            off = c * HC * 128 + hc * 128
                            tok = T(lambda e, o=o, ww=ww, off=off, xx=xx, xc=xc, i=i, j=j: e.matmul(
                                o, ww[:, bass.ds(regs["t", j] + off, 128)], xx.ap[:, xc, :], start=i == 0, stop=i == 5),
                                ev, k.rel, W.t1, inc=i == 5)
                    m = m32.take()
                    for h2 in range(2):
                        hc = 2 * g + h2
                        ta = A(lambda e, m=m, k=k, h2=h2, hc=hc, j=j: e.activation(
                            m.ap[:, h2, :], k.ap[:, h2 * TOK:(h2 + 1) * TOK], func,
                            bias=b1m[:, bass.ds(regs["a", j] + hc, 1)], scale=1.0 / WS), tok, m.rel)
                    k.rel = [ta]
                    h, l = mh.take(), ml.take()
                    th = vcopy(h.ap, m.ap, ta, h.rel)
                    tl = vtt(l.ap, m.ap, h.ap, ALU.subtract, th, l.rel)
                    m.rel = [tl]
                    mids.append((h, l, tl))
                xx.rel = [tok]
                if j + 1 < n:
                    nxt = load(j + 1)
                o2 = ob.take()
                for s in range(SUB):
                    k = bD.take()
                    i, last = 0, HC * 3 - 1
                    for hc in range(HC):
                        h, l, tl = mids[hc // 2]
                        for src, ww in ((h, W.w2h), (l, W.w2h), (h, W.w2l)):
                            tok = T(lambda e, k=k, src=src, hc=hc, s=s, ww=ww, i=i, j=j, last=last: e.matmul(
                                k.ap[:, 0:D], src.ap[:, hc % 2, s * 128:(s + 1) * 128],
                                ww[:, bass.ds(regs["t", j] + hc * D, D)], start=i == 0, stop=i == last),
                                tl, k.rel, W.t2, inc=i == last)
                            i += 1
                    tv = V(lambda e, o2=o2, k=k, s=s, j=j: e.scalar_tensor_tensor(
                        out=o2.ap[:, s, :], in0=k.ap[:, 0:D], scalar=1.0 / WS,
                        in1=b2m[:, bass.ds(regs["v", j], D)], op0=ALU.mult, op1=ALU.add), tok, o2.rel)
                    k.rel = [tv]
                for h, l, tl in mids:
                    h.rel = l.rel = [tok]
                to = dma(Y, f"{tag}o{ob.at % 2}", ov_[j], o2.ap, tv)
                o2.rel = [to]
                tout = ([tout] if tout else []) + [to] if j >= n - 2 else None
            return [t for t in flat(tout)]

        def gather(obuf, pi, s, t, dst, name, *w):
            chans.setdefault(name, [sem("d_" + name) if name not in chans else chans[name][0], 0])
            ch = chans[name]
            ch[1] += 16
            G(lambda e: e.indirect_dma_start(
                out=dst, out_offset=None, in_=obuf,
                in_offset=bass.IndirectOffsetOnAxis(ap=pi[:, s, t:t + 1].bitcast(U32), axis=0)).then_inc(ch[0], 16),
                *w, inc=False)
            return (ch[0], ch[1])

        MZ.reset()
        SZ.reset()
        W0 = Weights(MZ, E * 2 * H0, E * 2 * H0)
        LNZ = Zone(SZ.start, 19 * K)
        HLz = Zone(WA.start, 20 * K)
        HL = HLz(128, NT, 2 * D, dt=F16)
        b2m0 = LNZ(128, E * D)
        SRZ = Zone(LNZ.at, 8 * K)
        SR = Ring([LNZ(128, CH)[:, :] for _ in range(2)])
        tr0 = Zone(MZ.start + 96 * K, 32 * K)
        XN, XT_, HF, HT_ = (Buf(tr0(128, 4, D), bar) for _ in range(4))
        lgz = tr0(128, NT, E)
        rz = Zone(tr0.at, tr0.end - tr0.at)
        tb2 = dma(Y, "b2m0", b2m0[:, :], a["L0_ffn_b2"].rearrange("e d -> (e d)").partition_broadcast(128), bar)
        tzero0 = zero_rows(buf0, N0, rz, bar)
        bT, bS, bY = banks([0, 1]), banks([2, 3, 4]), banks([5, 6, 7])
        for r_ in (bT, bS, bY):
            for bb in r_.bufs:
                bb.rel = bar
        top, idxu = rz(128, NT, 8), rz(128, NT, 8)
        idxf, ww = rz(128, 2, NT), LNZ(128, 3, NT)
        lnz2 = Zone(rz.at, 2 * K)
        rz = Zone(lnz2.end, tr0.end - lnz2.end)

        def moe_pre(b):
            sc, tk = ln_stats([X[:, 4 * b + t, :] for t in range(4)], lnz2, bar)
            for t in range(4):
                c = vts(XN.ap[:, t, :], X[:, 4 * b + t, :], *sc[t], ALU.subtract, ALU.mult, tk, XN.rel)
            yield
            xt4 = XT_.ap[:, :, :].rearrange("p a n -> p (a n)").rearrange("p (c n) -> p c n", c=2)
            for c2 in range(2):
                ev = transpose4(bT, [XN.ap[:, t, c2 * 128:(c2 + 1) * 128] for t in range(4)],
                                lambda k, tok: acopy(xt4[:, c2, :], k, tok, XT_.rel), c)
            XN.rel = [T.last()]
            yield
            for t in range(4):
                k = bY.take()
                for c2 in range(2):
                    tok = mm(k.ap[:, 0:D], xt4[:, c2, t * 128:(t + 1) * 128], Win[:, c2, :], c2 == 0, c2 == 1, ev, t_wb,
                             k.rel, inc=c2 == 1)
                th = vtt(HF.ap[:, t, :], k.ap[:, 0:D], bin_[:, :], ALU.add, tok, HF.rel)
                k.rel = [th]
            XT_.rel = [tok]
            yield
            hs = HL[:, 4 * b:4 * b + 4, :]
            tc_ = acopy(hs[:, :, 0:D], HF.ap[:, :, :], th)
            tl = vtt(hs[:, :, D:2 * D], HF.ap[:, :, :], hs[:, :, 0:D], ALU.subtract, tc_)
            ht4 = HT_.ap[:, :, :].rearrange("p a n -> p (a n)").rearrange("p (c n) -> p c n", c=2)
            for c2 in range(2):
                ev = transpose4(bT, [HF.ap[:, t, c2 * 128:(c2 + 1) * 128] for t in range(4)],
                                lambda k, tok: acopy(ht4[:, c2, :], k, tok, HT_.rel), th)
            HF.rel = [T.last(), tl]
            yield
            k = bY.take()
            for t in range(4):
                for c2 in range(2):
                    tok = mm(k.ap[:, t * E:(t + 1) * E], ht4[:, c2, t * 128:(t + 1) * 128], Wg[:, c2, :], c2 == 0, c2 == 1,
                             ev, t_wb, k.rel, inc=c2 == 1)
            HT_.rel = [tok]
            lg = lgz[:, 4 * b:4 * b + 4, :]
            c = vtt(lg, k.ap[:, 0:4 * E].rearrange("p (t e) -> p t e", e=E), bgate[:, :].unsqueeze(1).to_broadcast([128, 4, E]),
                    ALU.add, tok)
            k.rel = [c]
            for t in range(4):
                tt = 4 * b + t
                cm = V(lambda e, tt=tt: e.max(top[:, tt, :], lgz[:, tt, :]), c)
            for t in range(4):
                tt = 4 * b + t
                ci = V(lambda e, tt=tt: e.max_index(idxu[:, tt, :].bitcast(U32), top[:, tt, :], lgz[:, tt, :]), cm)
            st[b]["i"], st[b]["hl"] = ci, tl
            yield

        sp1 = keep(split_weights(a["w1m0"], W0.w1h, W0.w1l, E * 2 * H0, SR, "wm", bar), W0.t1)
        weave(chain(*[moe_pre(b) for b in range(NB)]), sp1)
        cis, hls = [st[b]["i"] for b in range(NB)], [st[b]["hl"] for b in range(NB)]
        c = vcopy(idxf[:, :, :], idxu[:, :, 0:2].bitcast(U32).rearrange("p t s -> p s t"), cis)
        d01 = LNZ(128, NT)
        c1 = vtt(d01[:, :], top[:, :, 1], top[:, :, 0], ALU.subtract, cis)
        c1 = act(d01[:, :], d01[:, :], ACT.Exp, c1)
        c1 = vts(ww[:, 2, :], d01[:, :], 1.0, None, ALU.add, ALU.bypass, c1)
        c1 = V(lambda e: e.reciprocal(ww[:, 0, :], ww[:, 2, :]), c1)
        tw = vtt(ww[:, 1, :], d01[:, :], ww[:, 0, :], ALU.mult, c1)
        r = routing(2, idxf, N0, rz, c, t_wb)
        pi0z = Zone(PZ.at, PZ.end - PZ.at)
        rr = list(r)
        pi_keep = LNZ(128, 2, NT)
        tei_keep = [LNZ(1, N0) for _ in range(3)]
        rr[10], rr[12] = tei_keep, pi_keep
        pi0, tei0, te0, tpos = positions(2, rr, 8)
        tsc = scatter(buf0, HL, pi0, 2, "sc0", tpos, hls, tzero0)
        weave(keep(split_weights(a["w2m0"], W0.w2h, W0.w2l, E * 2 * H0, SR, "wm", [tpos, te0, tw, tzero0]), W0.t2))
        SRZ.reset()
        ez = Zones(Zone(WA.start, 20 * K), Zone(LNZ.at, LNZ.end - LNZ.at), SRZ)
        te0 = experts(ez, buf0, obuf0, N0, 8, W0, ACT.Relu, b1m, b2m0, tei0, "e0", tsc, te0, tb2, t_wb, W0.t2)

        bar = everyone()
        MZ.reset()
        cz = Zone(MZ.start, 128 * K)
        GB = Ring([cz(128, 2, D)[:, :, :] for _ in range(4)])
        MO = [cz(128, 4, D) for _ in range(2)]
        MT = [Buf(cz(128, 2, S)) for _ in range(2)]
        bT, bY = banks([0, 1, 2]), banks([3, 4, 5, 6, 7])
        for r_ in (bT, bY):
            for bb in r_.bufs:
                bb.rel = bar

        def combine(b):
            mo, mt = MO[b % 2], MT[b % 2]
            txo = vtt(X[:, 4 * b:4 * b + 4, :], X[:, 4 * b:4 * b + 4, :], bout.unsqueeze(1).to_broadcast([128, 4, D]),
                      ALU.add, bar, q=G)
            gs = []
            for t in range(4):
                tt = 4 * b + t
                g = GB.take()
                for s in range(2):
                    tg = gather(obuf0, pi0, s, tt, g.ap[:, s, :], f"g0{GB.at % 4}", te0, g.rel)
                gs.append((g, tg))
            for t in range(4):
                tt = 4 * b + t
                g, tg = gs[t]
                c = vts(mo[:, t, :], g.ap[:, 0, :], ww[:, 0, tt:tt + 1], None, ALU.mult, ALU.bypass, tg, tw, bar, st[b].get("mo"))
                c = vstt(mo[:, t, :], g.ap[:, 1, :], ww[:, 1, tt:tt + 1], mo[:, t, :], ALU.mult, ALU.add, c)
                g.rel = [c]
            for c2 in range(2):
                ev = transpose4(bT, [mo[:, t, c2 * 128:(c2 + 1) * 128] for t in range(4)],
                                lambda k, tok: acopy(mt.ap[:, c2, :], k, tok, mt.rel), c)
            st[(b + 2)] = dict(st.get(b + 2, {}), mo=T.last())
            for t in range(4):
                k = bY.take()
                for c2 in range(2):
                    tok = mm(k.ap[:, 0:D], mt.ap[:, c2, t * 128:(t + 1) * 128], Wout[:, c2, :], c2 == 0, c2 == 1, ev, k.rel,
                             t_wb, inc=c2 == 1)
                tx2 = vtt(X[:, 4 * b + t, :], k.ap[:, 0:D], X[:, 4 * b + t, :], ALU.add, tok, txo)
                k.rel = [tx2]
            mt.rel = [tok]
            return tx2

        x2 = [combine(b) for b in range(NB)]
        if stop == 2:
            finish()
            emit()
            return

        def qprep(b, *w):
            s = st3[b]
            sc, tk = ln_stats([X[:, 4 * b + t, :] for t in range(4)], AZ, *w)
            for t in range(4):
                c = vts(XN_.ap[:, t, :], X[:, 4 * b + t, :], *sc[t], ALU.subtract, ALU.mult, tk, XN_.rel)
            yield from pause(GAP + 2)
            xt = XTR.take()
            for c2 in range(2):
                ev = transpose4(bX, [XN_.ap[:, t, c2 * 128:(c2 + 1) * 128] for t in range(4)],
                                lambda k, tok, c2=c2: vcopy(xt.ap[:, c2, :], k, tok, xt.rel), c)
                yield from pause(GAP)
            XN_.rel = [T.last()]
            s["txb"] = vtt(X[:, 4 * b:4 * b + 4, :], X[:, 4 * b:4 * b + 4, :], bo.unsqueeze(1).to_broadcast([128, 4, D]),
                           ALU.add, c, t_wp, q=G)
            for c2 in range(2):
                hl = QHL.take()
                th, tl = project(bX, hl, xt.ap, 0, 12, c2, ev)
                tq = dma(Y, f"qw{c2}", qd[b].rearrange("q p c n -> p q c n")[:, :, c2, :], hl.ap.bitcast(F32), th, tl)
                s["qd"] = s.get("qd", []) + [tq]
                hl.rel = [tq]
                yield from pause(GAP)
            xt.rel = [T.last()]

        def load_qk(b, which, half):
            s, sl = st3[b], slice(4 * half, 4 * half + 4)
            if which == "q":
                dv = QS[b % 2][:, :, :].bitcast(F32)
                src, order, tok, rel = qd[b], (0, 0, 1), s["qd"], qrel[b % 2, half]
            else:
                dv = KS[b % 2][:, :, :].bitcast(F32).rearrange("p (s j) n -> p j s n", j=2)
                src, order, tok, rel = kd[b], (0, 1, 0), tkd[b], krel[b % 2, half]
            sv = src.rearrange("q (j r b) c n -> j q r (b c) n", j=2, r=16)
            for j in range(2):
                for g in range(3):
                    r0 = 64 * j + 16 * g
                    d = dv[r0:r0 + 16, sl] if which == "q" else dv[r0:r0 + 16, j, sl]
                    t = dma(Y, f"{which}s{b % 2}{half}", d, sv[j, order[g]][:, sl], tok, rel)
            if which == "q":
                for j in range(2):
                    t = dma(Y, f"qs{b % 2}{half}", QS[b % 2][64 * j + 48:64 * j + 49, sl, :].bitcast(F32),
                            MT_.ap[32:33, :].bitcast(F32).unsqueeze(1).to_broadcast([1, 4, S]), tz, rel)
            s[which, half] = t

        def load_v(b):
            st3[b]["v"] = dma(Y, f"va{b % 2}", VA[b % 2].ap, vd[b], tvd[b], VA[b % 2].rel)
            yield

        def maxima(b, ahead=None):
            s, mx = st3[b], MXB[b % 2]
            for half in range(2):
                for t in range(4):
                    if ahead is not None and (half, t) == (1, 1):
                        load_half(ahead, 0)
                    for h in range(8 * half, 8 * half + 8):
                        k = bM.take()
                        tok = mm(k.ap, QS[b % 2][:, h // 2, t * 128:(t + 1) * 128], KS[b % 2][:, h, :],
                                 True, True, s["q", half], s["k", half], k.rel, inc=True)
                        tm = V(lambda e, t=t, h=h, k=k: e.tensor_reduce(mx[:, t, h:h + 1], k.ap, AX.X, ALU.max), tok)
                        k.rel = [tm]
                        yield
            k = bX.take()
            for t in range(4):
                tt = tr(k.ap[0:16, t * 128:(t + 1) * 128], mx[:, t, :], ident[:, :], tm, k.rel, inc=t == 3)
            te = vts(MT_.ap[0:16, :], k.ap[0:16, :], -1.0, None, ALU.mult, ALU.bypass, tt, MT_.rel)
            k.rel = [te]
            tm = MT_.rel = [dma(Y, "md", md[b], MT_.ap[0:16, :].bitcast(F32), te)]
            for j in range(2):
                tq = dma(Y, f"qm{b % 2}", QS[b % 2][64 * j + 48:64 * j + 49, :, :].bitcast(F32),
                         md[b].rearrange("(s j) n -> j s n", j=2)[j:j + 1], tm, tok)
            s["m"] = tq
            yield

        LAG, RATE, GAP = 4, 1.15, 4

        def attend(b, share):
            s, va = st3[b], VA[b % 2]
            cxv = CX.ap.rearrange("p a n -> p (a n)").rearrange("p (t h d) -> p t h d", t=4, h=NH)
            pend, late = [], []

            def av(ko, j, h, kp, eh, el, th, tl):
                for i in range(2):
                    kc = 2 * kp + i
                    for e_, te in ((eh, th), (el, tl)):
                        tok = mm(ko.ap[64 * j:64 * j + 64, :], va.ap[:, kc, h, :], e_.ap[:, i, :], kc == 0 and e_ is eh,
                                 kc == 3 and e_ is el, te, s["v"], ko.rel, inc=i == 1)
                        e_.rel = [tok]
                if j == 1 and kp == 1:
                    o = OS.take()
                    ev = vcopy(o.ap, ko.ap, tok, o.rel)
                    ko.rel = [ev]
                    late.append((h // 2, o, ev))

            def norm(g, o, ev):
                k, rc = bX.take(), RC.take()
                for t in range(4):
                    tok = tr(k.ap[:, t * 128:(t + 1) * 128], o.ap[:, t * 128:(t + 1) * 128], ident[:, :], ev, k.rel, inc=t == 3)
                o.rel = [tok]
                kv = k.ap.rearrange("p (t j x) -> p t j x", t=4, j=2)
                c = V(lambda e: e.reciprocal(rc.ap[:, :, :, 0], kv[:, :, :, 16]), tok)
                dst = cxv[:, :, 2 * g:2 * g + 2, :]
                c1 = vtt(dst, kv[:, :, :, 0:16], rc.ap.to_broadcast([128, 4, 2, 16]), ALU.mult, c, CX.rel)
                tm = RD.take()
                c2 = vtt(tm.ap, kv[:, :, :, 32:48], rc.ap.to_broadcast([128, 4, 2, 16]), ALU.mult, c)
                k.rel = [c2]
                return vtt(dst, dst, tm.ap, ALU.add, c1, c2)

            def split(n, e32, eh, el, t32, th, ko, h, kp):
                if th is None:
                    th = vcopy(eh.ap, e32.ap, t32, eh.rel)
                tl = vtt(el.ap, e32.ap, eh.ap, ALU.subtract, th, t32, el.rel, q=V if n % 8 in share[1] else G)
                e32.rel = [tl]
                pend.append((ko, h % 2, h, kp, eh, el, th, tl))

            n, parts = 0, []
            for h in range(NH):
                if h % 2 == 0:
                    ko = bO.take()
                for kp in range(2):
                    k = bS.take()
                    for i in range(2):
                        kc = 2 * kp + i
                        tok = mm(k.ap[:, i * S:(i + 1) * S], KS[b % 2][:, h, kc * 128:(kc + 1) * 128],
                                 QS[b % 2][:, h // 2, :], True, True, s["m"], k.rel, inc=i == 1)
                    e32, eh, el = E32.take(), EH.take(), EL.take()
                    kv = k.ap.rearrange("p (i n) -> p i n", i=2)
                    t32 = act(e32.ap, kv, ACT.Exp, tok, e32.rel, t_ln, scale=0.25, bias=ebias[:, 0:1])
                    if n % 8 in share[0]:
                        th = None
                        k.rel = [t32]
                    else:
                        th = act(eh.ap, kv, ACT.Exp, tok, eh.rel, scale=0.25, bias=ebias[:, 0:1])
                        k.rel = [th]
                    parts.append((n, e32, eh, el, t32, th, ko, h, kp))
                    yield
                    if len(parts) > 1:
                        split(*parts.pop(0))
                    if len(pend) > LAG - 1:
                        av(*pend.pop(0))
                    if late:
                        norm(*late.pop())
                    n += 1
                    yield
                if h % 8 == 7:
                    qrel[b % 2, h // 8] = krel[b % 2, h // 8] = [tok]
            while parts:
                split(*parts.pop(0))
            s["tail"] = tail(b, pend, late, av, norm)

        def tail(b, pend, late, av, norm):
            s = st3[b]
            while pend:
                av(*pend.pop(0))
                yield
            VA[b % 2].rel = [T.last()]
            yield from pause(2)
            while late:
                tx_ = norm(*late.pop())
            yield from pause(GAP + 1)
            cx = CX.ap.rearrange("p a n -> p (a n)").rearrange("p (t d) -> p t d", t=4)
            ct = XTR.take()
            for c2 in range(2):
                ev = transpose4(bX, [cx[:, t, c2 * 128:(c2 + 1) * 128] for t in range(4)],
                                lambda k, tok: acopy(ct.ap[:, c2, :], k, tok, ct.rel), tx_)
                yield from pause(GAP)
            CX.rel = [T.last()]
            for t in range(4):
                k = bX.take()
                for c2 in range(2):
                    tok = mm(k.ap[:, 0:D], ct.ap[:, c2, t * 128:(t + 1) * 128], Wqkv[:, 3, c2, :], c2 == 0, c2 == 1, ev, t_wd,
                             k.rel, inc=c2 == 1)
                tx2 = vtt(X[:, 4 * b + t, :], k.ap[:, 0:D], X[:, 4 * b + t, :], ALU.add, tok, s["txb"])
                k.rel = [tx2]
                yield from pause(2)
            ct.rel = [tok]
            s["x"] = tx2

        bar = everyone()
        MZ.reset()
        QS = [MZ(128, 8, S, dt=F32R) for _ in range(2)]
        KS = [MZ(128, NH, S, dt=F32R) for _ in range(2)]
        VA = [Buf(MZ(128, 4, NH, 64, dt=F16), bar) for _ in range(2)]
        AZ = Zones(Zone(WA.start, 20 * K), Zone(SZ.start, 19 * K), MZ)
        E32 = Ring([AZ(128, 2, S) for _ in range(3)])
        EH = Ring([AZ(128, 2, S, dt=F16) for _ in range(LAG + 2)])
        EL = Ring([AZ(128, 2, S, dt=F16) for _ in range(LAG + 1)])
        QHL = Ring([AZ(128, 2, S, dt=F32R) for _ in range(1)])
        XN_, CX = Buf(AZ(128, 4, D), bar), Buf(AZ(128, 4, D), bar)
        XTR = Ring([AZ(128, 2, S) for _ in range(1)])
        MT_ = Buf(AZ(128, S, dt=F32R), bar)
        MXB = [AZ(128, 4, NH) for _ in range(2)]
        RC, RD = Ring([AZ(128, 4, 2, 1) for _ in range(2)]), Ring([AZ(128, 4, 2, 16) for _ in range(2)])
        ebias = AZ(128, 1)
        OS = Ring([at(Win_off, [128, S]), at(Wout_off, [128, S])])
        held((E32, EH, EL, XTR, QHL, OS, RC, RD), bar)
        krel, qrel = {}, {}
        tz = V(lambda e: e.memset(MT_.ap[32:33, :].bitcast(F32), 0.0), bar)
        t1row = V(lambda e: e.memset(MT_.ap[64:65, :].bitcast(F32), 1.0), bar)
        t_ln = V(lambda e: e.memset(ebias[:, :], LNES), bar)
        for i in range(2):
            qrel[i, 0] = qrel[i, 1] = [G(lambda e, i=i: e.memset(QS[i][:, :, :].bitcast(F32), 0.0), bar)]
            t0 = (V if i == 0 else G)(lambda e, i=i: e.memset(KS[i][:, :, :].bitcast(F32), 0.0), bar)
            for j in range(2):
                t0_ = dma(Y, f"one{i}", KS[i][64 * j + 48:64 * j + 49, :, :].bitcast(F32).rearrange(
                    "o (p j) n -> o p j n", j=2)[:, :, j, :],
                    MT_.ap[64:65, :].bitcast(F32).unsqueeze(1).to_broadcast([1, 8, S]), t0, t1row)
            krel[i, 0] = krel[i, 1] = [t0_]
        bX, bO, bM, bS = banks([0]), banks([1]), banks([2, 3]), pairs([2, 3])
        held((bX, bM, bS, bO), bar)
        st3 = {b: {} for b in range(NB)}
        nothing = lambda: iter(())

        def load_half(b, half):
            load_qk(b, "q", half)
            load_qk(b, "k", half)

        for b in range(2):
            for half in range(2):
                load_qk(b, "k", half)
            weave(load_v(b))
        weave(qprep(0, bar))
        for half in range(2):
            load_qk(0, "q", half)
        weave(chain(*[qprep(b, bar) for b in range(1, NB)]), maxima(0))
        load_qk(1, "q", 0)
        for b in range(NB):
            if b == 0:
                load_qk(1, "q", 1)
            elif b + 1 < NB:
                load_half(b + 1, 1)
            beside(attend(b, ((0, 4), (2,)) if b + 1 < NB else ((0, 2, 4, 6), (1, 5))),
                   (chain(st3[b - 1]["tail"] if b else nothing(), load_v(b + 1) if 1 <= b < NB - 1 else nothing()), 1.0),
                   (maxima(b + 1, b + 2 if b + 2 < NB else None) if b + 1 < NB else nothing(), RATE))
        weave(st3[NB - 1]["tail"])
        if stop == 3:
            finish()
            emit()
            return

        bar = everyone()
        MZ.reset()
        buf1 = nc.dram_tensor("buf1", (N1 * TOK, 2 * D), F16, kind="Internal").ap()
        obuf1 = nc.dram_tensor("obuf1", (N1 * TOK, D), F32, kind="Internal").ap()
        W1 = Weights(MZ, E * 2 * H1, E * 2 * H1)
        HL = MZ(128, NT, 2 * D, dt=F16)
        XN = [Buf(MZ(128, 4, D), bar) for _ in range(2)]
        XT_ = [Buf(MZ(128, 2, S), bar) for _ in range(2)]
        rz = Zone(MZ.at, MZ.end - MZ.at)
        SRZ = Zone(WA.start, 20 * K)
        SR = Ring([SRZ(128, CH) for _ in range(4)])
        LNZ = Zone(SZ.start, 19 * K)
        b2m1 = LNZ(128, E * D)
        b1m1 = LNZ(128, 32)
        wgT, xrT, wgt = LNZ(16, E), [Buf(rz(16, S), bar) for _ in range(2)], LNZ(E, 64)
        lgz1, top1, idxu1, idxf1, exz, scr = rz(128, NT, E), rz(128, NT, 8), rz(128, NT, 8), rz(128, 1, NT), rz(128, NT, E), LNZ(128, NT)
        dma(Y, "we", b2m1[:, :], a["L1_ffn_b2"].rearrange("e d -> (e d)").partition_broadcast(128), bar)
        dma(Y, "we", b1m1[:, :], a["b1m1"], bar)
        dma(Y, "we", wred[:, :, :], a["wred"], bar)
        t_we = dma(Y, "we", wg8[:, :], a["L1_ffn_wg"], bar)
        tzero1 = zero_rows(buf1, N1, rz, bar)
        bT, bS, bY = banks([0, 1]), banks([2, 3, 4]), banks([5, 6, 7])
        held((bT, bS, bY), bar)
        c = V(lambda e: e.tensor_tensor(wgt[:, 0:16], wg8[:, :], wg8[:, :], ALU.mult), t_we, bar)
        c = V(lambda e: e.tensor_reduce(wgt[:, 16:17], wgt[:, 0:16], AX.X, ALU.add), c)
        y, c = rsqrt(wgt[:, 16:17], 1, wgt[:, 20:24], c, parts=E)
        c = vtt(wgt[:, 17:18], wgt[:, 16:17], y, ALU.mult, c)
        c = vts(wgt[:, 17:18], wgt[:, 17:18], 1e-4, None, ALU.max, ALU.bypass, c)
        c = V(lambda e: e.reciprocal(wgt[:, 18:19], wgt[:, 17:18]), c)
        c = vts(wgt[:, 32:48], wg8[:, :], wgt[:, 18:19], None, ALU.mult, ALU.bypass, c)
        k = bY.take()
        tok = tr(k.ap[0:16, 0:E], wgt[:, 32:48], ident[0:E, 0:E], c, k.rel, inc=True)
        t_wg = vcopy(wgT[:, :], k.ap[0:16, 0:E], tok)
        k.rel = [t_wg]

        def gate(b):
            xn, xt, xr = XN[b % 2], XT_[b % 2], xrT[b % 2]
            sc, tk = ln_stats([X[:, 4 * b + t, :] for t in range(4)], LNZ, bar)
            for t in range(4):
                c = vts(xn.ap[:, t, :], X[:, 4 * b + t, :], *sc[t], ALU.subtract, ALU.mult, tk, xn.rel)
            yield
            hs = HL[:, 4 * b:4 * b + 4, :]
            tc_ = acopy(hs[:, :, 0:D], xn.ap, c)
            tl = vtt(hs[:, :, D:2 * D], xn.ap, hs[:, :, 0:D], ALU.subtract, tc_)
            for c2 in range(2):
                ev = transpose4(bT, [xn.ap[:, t, c2 * 128:(c2 + 1) * 128] for t in range(4)],
                                lambda k, tok: acopy(xt.ap[:, c2, :], k, tok, xt.rel), c)
            xn.rel = [T.last(), tl]
            yield
            k = bY.take()
            for c2 in range(2):
                tok = mm(k.ap[0:16, :], wred[:, c2, :], xt.ap[:, c2, :], c2 == 0, c2 == 1, ev, t_we, k.rel, inc=c2 == 1)
            xt.rel = [tok]
            ex = acopy(xr.ap, k.ap[0:16, :], tok, xr.rel)
            k.rel = [ex]
            k = bY.take()
            for t in range(4):
                tok = mm(k.ap[:, t * E:(t + 1) * E], xr.ap[:, t * 128:(t + 1) * 128], wgT[:, :], True, True, ex, t_wg, k.rel, inc=t == 3)
            xr.rel = [tok]
            c = vcopy(lgz1[:, 4 * b:4 * b + 4, :], k.ap[:, 0:4 * E].rearrange("p (t e) -> p t e", e=E), tok)
            k.rel = [c]
            for t in range(4):
                tt = 4 * b + t
                cm = V(lambda e, tt=tt: e.max(top1[:, tt, :], lgz1[:, tt, :]), c)
            for t in range(4):
                tt = 4 * b + t
                ci = V(lambda e, tt=tt: e.max_index(idxu1[:, tt, :].bitcast(U32), top1[:, tt, :], lgz1[:, tt, :]), cm)
            st[b]["i"], st[b]["hl"] = ci, tl
            yield

        weave(chain(*[gate(b) for b in range(NB)]),
              chain(keep(split_weights(a["w1m1"], W1.w1h, W1.w1l, E * 2 * H1, SR, "wn", bar), W1.t1),
                    keep(split_weights(a["w2m1"], W1.w2h, W1.w2l, E * 2 * H1, SR, "wn", bar), W1.t2)))
        cis, hls = [st[b]["i"] for b in range(NB)], [st[b]["hl"] for b in range(NB)]
        c = vcopy(idxf1[:, :, :], idxu1[:, :, 0:1].bitcast(U32).rearrange("p t s -> p s t"), cis)
        c1 = vtt(exz[:, :, :], lgz1[:, :, :], top1[:, :, 0:1].to_broadcast([128, NT, E]), ALU.subtract, cis)
        c1 = act(exz[:, :, :], exz[:, :, :], ACT.Exp, c1)
        c1 = V(lambda e: e.tensor_reduce(scr[:, :], exz[:, :, :], AX.X, ALU.add), c1)
        tsc1 = V(lambda e: e.reciprocal(scr[:, :], scr[:, :]), c1)
        rr = list(routing(1, idxf1, N1, rz, c, t_wb))
        rr[10], rr[12] = [LNZ(1, N1) for _ in range(3)], LNZ(128, 1, NT)
        pi1, tei1, te1, tpos = positions(1, rr, 4)
        tsc = scatter(buf1, HL, pi1, 1, "sc1", tpos, hls, tzero1)
        ez = Zones(Zone(MZ.start + 64 * K, 64 * K))
        tout = experts(ez, buf1, obuf1, N1, 4, W1, ACT.Gelu, b1m1, b2m1, tei1, "e1", tsc, te1, tpos, tsc1, t_we, W1.t1, W1.t2)
        GB = Ring([SRZ0(128, D) for SRZ0 in [Zone(WA.start, 20 * K)] for _ in range(8)])
        ov = out.rearrange("b (t p) d -> p (b t) d", p=128)
        for t in range(NT):
            g = GB.take()
            tg = gather(obuf1, pi1, 0, t, g.ap, f"g1{GB.at % 8}", tout, g.rel)
            c = vstt(X[:, t, :], g.ap, scr[:, t:t + 1], X[:, t, :], ALU.mult, ALU.add, tg, tsc1)
            g.rel = [c]
            if t % 4 == 3:
                to = dma(Y, "out", ov[:, t - 3:t + 1, :], X[:, t - 3:t + 1, :], c)
        Y(lambda e: e.wait_ge(*to), inc=False)
        emit()


def layouts(v):
    f = np.float32
    c = np.ascontiguousarray

    def kmaj(w, k):
        return c(w.reshape(k, 128, w.shape[-1]).transpose(1, 0, 2))

    def heads(w):
        return w.reshape(-1, 4, 2, 2, 16).transpose(0, 2, 3, 4, 1).reshape(w.shape)

    d = {}
    for n in ("x", "ctx_1024", "L0_xattn_ln_g", "L0_xattn_ln_b", "L0_xattn_b_diff", "L0_xattn_b2", "L0_ffn_b_out",
              "L1_xattn_bo", "L1_xattn_bv", "L0_ffn_b_in", "L0_ffn_b_gate"):
        d[n] = c(v[n])
    d["ident"] = np.eye(128, dtype=f)
    d["U"] = np.triu(np.ones((128, 128), f), 1)
    d["io8"] = np.broadcast_to(np.arange(8, dtype=f), (128, 8)).copy()
    d["ioj"] = np.broadcast_to(np.arange(32, dtype=f), (128, 32)).copy()
    d["WdT"] = kmaj(v["L0_xattn_W_diff"].T, 2)
    d["W1T"] = kmaj(v["L0_xattn_W1"].T, 2)
    d["W2T"] = kmaj(v["L0_xattn_W2"].T, 8)
    pp = np.zeros((128, 16), f)
    pp[:, 0:2] = v["L0_xattn_ln_g"].reshape(2, 128).T
    pp[:, 2:4] = v["L0_xattn_ln_b"].reshape(2, 128).T
    pp[:, 4:12] = v["L0_xattn_b1"].reshape(8, 128).T
    pp[:, 12:14] = heads(v["L1_xattn_bq"]).reshape(2, 128).T
    pp[:, 14:16] = heads(v["L1_xattn_bk"]).reshape(2, 128).T
    d["pp"] = pp
    d["Win"] = kmaj(v["L0_ffn_W_in"], 2)
    d["Wg"] = kmaj(v["L0_ffn_W_gate"], 2)
    d["Wout"] = kmaj(v["L0_ffn_W_out"], 2)
    d["L0_ffn_b2"] = c(v["L0_ffn_b2"])
    d["w1m0"] = c(v["L0_ffn_W1"].reshape(8, 2, 128, H0).transpose(2, 0, 1, 3).reshape(128, -1))
    d["w2m0"] = c(v["L0_ffn_W2"].reshape(8, 8, 128, D).transpose(2, 0, 1, 3).reshape(128, -1))
    d["ctxT"] = c(v["ctx_1024"].reshape(NB, S, 2, 128).transpose(0, 3, 2, 1))
    d["Wqkv"] = c(np.stack([kmaj(w, 2) for w in (heads(v["L1_xattn_Wq"]), heads(v["L1_xattn_Wk"]), v["L1_xattn_Wv"],
                                                  v["L1_xattn_Wo"])], 1))
    d["wred"] = kmaj(v["L1_ffn_w_red"], 2)
    d["L1_ffn_wg"], d["L1_ffn_b2"] = c(v["L1_ffn_wg"]), c(v["L1_ffn_b2"])
    d["w1m1"] = c(v["L1_ffn_W1"].reshape(8, 2, 128, H1).transpose(2, 0, 1, 3).reshape(128, -1))
    d["w2m1"] = c(v["L1_ffn_W2"].reshape(8, 4, 128, D).transpose(2, 0, 1, 3).reshape(128, -1))
    d["b1m1"] = c(v["L1_ffn_b1"].reshape(32, 128).T)
    d["b1m0"] = c(v["L0_ffn_b1"].reshape(64, 128).T)
    return d


def kernel(**inputs):
    import concourse.bacc as bacc
    from concourse.bass_utils import run_bass_kernel_spmd

    arrays = layouts({n: np.asarray(x) for n, x in inputs.items()})
    nc = bacc.Bacc("TRN2", target_bir_lowering=False, num_devices=1)
    aps = {n: nc.dram_tensor("in_" + n, x.shape, mybir.dt.from_np(x.dtype), kind="ExternalInput").ap()
           for n, x in arrays.items()}
    out = nc.dram_tensor("out_0", (NB, S, D), F32, kind="ExternalOutput").ap()
    build(nc, aps, out)
    r = run_bass_kernel_spmd(nc, [{"in_" + n: x for n, x in arrays.items()}], core_ids=[0])
    return r.results[0]["out_0"]
```

```python
import numpy as np
import concourse.bass as bass
from concourse import mybir
from contextlib import ExitStack
from itertools import islice

F32 = mybir.dt.float32
F32R = mybir.dt.float32r
F16 = mybir.dt.float16
I32 = mybir.dt.int32
U32 = mybir.dt.uint32
ALU = mybir.AluOpType
ACT = mybir.ActivationFunctionType
AX = mybir.AxisListType

NB, TB, P, D = 4, 4, 128, 256
NT = NB * TB
S = 512
E = 8
TOK = 256
SUB = TOK // P
N0 = (2 * NT * P + E * (TOK - 1)) // TOK
N1 = (NT * P + E * (TOK - 1)) // TOK
H0, H1 = 1024, 512
NH, HD = 16, 16
WS = 64.0
VS = 64.0
LNES = float(np.log(1024.0))


class Queue:

    def __init__(self, sem):
        self.sem, self.n, self.items = sem, 0, []

    def __call__(self, fn, *waits, inc=True):
        self.items.append((fn, flat(waits), inc))
        if inc:
            self.n += 1
            return (self.sem, self.n)
        return None

    def last(self):
        return (self.sem, self.n)

    def play(self, eng):
        seen = {}
        for fn, waits, inc in self.items:
            for sem, value in waits:
                if value > seen.get(sem.name, 0):
                    eng.wait_ge(sem, value)
                    seen[sem.name] = value
            made = fn(eng)
            if inc:
                made.then_inc(self.sem, 1)


def flat(waits):
    out = []
    for w in waits:
        if w is None:
            continue
        if isinstance(w, list):
            out += flat(w)
        else:
            out.append(w)
    return out


class Buf:

    def __init__(self, ap, rel=None):
        self.ap, self.rel = ap[(slice(None),) * len(ap.shape)], rel or []


class Ring:
    def __init__(self, aps):
        self.bufs, self.at = [Buf(a) for a in aps], 0

    def take(self):
        b = self.bufs[self.at % len(self.bufs)]
        self.at += 1
        return b


def build(nc, a, out, stop=4):
    ctx = ExitStack()
    with ctx:
        base = [nc.sbuf_base + (-nc.sbuf_base) % 64]
        names = [0]

        def at(off, shape, dt=F32):
            names[0] += 1
            return nc.alloc_sbuf_tensor_at(f"t{names[0]}", shape, dt, offset=off)

        def size(shape, dt):
            n = 2 if dt == F16 else 4
            for s in shape[1:]:
                n *= s
            return n + (-n) % 32

        class Zone:
            def __init__(self, start, length):
                self.start, self.end, self.at = start, start + length, start

            def __call__(self, *shape, dt=F32):
                t = at(self.at, list(shape), dt)
                self.at += size(shape, dt)
                assert self.at <= self.end, (shape, self.at - self.end)
                return t

            def reset(self):
                self.at = self.start

        class Zones:

            def __init__(self, *zones):
                self.zones = zones

            def __call__(self, *shape, dt=F32):
                n = size(shape, dt)
                for z in self.zones:
                    if z.at + n <= z.end:
                        return z(*shape, dt=dt)
                raise AssertionError(("no room", shape, [z.end - z.at for z in self.zones]))

        def sem(name):
            return ctx.enter_context(nc.semaphore(name))

        K = 1024
        b0 = base[0]
        PZ = Zone(b0, 40 * K)
        WA = Zone(PZ.end, 20 * K)
        SZ = Zone(WA.end, 19 * K)
        MZ = Zone(SZ.end, 128 * K)
        assert MZ.end <= nc.sbuf_usable_end, (MZ.end, nc.sbuf_usable_end)

        T = Queue(sem("s_pe"))
        V = Queue(sem("s_dve"))
        A = Queue(sem("s_act"))
        G = Queue(sem("s_pool"))
        Y = Queue(None)
        chans = {}

        def dma(q, name, o, i, *waits):
            if name not in chans:
                chans[name] = [sem("d_" + name), 0]
            c = chans[name]
            c[1] += 16
            s, v = c[0], c[1]
            q(lambda e: e.dma_start(o, i).then_inc(s, 16), *waits, inc=False)
            return (s, v)

        def everyone():
            return [T.last(), V.last(), A.last(), G.last()] + [(c[0], c[1]) for c in chans.values()]

        PB = [ctx.enter_context(nc.psum_tensor(f"pb{i}", [128, 1024], F32)) for i in range(4)]

        def banks(ids):
            return Ring([PB[i // 2][:, i % 2 * 512:i % 2 * 512 + 512] for i in ids])

        def pairs(ids):
            return Ring([PB[i][:, :] for i in ids])

        def held(rings, toks):
            for r in rings:
                for b in r.bufs:
                    b.rel = toks

        X = PZ(128, NT, D)
        ident = PZ(128, 128)
        identh = PZ(128, 128, dt=F16)
        bc_off = PZ.at
        bc = PZ(128, 7, D)
        bgate = PZ(128, E)
        Win_off = PZ.at
        Win = PZ(128, 2, D)
        bin_off = PZ.at
        bin_ = PZ(128, D)
        Wg = PZ(128, 2, E)
        Wout_off = PZ.at
        Wout = PZ(128, 2, D)
        Wqkv = PZ(128, 4, 2, D)
        wred = PZ(128, 2, 16)
        wg8 = PZ(8, 16)
        pp = PZ(128, 16)
        b1m = PZ(128, 64)
        U = PZ(128, 128)
        ones = PZ(128, 128)
        io8 = PZ(128, E)
        ioj = PZ(128, 32)
        W1x = [WA(128, 2 * H0, dt=F16) for _ in range(2)]
        W2x = [WA(128, 8 * D, dt=F16) for _ in range(2)]
        WdT = WA(128, 2, D)
        lng, lnb, bdiff, b2a, bout, bo, bv = (bc[:, i, :] for i in range(7))

        ld = {}
        ld["ident"] = dma(Y, "ident", ident[:, :], a["ident"])
        xv = a["x"].rearrange("b (t p) d -> b p t d", p=128)
        cv = a["ctx_1024"].rearrange("b (t p) d -> b p t d", p=128)
        tx = {}

        def load_x(b):
            tx[b] = dma(Y, f"x{b}", X[:, 4 * b:4 * b + 4, :], xv[b])

        def bcast(n):
            return a[n].partition_broadcast(128)

        def loads_p():
            dma(Y, "wp", pp[:, :], a["pp"])
            for i, n in enumerate(["L0_xattn_ln_g", "L0_xattn_ln_b", "L0_xattn_b_diff", "L0_xattn_b2", "L0_ffn_b_out",
                                   "L1_xattn_bo", "L1_xattn_bv"]):
                t = dma(Y, "wp", bc[:, i, :], bcast(n))
            return t

        def loads_a():
            return dma(Y, "wa", WdT[:, :, :], a["WdT"])

        def loads_b():
            dma(Y, "wb", Win[:, :, :], a["Win"])
            dma(Y, "wb", bin_[:, :], bcast("L0_ffn_b_in"))
            dma(Y, "wb", Wg[:, :, :], a["Wg"])
            dma(Y, "wb", bgate[:, :], bcast("L0_ffn_b_gate"))
            dma(Y, "wb", U[:, :], a["U"])
            dma(Y, "wb", io8[:, :], a["io8"])
            dma(Y, "wb", ioj[:, :], a["ioj"])
            dma(Y, "wb", Wout[:, :, :], a["Wout"])
            return dma(Y, "wb", b1m[:, :], a["b1m0"])

        t_oneset = V(lambda e: e.memset(ones[:, :], 1.0))
        t_idh = V(lambda e: e.tensor_copy(identh[:, :], ident[:, :]), ld["ident"])

        def vts(o, i, s1, s2, o0, o1, *w):
            return V(lambda e: e.tensor_scalar(o, i, s1, s2, o0, o1), *w)

        def vtt(o, x, y, op, *w, q=None):
            return (q or V)(lambda e: e.tensor_tensor(o, x, y, op), *w)

        def vstt(o, x, s, y, o0, o1, *w):
            return V(lambda e: e.scalar_tensor_tensor(out=o, in0=x, scalar=s, in1=y, op0=o0, op1=o1), *w)

        def vcopy(o, i, *w):
            return V(lambda e: e.tensor_copy(o, i), *w)

        def act(o, i, f, *w, bias=0.0, scale=1.0, accum=None):
            if accum is None:
                return A(lambda e: e.activation(o, i, f, bias=bias, scale=scale), *w)
            return A(lambda e: e.activation(o, i, f, bias=bias, scale=scale, accum_out=accum), *w)

        def acopy(o, i, *w):
            return act(o, i, ACT.Copy, *w)

        def mm(o, l, r, st, sp, *w, inc=False, skip=False):
            return T(lambda e: e.matmul(o, l, r, start=st, stop=sp, skip_group_check=skip), *w, inc=inc)

        def tr(o, i, idn, *w, inc=False):
            return T(lambda e: e.transpose(o, i, idn), *w, inc=inc)

        smalls = []

        def rsqrt(v, n, tmp, *w, parts=128):
            y, i1, t1, hv = (tmp[0:parts, k * n:(k + 1) * n] for k in range(4))
            c = V(lambda e: e.tensor_single_scalar(i1.bitcast(I32), v.bitcast(I32), 1, ALU.logical_shift_right), *w)
            vts(hv, v, -0.5, None, ALU.mult, ALU.bypass)
            c = V(lambda e: e.tensor_scalar(y.bitcast(I32), i1.bitcast(I32), -1.0, float(0x5f3759df), ALU.mult, ALU.add), c)
            for _ in range(3):
                c = vtt(t1, y, hv, ALU.mult, c)
                c = vtt(t1, t1, y, ALU.mult, c)
                c = vstt(y, t1, 1.5, y, ALU.add, ALU.mult, c)
            return y, c

        def ln_stats(tiles, zone, *w):
            n = len(tiles)
            st, mv, ve, tmp = zone(128, n, 6), zone(128, n, 2), zone(128, n), zone(128, 4 * n)
            for i, t in enumerate(tiles):
                wi = w[0][i] if isinstance(w[0], list) and len(w[0]) == n and len(w) == 1 else list(w)
                s = V(lambda e, i=i, t=t: e.bn_stats(st[:, i, :], t), wi)
            for i in range(n):
                g = V(lambda e, i=i: e.bn_aggr(mv[:, i, :], st[:, i, :]), s)
            c = vts(ve[:, :], mv[:, :, 1], 1e-5, None, ALU.add, ALU.bypass, g)
            y, c = rsqrt(ve[:, :], n, tmp[:, :], c)
            return [(mv[:, i, 0:1], y[:, i:i + 1]) for i in range(n)], c

        def weave(*gens):
            gens = [g for g in gens if g is not None]
            while gens:
                for g in list(gens):
                    if next(g, gens) is gens:
                        gens.remove(g)

        def beside(main, *sides, drain=True):
            due = [0.0] * len(sides)
            for _ in main:
                for i, (side, rate) in enumerate(sides):
                    due[i] += rate
                    while due[i] >= 1:
                        due[i] -= 1
                        next(side, None)
            for side, _ in sides:
                weave(side if drain else None)

        def pause(n):
            for _ in range(n):
                yield

        def chain(*gens):
            for g in gens:
                yield from g

        def keep(g, box):
            box += (yield from g)

        load_x(0)
        t_wc = dma(Y, "wc", Wqkv[:, 1:3, :, :], a["Wqkv"][:, 1:3])

        PS = Zone(PZ.at, PZ.end - PZ.at)
        ww, d01, pi_keep = PS(128, 3, NT), PS(128, NT), PS(128, 2, NT)
        tei_keep = [PS(1, N0) for _ in range(3)]
        LNZ = Zones(Zone(SZ.start + 16 * K, 3 * K), PS)
        CT = [Buf(MZ(128, 4, D + 1)) for _ in range(2)]
        TQ, TC, LQ, LC = (Buf(MZ(128, 4, D)) for _ in range(4))
        DT = [Buf(MZ(128, 2, S)) for _ in range(2)]
        LT = [Buf(MZ(128, 2, S)) for _ in range(2)]
        ET = [Buf(MZ(128, 4, S)) for _ in range(2)]
        UB = Ring([MZ(128, D)[:, :] for _ in range(2)])
        UT = Ring([MZ(128, 2, 128)[:, :, :] for _ in range(2)])
        XB = [Buf(MZ(128, 4, D))]
        stage = [MZ.at, MZ.at + 8 * K, MZ.at + 12 * K, MZ.at + 16 * K]
        UZ = [Buf(MZ(128, 4, D)) for _ in range(1)] * 2
        Q = [Buf(MZ(128, 4, D)) for _ in range(3)]
        HT = [Buf(MZ(128, 2, 2, S, dt=F16)) for _ in range(2)]
        gt_at = MZ.at
        G32 = Ring([MZ(128, S)[:, :] for _ in range(2)])
        GT = Ring([MZ(128, 2, S, dt=F16) for _ in range(8)])
        FZ = Zone(MZ.at, MZ.end - MZ.at)
        bT, bS, bY = banks([0, 1]), banks([2, 3, 4]), banks([5, 6, 7])
        t_neg = [V(lambda e, c=c: e.memset(c.ap[:, :, D:D + 1], -1.0)) for c in CT]
        st = {}

        def transpose4(ring, tiles, evac, *w):
            k = ring.take()
            for i, t in enumerate(tiles):
                tok = tr(k.ap[:, i * 128:(i + 1) * 128], t, ident[:, :], k.rel, ld["ident"], *w, inc=i == len(tiles) - 1)
            tok = evac(k.ap, tok)
            k.rel = [tok]
            return tok

        def pre(b):
            ct, q = CT[b % 2], Q[b % 3]
            tc = dma(Y, f"c{b % 2}", ct.ap[:, :, 0:D], cv[b], ct.rel)
            sc, tk = ln_stats([X[:, 4 * b + t, :] for t in range(4)], LNZ, tx[b])
            for t in range(4):
                tq = vts(q.ap[:, t, :], X[:, 4 * b + t, :], *sc[t], ALU.subtract, ALU.mult, tk, q.rel)
            yield from pause(2)
            sums, r = LNZ(128, 8), LNZ(128, 24)
            for t in range(4):
                th = act(TC.ap[:, t, :], ct.ap[:, t, 0:D], ACT.Tanh, tc, TC.rel, accum=sums[:, 4 + t:5 + t])
            for t in range(4):
                th = act(TQ.ap[:, t, :], q.ap[:, t, :], ACT.Tanh, tq, TQ.rel, accum=sums[:, t:t + 1])
            yield from pause(3)
            c = vts(r[:, 0:8], sums[:, :], 0.499, 128.0 + 1e-8, ALU.mult, ALU.add, th)
            c = V(lambda e: e.reciprocal(r[:, 0:8], r[:, 0:8]), c)
            vts(r[:, 8:16], r[:, 0:8], 0.499, None, ALU.mult, ALU.bypass, c)
            c = vts(r[:, 16:24], r[:, 0:8], 0.5, None, ALU.mult, ALU.bypass, c)
            yield
            for src, dst, o in ((TQ, LQ, 0), (TC, LC, 4)):
                for t in range(4):
                    tl = act(dst.ap[:, t, :], src.ap[:, t, :], ACT.Ln, c, dst.rel,
                             scale=r[:, 8 + o + t:9 + o + t], bias=r[:, 16 + o + t:17 + o + t])
            yield from pause(3)
            for src, o in ((TQ, 0), (TC, 4)):
                for t in range(4):
                    tp = vts(src.ap[:, t, :], src.ap[:, t, :], r[:, 8 + o + t:9 + o + t], r[:, 16 + o + t:17 + o + t],
                             ALU.mult, ALU.add, tl)
            tr_ = vtt(LQ.ap[:, :, :], LQ.ap[:, :, :], LC.ap[:, :, :], ALU.subtract, tl, q=G)
            td = vtt(TQ.ap[:, :, :], TQ.ap[:, :, :], TC.ap[:, :, :], ALU.subtract, tp)
            TC.rel, LC.rel = [td], [tr_]
            yield from pause(3)
            for c in range(2):
                e1 = transpose4(bT, [TQ.ap[:, t, c * 128:(c + 1) * 128] for t in range(4)],
                                lambda k, tok, c=c: acopy(DT[b % 2].ap[:, c, :], k, tok, DT[b % 2].rel), td)
                yield
            TQ.rel = [T.last()]
            tqb = vtt(q.ap[:, :, :], q.ap[:, :, :], bdiff.unsqueeze(1).to_broadcast([128, 4, D]), ALU.add, t_wp, th, tq, q=G)
            txb = vtt(X[:, 4 * b:4 * b + 4, :], X[:, 4 * b:4 * b + 4, :], lnb.unsqueeze(1).to_broadcast([128, 4, D]),
                      ALU.add, t_wp, tq, q=G)
            for c in range(2):
                e2 = transpose4(bT, [LQ.ap[:, t, c * 128:(c + 1) * 128] for t in range(4)],
                                lambda k, tok, c=c: acopy(LT[b % 2].ap[:, c, :], k, tok, LT[b % 2].rel), tr_)
                yield
            LQ.rel = [T.last()]
            st[b] = dict(tc=tc, e=[e1, e2], tqb=tqb, txb=txb)

        def s_exp(b):
            s = st[b]
            for mc in range(4):
                k = bS.take()
                for c in range(2):
                    tok = mm(k.ap, LT[b % 2].ap[:, c, mc * 128:(mc + 1) * 128], DT[b % 2].ap[:, c, :], c == 0, c == 1,
                             s["e"], k.rel, inc=c == 1)
                te = act(ET[b % 2].ap[:, mc, :], k.ap, ACT.Exp, tok, ET[b % 2].rel, scale=-1.0 / 16)
                k.rel = [te]
                yield
            DT[b % 2].rel = LT[b % 2].rel = [tok]
            s["te"] = te

        def rest(b):
            s, ct, q = st[b], CT[b % 2], Q[b % 3]
            rinv = LNZ(128, 4)
            tf, us = [], []
            for t in range(4):
                k = bY.take()
                for mc in range(4):
                    tok = mm(k.ap[:, 0:D + 1], ET[b % 2].ap[:, mc, t * 128:(t + 1) * 128], ct.ap[:, mc, :], mc == 0, mc == 3,
                             s["te"], s["tc"], t_neg, k.rel, inc=mc == 3)
                u = UB.take()
                c = V(lambda e, k=k, t=t: e.reciprocal(rinv[:, t:t + 1], k.ap[:, D:D + 1]), tok)
                c = vstt(u.ap, k.ap[:, 0:D], rinv[:, t:t + 1], ct.ap[:, t, 0:D], ALU.mult, ALU.add, c, u.rel)
                k.rel = [c]
                us.append((u, c))
                if t % 2 == 1:
                    yield
                    for tt in (t - 1, t):
                        u, c = us[tt]
                        kt = bT.take()
                        for cc in range(2):
                            tok = tr(kt.ap[:, cc * 128:(cc + 1) * 128], u.ap[:, cc * 128:(cc + 1) * 128], ident[:, :], c,
                                     kt.rel, inc=cc == 1)
                        u.rel = [tok]
                        ut = UT.take()
                        ev = acopy(ut.ap, kt.ap[:, 0:256].rearrange("p (c n) -> p c n", c=2), tok, ut.rel)
                        kt.rel = [ev]
                        ky = bY.take()
                        for cc in range(2):
                            tok = mm(ky.ap[:, 0:D], ut.ap[:, cc, :], WdT[:, cc, :], cc == 0, cc == 1, ev, t_wa, ky.rel,
                                     inc=cc == 1)
                        ut.rel = [tok]
                        f = vtt(q.ap[:, tt, :], ky.ap[:, 0:D], q.ap[:, tt, :], ALU.add, tok, s["tqb"])
                        ky.rel = [f]
                        tf.append(f)
                        yield
            ET[b % 2].rel = [tok]
            ct.rel = [T.last(), V.last()]
            sc, tk = ln_stats([q.ap[:, t, :] for t in range(4)], LNZ, tf)
            z = UZ[b % 2]
            for t in range(4):
                tz = vts(z.ap[:, t, :], q.ap[:, t, :], *sc[t], ALU.subtract, ALU.mult, tk, z.rel)
            tfb = vtt(q.ap[:, :, :], q.ap[:, :, :], b2a.unsqueeze(1).to_broadcast([128, 4, D]), ALU.add, tz, q=G)
            yield
            for c in range(2):
                eh = transpose4(bT, [z.ap[:, t, c * 128:(c + 1) * 128] for t in range(4)],
                                lambda k, tok, c=c: vts(z.ap[:, :, c * 128:(c + 1) * 128], k.rearrange("p (t n) -> p t n", t=4),
                                                        pp[:, c:c + 1], pp[:, 2 + c:3 + c], ALU.mult, ALU.add, tok), tz)
            ht = HT[b % 2]
            zc = z.ap.rearrange("p t (c n) -> p c t n", c=2)
            hi, lo = (ht.ap[:, i, :, :].rearrange("p c (t n) -> p c t n", t=4) for i in range(2))
            for c in range(2):
                th = vcopy(hi[:, c], zc[:, c], eh, ht.rel)
            for c in range(2):
                tl = vtt(lo[:, c], zc[:, c], hi[:, c], ALU.subtract, th, eh, ht.rel, q=G)
            z.rel = [tl]
            s["eh"], s["tfb"] = [th, tl], tfb
            yield

        def mlp(b):
            s, q = st[b], Q[b % 3]
            gts = []
            for hc in range(8):
                k, g32, g = bS.take(), G32.take(), GT.take()
                seq = [(W1x[w], i, c) for w, i in ((0, 0), (1, 0), (0, 1)) for c in range(2)]
                for n, (w, i, c) in enumerate(seq):
                    off = c * H0 + hc * 128
                    tok = mm(k.ap, w[:, off:off + 128], HT[b % 2].ap[:, i, c, :], n == 0, n == 5, s["eh"], t_w1,
                             k.rel, inc=n == 5)
                tg = act(g32.ap, k.ap, ACT.Gelu, tok, g32.rel, bias=pp[:, 4 + hc:5 + hc], scale=1.0 / WS)
                k.rel = [tg]
                th = vcopy(g.ap[:, 0, :], g32.ap, tg, g.rel)
                tl = vtt(g.ap[:, 1, :], g32.ap, g.ap[:, 0, :], ALU.subtract, th, tg, g.rel, q=G)
                g32.rel = [tl]
                gts.append((g, [th, tl]))
                yield
            HT[b % 2].rel = [tok]
            to = []
            for t in range(4):
                k = bY.take()
                for hc in range(8):
                    g, tg = gts[hc]
                    for n, (i, w) in enumerate(((0, 0), (0, 1), (1, 0))):
                        tok = mm(k.ap[:, 0:D], g.ap[:, i, t * 128:(t + 1) * 128], W2x[w][:, hc * D:(hc + 1) * D],
                                 hc == 0 and n == 0, hc == 7 and n == 2, tg, t_w2, k.rel, inc=hc == 7 and n == 2)
                    if t == 3:
                        g.rel = [(T.sem, T.n + (hc < 7))]
                o = vstt(q.ap[:, t, :], k.ap[:, 0:D], 1.0 / WS, q.ap[:, t, :], ALU.mult, ALU.add, tok, s["tfb"])
                k.rel = [o]
                to.append(o)
                yield
            sc, tk = ln_stats([q.ap[:, t, :] for t in range(4)], LNZ, to)
            z = XB[0]
            for t in range(4):
                tz = vstt(z.ap[:, t, :], q.ap[:, t, :], sc[t][0], lng, ALU.subtract, ALU.mult, tk, z.rel)
            q.rel = [tz]
            s["x1"] = []
            for t in range(4):
                tx1 = vstt(X[:, 4 * b + t, :], z.ap[:, t, :], sc[t][1], X[:, 4 * b + t, :], ALU.mult, ALU.add, tz, s["txb"])
                s["x1"].append(tx1)
            z.rel = [tx1]
            yield


        kd = nc.dram_tensor("kd", (NB, 2, 128, 2, S), F32, kind="Internal").ap()
        qd = nc.dram_tensor("qd", (NB, 2, 128, 2, S), F32, kind="Internal").ap()
        md = nc.dram_tensor("md", (NB, NH, S), F32, kind="Internal").ap()
        vd = nc.dram_tensor("vd", (NB, 128, 4, NH, 64), F16, kind="Internal").ap()
        tkd, tvd = {}, {}

        def project(ring, hl, src, wi, bi, c, *w):
            k = ring.take()
            for kk in range(2):
                tok = mm(k.ap, Wqkv[:, wi, kk, c * 128:(c + 1) * 128], src[:, kk, :], kk == 0, kk == 1, *w, k.rel, t_wc if wi == 1 else t_wd,
                         inc=kk == 1)
            hi = hl.ap[:, 0, :]
            th = act(hi, k.ap, ACT.Identity, tok, hl.rel, t_wp, bias=pp[:, bi + c:bi + c + 1])
            tl = vstt(hl.ap[:, 1, :], k.ap, pp[:, bi + c:bi + c + 1], hi.bitcast(F32), ALU.add, ALU.subtract, th, hl.rel)
            k.rel = [tl]
            return th, tl

        ctts = {}

        def kv_load(b):
            ct = KVC.take()
            ctts[b] = ct, dma(Y, f"ctt{b % 2}", ct.ap, a["ctxT"][b], ct.rel)

        def kv(b):
            ct, tct = ctts[b]
            for c in range(2):
                hl = KHL.take()
                th, tl = project(bS, hl, ct.ap, 1, 14, c, tct)
                tw = dma(G, f"kw{c}", kd[b].rearrange("q p c n -> p q c n")[:, :, c, :], hl.ap.bitcast(F32), th, tl)
                tkd[b] = tkd.get(b, []) + [tw]
                hl.rel = [tw]
                yield
            for t in range(4):
                k, f = bY.take(), VF.take()
                for kk in range(2):
                    tok = mm(k.ap[:, 0:D], ct.ap[:, kk, t * 128:(t + 1) * 128], Wqkv[:, 2, kk, :], kk == 0, kk == 1,
                             tct, k.rel, t_wc, inc=kk == 1)
                c = vstt(f.ap, k.ap[:, 0:D], VS, bv64[:, :], ALU.mult, ALU.add, tok, t_bv, f.rel)
                k.rel = [c]
                fv = f.ap.rearrange("p (h d) -> p h d", d=16)
                th = acopy(VAB.ap[:, t, :, 0:16], fv, c, VAB.rel, t_va)
                tl = vtt(VAB.ap[:, t, :, 32:48], fv, VAB.ap[:, t, :, 0:16], ALU.subtract, th)
                f.rel = [tl]
                yield
            ct.rel = [tok]
            if b + 2 < NB:
                kv_load(b + 2)
            tvd[b] = dma(G, f"vw{b}", vd[b], VAB.ap, tl)
            VAB.rel = [tvd[b]]

        CH = 1024

        def split_weights(src, hi, lo, n, ring, tag, *w, late=()):
            toks, ahead, r = [], [], [slice(i * CH, (i + 1) * CH) for i in range(n // CH)]

            def fetch(i):
                s = ring.take()
                ahead.append((s, dma(Y, f"{tag}{ring.at % len(ring.bufs)}", s.ap, src[:, r[i]], s.rel, *w)))

            for i in range(min(len(ring.bufs), len(r))):
                fetch(i)
            yield
            for i in range(len(r)):
                s, td = ahead.pop(0)
                th = act(hi[:, r[i]], s.ap, ACT.Copy, td, *w, *late, scale=WS)
                yield
                tl = vstt(lo[:, r[i]], s.ap, WS, hi[:, r[i]], ALU.mult, ALU.subtract, th, td, *w, *late)
                s.rel = [tl]
                toks = [tl]
                if i + len(ring.bufs) < len(r):
                    fetch(i + len(ring.bufs))
                yield
            return toks

        gz = Zone(gt_at, 28 * K)
        KVC = Ring([gz(128, 2, S) for _ in range(2)])
        KHL = Ring([gz(128, 2, S, dt=F32R) for _ in range(2)])
        VAB = Buf(gz(128, 4, NH, 64, dt=F16))
        VF = Ring([gz(128, D) for _ in range(2)])
        bv64 = gz(128, D)
        t_wp = loads_p()
        t_bv = vts(bv64[:, :], bv, VS, None, ALU.mult, ALU.bypass, t_wp)
        t0 = V(lambda e: e.memset(VAB.ap[:, :, :, 16:64], 0.0))
        t_va = V(lambda e: e.memset(VAB.ap[:, :, :, 16:17], VS), t0)
        def finish():
            ov = out.rearrange("b (t p) d -> p (b t) d", p=128)
            t = dma(Y, "out", ov, X[:, :, :], everyone())
            Y(lambda e: e.wait_ge(*t), inc=False)

        def emit():
            block = ctx.enter_context(nc.Block())

            @block.sync
            def _(eng):
                Y.play(eng)

            @block.gpsimd
            def _(eng):
                G.play(eng)

            @block.scalar
            def _(eng):
                A.play(eng)

            @block.vector
            def _(eng):
                V.play(eng)

            @block.tensor
            def _(eng):
                T.play(eng)

        buf0 = nc.dram_tensor("buf0", (N0 * TOK, 2 * D), F16, kind="Internal").ap()
        obuf0 = nc.dram_tensor("obuf0", (N0 * TOK, D), F32, kind="Internal").ap()

        buf1 = nc.dram_tensor("buf1", (N1 * TOK, 2 * D), F16, kind="Internal").ap()
        obuf1 = nc.dram_tensor("obuf1", (N1 * TOK, D), F32, kind="Internal").ap()

        def zero_rows(buf, n):
            return dma(Y, buf.tensor.name, buf.rearrange("(j p) d -> p j d", p=128),
                       zt[:, :].unsqueeze(1).to_broadcast([128, n * SUB, 2 * D]), t_zt, T.last())

        class Weights:

            def __init__(self, zone, e1, e2):
                self.w1h, self.w1l = zone(128, e1, dt=F16), zone(128, e1, dt=F16)
                self.w2h, self.w2l = zone(128, e2, dt=F16), zone(128, e2, dt=F16)
                self.t1, self.t2 = [], []

        QR, R0, RATE0 = 3, 1.3, 1.6
        SP, MP = (1.4, 1.4), 5

        def routing(ns, idx, nt_max, zone, *w):
            O = [zone(128, NT, E) for _ in range(ns)]
            M = O[0] if ns == 1 else zone(128, NT, E)
            C = [zone(128, NT, E) for _ in range(2)]
            tot, tmp = zone(128, NT, E), zone(128, NT, E)
            sm, smi, cmp, tef = zone(128, 6, E), zone(128, E), zone(1, nt_max, E), zone(1, nt_max)
            tei = [zone(1, nt_max) for _ in range(3)]
            pf, pi = zone(128, ns, NT), zone(128, ns, NT)
            io = io8[:, :].unsqueeze(1).to_broadcast([128, NT, E])
            for s in range(ns):
                c = vtt(O[s][:, :, :], io, idx[:, s, :].unsqueeze(2).to_broadcast([128, NT, E]), ALU.is_equal, *w)
            if ns == 2:
                c = vtt(M[:, :, :], O[0][:, :, :], O[1][:, :, :], ALU.add, c)
            m2 = M[:, :, :].rearrange("p t e -> p (t e)")
            k1, k2 = bY.take(), bY.take()
            mm(k1.ap[:, 0:128], U[:, :], m2, True, True, c, k1.rel, *w)
            tp = mm(k2.ap[:, 0:128], ones[:, :], m2, True, True, k2.rel, t_oneset, inc=True)
            c = vcopy(tot[:, :, :], k2.ap[:, 0:128].rearrange("p (t e) -> p t e", e=E), tp)
            k2.rel = [c]
            cur = tot
            for i, sh in enumerate((1, 2, 4, 8)):
                nx = C[i % 2]
                vcopy(nx[:, 0:sh, :], cur[:, 0:sh, :], c)
                c = vtt(nx[:, sh:, :], cur[:, sh:, :], cur[:, 0:NT - sh, :], ALU.add, c)
                cur = nx
            V(lambda e: e.tensor_scalar(smi[:, :].bitcast(I32), cur[:, NT - 1, :], float(TOK - 1), None, ALU.add, ALU.bypass), c)
            c = V.last()
            c = V(lambda e: e.tensor_single_scalar(smi[:, :].bitcast(I32), smi[:, :].bitcast(I32), 8, ALU.logical_shift_right), c)
            c = vcopy(sm[:, 0, :], smi[:, :].bitcast(I32), c)
            p = 0
            for i, sh in enumerate((1, 2, 4)):
                vcopy(sm[:, i + 1, 0:sh], sm[:, p, 0:sh], c)
                c = vtt(sm[:, i + 1, sh:], sm[:, p, sh:], sm[:, p, 0:E - sh], ALU.add, c)
                p = i + 1
            vtt(sm[:, 4, :], sm[:, 3, :], sm[:, 0, :], ALU.subtract, c)
            ce = vtt(cmp[:, :, :], sm[0:1, 3, :].unsqueeze(1).to_broadcast([1, nt_max, E]),
                     ioj[0:1, 0:nt_max].unsqueeze(2).to_broadcast([1, nt_max, E]), ALU.is_le, c)
            ce = V(lambda e: e.tensor_reduce(tef[:, :], cmp[:, :, :], AX.X, ALU.add), ce)
            return O, M, C, cur, tot, tmp, sm, k1, ce, tef, tei, pf, pi, c

        def positions(ns, r, hc):
            O, M, C, cur, tot, tmp, sm, k1, ce, tef, tei, pf, pi, c = r
            n2 = 2 * hc * 128
            vts(tei[0][:, :].bitcast(I32), tef[:, :], float(E - 1), float(n2), ALU.min, ALU.mult, ce)
            vts(tei[1][:, :].bitcast(I32), tef[:, :], float(E - 1), float(hc), ALU.min, ALU.mult, ce)
            te = vts(tei[2][:, :].bitcast(I32), tef[:, :], float(E - 1), float(D), ALU.min, ALU.mult, ce)
            c = vtt(tmp[:, :, :], cur[:, :, :], tot[:, :, :], ALU.subtract, c)
            c = vtt(tmp[:, :, :], k1.ap[:, 0:128].rearrange("p (t e) -> p t e", e=E), tmp[:, :, :], ALU.add, c)
            k1.rel = [c]
            c = vstt(tmp[:, :, :], sm[:, 4, :].unsqueeze(1).to_broadcast([128, NT, E]), float(TOK), tmp[:, :, :],
                     ALU.mult, ALU.add, c)
            for s in range(ns):
                o = C[s % 2]
                c2 = vtt(o[:, :, :], O[s][:, :, :], tmp[:, :, :], ALU.mult, c)
                c2 = V(lambda e, s=s, o=o: e.tensor_reduce(pf[:, s, :], o[:, :, :], AX.X, ALU.add), c2)
                c2 = vcopy(pi[:, s, :].bitcast(U32), pf[:, s, :], c2)
            return pi, tei, te, c2

        def scatter(buf, rows, pi, ns, tag, *w):
            for t in range(NT):
                for s in range(ns):
                    name = tag
                    chans.setdefault(name, [sem("d_" + name) if name not in chans else chans[name][0], 0])
                    ch = chans[name]
                    ch[1] += 16
                    G(lambda e, t=t, s=s, ch=ch: e.indirect_dma_start(
                        out=buf, out_offset=bass.IndirectOffsetOnAxis(ap=pi[:, s, t:t + 1].bitcast(U32), axis=0),
                        in_=rows[:, t, :], in_offset=None).then_inc(ch[0], 16), *w, inc=False)
            return (ch[0], ch[1])

        def experts(zone, buf, obuf, n, HC, W, func, b1m, b2m, tei, tag, *w, deep=False):
            xr = Ring([zone(128, SUB, 2 * D, dt=F16) for _ in range(2)])
            xt = Ring([zone(128, 4, TOK, dt=F16) for _ in range(2)])
            m32 = Ring([zone(128, 2, TOK) for _ in range(2)])
            mh = Ring([zone(128, 2, TOK, dt=F16) for _ in range(HC // 2 + 2)])
            ml = Ring([zone(128, 2, TOK, dt=F16) for _ in range(HC // 2 + 2)])
            ob = Ring([zone(128, SUB, D) for _ in range(2)])
            bX, bU, bD = banks([0, 1]), banks([2, 3, 4]), banks([5, 6, 7])
            for r_ in (bX, bU, bD):
                for bb in r_.bufs:
                    bb.rel = flat(w)
            bv_ = buf.rearrange("(j s p) d -> j p s d", p=128, s=SUB)
            ov_ = obuf.rearrange("(j s p) d -> j p s d", p=128, s=SUB)
            regs = {}

            def reg(q, key, src, top):
                def go(e):
                    regs[key] = e.value_load(src, min_val=0, max_val=top)
                q(go, *w, inc=False)

            fetched = []

            def fetch(j):
                if j < n:
                    x = xr.take()
                    fetched.append((x, dma(Y, f"{tag}x{xr.at % 2}", x.ap, bv_[j], x.rel, *w)))

            def load(j):
                x, td = fetched.pop(0)
                k = bX.take()
                kh = k.ap.bitcast(F16).rearrange("p (c n) -> p c n", c=4)
                for s in range(SUB):
                    for c in range(4):
                        tok = tr(kh[:, c, s * 128:(s + 1) * 128], x.ap[:, s, c * 128:(c + 1) * 128], identh[:, :], td,
                                 t_idh, k.rel, inc=s == SUB - 1 and c == 3)
                x.rel = [tok]
                xx = xt.take()
                ev = vcopy(xx.ap, kh, tok, xx.rel)
                k.rel = [ev]
                return xx, ev

            def up(j, xx, ev):
                reg(T, ("t", j), tei[0][0:1, j:j + 1].bitcast(I32), (E - 1) * 2 * HC * 128)
                reg(A, ("a", j), tei[1][0:1, j:j + 1].bitcast(I32), (E - 1) * HC)
                mids = []
                for g in range(HC // 2):
                    k = bU.take()
                    for h2 in range(2):
                        hc = 2 * g + h2
                        o = k.ap[:, h2 * TOK:(h2 + 1) * TOK]
                        seq = [(W.w1h, c, c) for c in range(2)] + [(W.w1h, c, 2 + c) for c in range(2)] + \
                              [(W.w1l, c, c) for c in range(2)]
                        for i, (ww, c, xc) in enumerate(seq):
                            off = c * HC * 128 + hc * 128
                            tok = T(lambda e, o=o, ww=ww, off=off, xc=xc, i=i: e.matmul(
                                o, ww[:, bass.ds(regs["t", j] + off, 128)], xx.ap[:, xc, :], start=i == 0, stop=i == 5),
                                ev, k.rel, W.t1, inc=i == 5)
                    m = m32.take()
                    for h2 in range(2):
                        hc = 2 * g + h2
                        ta = A(lambda e, m=m, k=k, h2=h2, hc=hc: e.activation(
                            m.ap[:, h2, :], k.ap[:, h2 * TOK:(h2 + 1) * TOK], func,
                            bias=b1m[:, bass.ds(regs["a", j] + hc, 1)], scale=1.0 / WS), tok, m.rel)
                    k.rel = [ta]
                    h, l = mh.take(), ml.take()
                    th = vcopy(h.ap, m.ap, ta, h.rel)
                    tl = vtt(l.ap, m.ap, h.ap, ALU.subtract, th, l.rel)
                    m.rel = [tl]
                    mids.append((h, l, tl))
                xx.rel = [tok]
                return mids

            def down(j, mids):
                reg(V, ("v", j), tei[2][0:1, j:j + 1].bitcast(I32), (E - 1) * D)
                o2 = ob.take()
                for s in range(SUB):
                    k = bD.take()
                    i, last = 0, HC * 3 - 1
                    for hc in range(HC):
                        h, l, tl = mids[hc // 2]
                        for src, ww in ((h, W.w2h), (l, W.w2h), (h, W.w2l)):
                            tok = T(lambda e, k=k, src=src, hc=hc, s=s, ww=ww, i=i: e.matmul(
                                k.ap[:, 0:D], src.ap[:, hc % 2, s * 128:(s + 1) * 128],
                                ww[:, bass.ds(regs["t", j] + hc * D, D)], start=i == 0, stop=i == last),
                                tl, k.rel, W.t2, inc=i == last)
                            i += 1
                    tv = V(lambda e, k=k, s=s: e.scalar_tensor_tensor(
                        out=o2.ap[:, s, :], in0=k.ap[:, 0:D], scalar=1.0 / WS,
                        in1=b2m[:, bass.ds(regs["v", j], D)], op0=ALU.mult, op1=ALU.add), tok, o2.rel)
                    k.rel = [tv]
                for h, l, tl in mids:
                    h.rel = l.rel = [tok]
                o2.rel = [dma(Y, f"{tag}o{ob.at % 2}", ov_[j], o2.ap, tv)]
                return o2.rel

            tout, mids = [], None
            fetch(0)
            fetch(1)
            nxt = load(0)
            for j in range(n):
                fetch(j + 2)
                cur = up(j, *nxt)
                if j + 1 < n:
                    nxt = load(j + 1)
                if deep and mids is not None:
                    tout = tout[-1:] + down(j - 1, mids)
                mids = cur
                if not deep:
                    tout = tout[-1:] + down(j, mids)
            if deep:
                tout = tout[-1:] + down(n - 1, mids)
            return tout

        def gather(obuf, pi, s, t, dst, name, *w):
            chans.setdefault(name, [sem("d_" + name) if name not in chans else chans[name][0], 0])
            ch = chans[name]
            ch[1] += 16
            G(lambda e: e.indirect_dma_start(
                out=dst, out_offset=None, in_=obuf,
                in_offset=bass.IndirectOffsetOnAxis(ap=pi[:, s, t:t + 1].bitcast(U32), axis=0)).then_inc(ch[0], 16),
                *w, inc=False)
            return (ch[0], ch[1])

        W0 = Weights(Zone(MZ.start, 128 * K), E * 2 * H0, E * 2 * H0)
        HL = at(SZ.start, [128, NT, 2 * D], F16)
        rz = Zone(FZ.at, 8 * K)
        XN = HF = Buf(FZ(128, 4, D))
        XT_ = HT_ = Buf(FZ(128, 4, D))
        SR = Ring([FZ(128, CH) for _ in range(2)] + [at(o, [128, CH]) for o in stage])
        zt = FZ(128, 2 * D, dt=F16)
        lgz, top, idxu = FZ(128, NT, E), FZ(128, NT, 8), FZ(128, NT, 8)
        b2m0 = at(WA.start, [128, E * D])
        SRW = Ring([at(WA.start + 8 * K + 4 * K * i, [128, CH]) for i in range(3)])

        def moe_pre(b):
            sc, tk = ln_stats([X[:, 4 * b + t, :] for t in range(4)], FZ, st[b]["x1"])
            for t in range(4):
                c = vts(XN.ap[:, t, :], X[:, 4 * b + t, :], *sc[t], ALU.subtract, ALU.mult, tk, XN.rel)
            yield from pause(MP)
            xt4 = XT_.ap[:, :, :].rearrange("p a n -> p (a n)").rearrange("p (c n) -> p c n", c=2)
            for c2 in range(2):
                ev = transpose4(bT, [XN.ap[:, t, c2 * 128:(c2 + 1) * 128] for t in range(4)],
                                lambda k, tok: acopy(xt4[:, c2, :], k, tok, XT_.rel), c)
            XN.rel = [T.last()]
            yield from pause(2)
            for t in range(4):
                k = bY.take()
                for c2 in range(2):
                    tok = mm(k.ap[:, 0:D], xt4[:, c2, t * 128:(t + 1) * 128], Win[:, c2, :], c2 == 0, c2 == 1, ev, t_wb,
                             k.rel, inc=c2 == 1)
                th = vtt(HF.ap[:, t, :], k.ap[:, 0:D], bin_[:, :], ALU.add, tok, HF.rel, t_wb)
                k.rel = [th]
                if t % 2:
                    yield
            XT_.rel = [tok]
            hs = HL[:, 4 * b:4 * b + 4, :]
            tc_ = acopy(hs[:, :, 0:D], HF.ap[:, :, :], th)
            ht4 = HT_.ap[:, :, :].rearrange("p a n -> p (a n)").rearrange("p (c n) -> p c n", c=2)
            for c2 in range(2):
                ev = transpose4(bT, [HF.ap[:, t, c2 * 128:(c2 + 1) * 128] for t in range(4)],
                                lambda k, tok: acopy(ht4[:, c2, :], k, tok, HT_.rel), th)
            tl = vtt(hs[:, :, D:2 * D], HF.ap[:, :, :], hs[:, :, 0:D], ALU.subtract, tc_, q=G)
            HF.rel = [T.last(), tl]
            yield from pause(2)
            k = bY.take()
            for t in range(4):
                for c2 in range(2):
                    tok = mm(k.ap[:, t * E:(t + 1) * E], ht4[:, c2, t * 128:(t + 1) * 128], Wg[:, c2, :], c2 == 0, c2 == 1,
                             ev, t_wb, k.rel, inc=c2 == 1)
            HT_.rel = [tok]
            lg = lgz[:, 4 * b:4 * b + 4, :]
            c = vtt(lg, k.ap[:, 0:4 * E].rearrange("p (t e) -> p t e", e=E), bgate[:, :].unsqueeze(1).to_broadcast([128, 4, E]),
                    ALU.add, tok)
            k.rel = [c]
            for t in range(4):
                tt = 4 * b + t
                cm = V(lambda e, tt=tt: e.max(top[:, tt, :], lgz[:, tt, :]), c)
            for t in range(4):
                tt = 4 * b + t
                ci = V(lambda e, tt=tt: e.max_index(idxu[:, tt, :].bitcast(U32), top[:, tt, :], lgz[:, tt, :]), cm)
            st[b]["i"], st[b]["hl"] = ci, tl
            yield

        kvs = chain(*[kv(b) for b in range(NB)])
        def head(b):
            yield from pre(b)
            yield from s_exp(b)

        t_w1, t_w2 = [], []
        SR0 = Ring([at(gz.at + 4 * K * i, [128, CH]) for i in range(3)])
        assert gz.at + 12 * K <= MZ.end
        sp0 = chain(keep(split_weights(a["W1T"].rearrange("p c n -> p (c n)"), *W1x, 2 * H0, SR0, "wa1"), t_w1),
                    keep(split_weights(a["W2T"].rearrange("p c n -> p (c n)"), *W2x, 8 * D, SR0, "wa2"), t_w2))
        h0 = head(0)
        kv_load(0)
        next(h0)
        kv_load(1)
        load_x(1)
        t_wa = loads_a()
        load_x(2)
        load_x(3)
        t_wd = dma(Y, "wd", Wqkv[:, ::3, :, :], a["Wqkv"][:, ::3])
        next(sp0)
        t_wb = loads_b()
        beside(h0, (kvs, 1.0), drain=False)
        for b in range(NB):
            weave(head(b + 1) if b + 1 < NB else None, rest(b), mlp(b - 1) if b else kvs, None if b else sp0, moe_pre(b - 2) if b >= 2 else None)
            if b == 0:
                done = [*tkd[NB - 1], tvd[NB - 1], T.last(), V.last(), A.last()]
                held((GT, G32), done)
                XN.rel = XT_.rel = done
            if b == 2:
                t_zt = V(lambda e: e.memset(zt[:, :], 0.0), t_w2)
                tzero0 = zero_rows(buf0, N0)
                tzero1 = zero_rows(buf1, N1)
        free = [T.last(), V.last(), A.last(), G.last()]
        held((SR,), free)
        sp1 = keep(split_weights(a["w1m0"], W0.w1h, W0.w1l, E * 2 * H0, SR, "wm", free), W0.t1)
        beside(mlp(NB - 1), (moe_pre(NB - 2), 1.0), (sp1, SP[0]), drain=False)
        if stop == 1:
            finish()
            emit()
            return

        free = [T.last(), V.last(), A.last(), G.last()]
        tb2 = dma(Y, "b2m0", b2m0[:, :], a["L0_ffn_b2"].rearrange("e d -> (e d)").partition_broadcast(128), free)
        sp2w = list(free)
        sp2 = keep(split_weights(a["w2m0"], W0.w2h, W0.w2l, E * 2 * H0, SRW, "wp", free, late=sp2w), W0.t2)
        beside(moe_pre(NB - 1), (sp1, SP[1]), drain=False)
        cis, hls = [st[b]["i"] for b in range(NB)], [st[b]["hl"] for b in range(NB)]
        idxf = rz(128, 2, NT)
        c = vcopy(idxf[:, :, :], idxu[:, :, 0:2].bitcast(U32).rearrange("p t s -> p s t"), cis, hls)
        c1 = vtt(d01[:, :], top[:, :, 1], top[:, :, 0], ALU.subtract, cis)
        c1 = act(d01[:, :], d01[:, :], ACT.Exp, c1)
        c1 = vts(ww[:, 2, :], d01[:, :], 1.0, None, ALU.add, ALU.bypass, c1)
        c1 = V(lambda e: e.reciprocal(ww[:, 0, :], ww[:, 2, :]), c1)
        tw = vtt(ww[:, 1, :], d01[:, :], ww[:, 0, :], ALU.mult, c1)
        r = routing(2, idxf, N0, rz, c, t_wb)
        rr = list(r)
        rr[10], rr[12] = tei_keep, pi_keep
        pi0, tei0, te0, tpos = positions(2, rr, 8)
        tsc = scatter(buf0, HL, pi0, 2, "sc0", tpos, hls, tzero0)
        txo = [vtt(X[:, 4 * b:4 * b + 4, :], X[:, 4 * b:4 * b + 4, :], bout.unsqueeze(1).to_broadcast([128, 4, D]),
                   ALU.add, cis, q=G) for b in range(NB)]
        weave(sp1)
        sp2w += [*W0.t1, tpos, te0, tw, tzero0, tzero1]
        weave(sp2)
        ez = Zones(Zone(SZ.start, 16 * K), Zone(WA.start + 8 * K, 12 * K), Zone(SZ.start + 16 * K, 3 * K))
        te0 = experts(ez, buf0, obuf0, N0, 8, W0, ACT.Relu, b1m, b2m0, tei0, "e0", tsc, te0, tb2, t_wb, W0.t2)

        bar = everyone()
        cz = Zones(Zone(WA.start, 18 * K), Zone(SZ.start, 16 * K))
        GB = Ring([at(MZ.start + 64 * K + 2 * K * i, [128, 2, D]) for i in range(NT)])
        MO = Ring([cz(128, 4, D) for _ in range(2)])
        MT = Ring([cz(128, 2, S) for _ in range(2)])
        bT, bY = banks([4, 5]), banks([6, 7])
        held((GB, MO, MT, bT, bY), bar)

        def combine(b):
            mo, mt = MO.take(), MT.take()
            gs = []
            for t in range(4):
                tt = 4 * b + t
                g = GB.take()
                for s in range(2):
                    tg = gather(obuf0, pi0, s, tt, g.ap[:, s, :], f"g0{GB.at}", te0, g.rel)
                gs.append((g, tg))
            yield
            for t in range(4):
                tt = 4 * b + t
                g, tg = gs[t]
                c = act(mo.ap[:, t, :], g.ap[:, 0, :], ACT.Copy, tg, tw, mo.rel, scale=ww[:, 0, tt:tt + 1])
                c = vstt(mo.ap[:, t, :], g.ap[:, 1, :], ww[:, 1, tt:tt + 1], mo.ap[:, t, :], ALU.mult, ALU.add, c)
                g.rel = [c]
                if t % 2:
                    yield
            for c2 in range(2):
                ev = transpose4(bT, [mo.ap[:, t, c2 * 128:(c2 + 1) * 128] for t in range(4)],
                                lambda k, tok: acopy(mt.ap[:, c2, :], k, tok, mt.rel), c)
            mo.rel = [T.last()]
            yield
            for t in range(4):
                k = bY.take()
                for c2 in range(2):
                    tok = mm(k.ap[:, 0:D], mt.ap[:, c2, t * 128:(t + 1) * 128], Wout[:, c2, :], c2 == 0, c2 == 1, ev, k.rel,
                             t_wb, inc=c2 == 1)
                tx2 = vtt(X[:, 4 * b + t, :], k.ap[:, 0:D], X[:, 4 * b + t, :], ALU.add, tok, txo[b])
                k.rel = [tx2]
                st[b].setdefault("x2", []).append(tx2)
                if t % 2:
                    yield
            mt.rel = [tok]

        if stop == 2:
            weave(chain(*[combine(b) for b in range(NB)]))
            finish()
            emit()
            return

        def norms(bs):
            sc, tk = ln_stats([X[:, 4 * b + t, :] for b in bs for t in range(4)], LZ, [t for b in bs for t in st[b]["x2"]])
            shift = LZ(128, len(sc))
            for i, (m, r) in enumerate(sc):
                ts = vstt(shift[:, i:i + 1], m, -1.0, r, ALU.mult, ALU.mult, tk)
            for i, b in enumerate(bs):
                st3[b]["ln"] = sc[4 * i:4 * i + 4], shift[:, 4 * i:4 * i + 4], ts

        def qprep(b):
            s = st3[b]
            sc, shift, ts = s["ln"]
            for t in range(4):
                c = act(XN_.ap[:, t, :], X[:, 4 * b + t, :], ACT.Identity, ts, XN_.rel, scale=sc[t][1], bias=shift[:, t:t + 1])
            yield from pause(GAP + 2)
            xt = XTR.take()
            for c2 in range(2):
                ev = transpose4(bX, [XN_.ap[:, t, c2 * 128:(c2 + 1) * 128] for t in range(4)],
                                lambda k, tok, c2=c2: acopy(xt.ap[:, c2, :], k, tok, xt.rel), c)
                yield from pause(GAP)
            XN_.rel = [T.last()]
            s["txb"] = vtt(X[:, 4 * b:4 * b + 4, :], X[:, 4 * b:4 * b + 4, :], bo.unsqueeze(1).to_broadcast([128, 4, D]),
                           ALU.add, c, t_wp, q=G)
            for c2 in range(2):
                hl = QHL[c2]
                if c2:
                    hl.rel = XN_.rel
                th, tl = project(bX, hl, xt.ap, 0, 12, c2, ev)
                tq = dma(Y, f"qw{c2}", qd[b].rearrange("q p c n -> p q c n")[:, :, c2, :], hl.ap.bitcast(F32), th, tl)
                s["qd"] = s.get("qd", []) + [tq]
                hl.rel = [tq]
                if c2:
                    XN_.rel = [tq]
                yield from pause(GAP)
            xt.rel = [T.last()]

        def load_qk(b, which, half=None):
            s, sl = st3[b], slice(0, 8) if half is None else slice(4 * half, 4 * half + 4)
            first, half = half is None, half or 0
            if which == "q":
                dv = QS[b % 2][:, :, :].bitcast(F32)
                src, order, tok, rel = qd[b], (0, 0, 1), s["qd"], qrel[b % 2, half]
            else:
                dv = KS[b % 2][:, :, :].bitcast(F32).rearrange("p (s j) n -> p j s n", j=2)
                src, order, tok, rel = kd[b], (0, 1, 0), tkd[b], krel[b % 2, half]
            assert len(tok) == 2
            sv = src.rearrange("q (j r b) c n -> j q r (b c) n", j=2, r=16)
            for j in range(2):
                for g in range(3):
                    r0 = 64 * j + 16 * g
                    d = dv[r0:r0 + 16, sl] if which == "q" else dv[r0:r0 + 16, j, sl]
                    t = dma(Y, f"{which}s{b % 2}{half}", d, sv[j, order[g]][:, sl], tok, rel)
            if which == "q" and not first:
                for j in range(2):
                    t = dma(Y, f"qs{b % 2}{half}", QS[b % 2][64 * j + 48:64 * j + 49, sl, :].bitcast(F32),
                            MT_.ap[32:33, :].bitcast(F32).unsqueeze(1).to_broadcast([1, 4, S]), tz, rel)
            s[which, half] = t
            if first:
                s[which, 1] = t

        def load_v(b):
            st3[b]["v"] = dma(Y, f"va{b % 2}", VA[b % 2].ap, vd[b], tvd[b], VA[b % 2].rel)
            yield

        def maxima(b, ahead=None):
            s, mx = st3[b], MXB[b % 2]
            for half in range(2):
                for t in range(4):
                    if ahead is not None and (half, t) == (1, 3):
                        load_half(ahead, 0)
                    for h in range(8 * half, 8 * half + 8):
                        k = bM.take()
                        tok = mm(k.ap, QS[b % 2][:, h // 2, t * 128:(t + 1) * 128], KS[b % 2][:, h, :],
                                 True, True, s["q", half], s["k", half], k.rel, inc=True)
                        tm = V(lambda e, t=t, h=h, k=k: e.tensor_reduce(mx[:, t, h:h + 1], k.ap, AX.X, ALU.max), tok)
                        k.rel = [tm]
                        yield
                k = bX.take()
                for t in range(4):
                    tt = tr(k.ap[0:8, t * 128:(t + 1) * 128], mx[:, t, 8 * half:8 * half + 8], ident[:, :], tm, k.rel, inc=t == 3)
                te = vts(MT_.ap[0:8, :], k.ap[0:8, :], -1.0, None, ALU.mult, ALU.bypass, tt, MT_.rel)
                k.rel = [te]
                tm = dma(Y, "md", md[b][8 * half:8 * half + 8], MT_.ap[0:8, :].bitcast(F32), te)
                MT_.rel = [tm]
                for j in range(2):
                    tq = dma(Y, f"qm{b % 2}{half}", QS[b % 2][64 * j + 48:64 * j + 49, 4 * half:4 * half + 4, :].bitcast(F32),
                             md[b].rearrange("(s j) n -> j s n", j=2)[j:j + 1, 4 * half:4 * half + 4], tm, tok)
                s["m", half] = tq
                yield

        SH, SH3 = ((0, 4), ()), ((0, 2, 4, 6), (1, 5))
        LAG, RATE, GAP = 4, 1.1, 3

        def attend(b, share):
            s, va = st3[b], VA[b % 2]
            cxv = CX.ap.rearrange("p a n -> p (a n)").rearrange("p (t h d) -> p t h d", t=4, h=NH)
            pend, late, box = [], [], {"n": 0}

            def av(j, h, kp, eh, el, th, tl):
                if kp == 0:
                    box["ko", j] = bO[j].take()
                ko = box["ko", j]
                for i in range(2):
                    kc = 2 * kp + i
                    for e_, te in ((eh, th), (el, tl)):
                        tok = mm(ko.ap, va.ap[:, kc, h, :], e_.ap[:, i, :], kc == 0 and e_ is eh,
                                 kc == 3 and e_ is el, te, s["v"], ko.rel, inc=i == 1)
                        e_.rel = [tok]
                if kp == 1:
                    if j == 0:
                        box["o"] = OS.take()
                    o = box["o"]
                    ev = (acopy if j == 0 else vcopy)(o.ap[64 * j:64 * j + 64, :], ko.ap, tok, o.rel)
                    ko.rel = [ev]
                    box["ev", j] = ev
                    if j == 1:
                        late.append((box["n"], h // 2, o, [box["ev", 0], ev]))

            def norm(at, g, o, ev):
                k, rc = box.get("ring", bX).take(), RC.take()
                for t in range(4):
                    tok = tr(k.ap[:, t * 128:(t + 1) * 128], o.ap[:, t * 128:(t + 1) * 128], ident[:, :], ev, k.rel, inc=t == 3)
                o.rel = [tok]
                kv = k.ap.rearrange("p (t j x) -> p t j x", t=4, j=2)
                c = V(lambda e: e.reciprocal(rc.ap[:, :, :, 0], kv[:, :, :, 16]), tok)
                dst = cxv[:, :, 2 * g:2 * g + 2, :]
                c1 = vtt(dst, kv[:, :, :, 0:16], rc.ap.to_broadcast([128, 4, 2, 16]), ALU.mult, c, CX.rel)
                tm = RD.take()
                c2 = vtt(tm.ap, kv[:, :, :, 32:48], rc.ap.to_broadcast([128, 4, 2, 16]), ALU.mult, c)
                k.rel = [c2]
                return vtt(dst, dst, tm.ap, ALU.add, c1, c2)

            def split(n, e32, eh, el, t32, th, h, kp):
                if th is None:
                    th = vcopy(eh.ap, e32.ap, t32, eh.rel)
                tl = vtt(el.ap, e32.ap, eh.ap, ALU.subtract, th, t32, el.rel, q=V if n % 8 in share[1] else G)
                e32.rel = [tl]
                pend.append((h % 2, h, kp, eh, el, th, tl))

            n, parts = 0, []
            for h in range(NH):
                for kp in range(2):
                    k = bS.take()
                    for i in range(2):
                        kc = 2 * kp + i
                        tok = mm(k.ap[:, i * S:(i + 1) * S], KS[b % 2][:, h, kc * 128:(kc + 1) * 128],
                                 QS[b % 2][:, h // 2, :], True, True, s["m", h // 8], k.rel, inc=i == 1)
                    e32, eh, el = E32.take(), EH.take(), EL.take()
                    kv = k.ap.rearrange("p (i n) -> p i n", i=2)
                    t32 = act(e32.ap, kv, ACT.Exp, tok, e32.rel, t_ln, scale=0.25, bias=ebias[:, 0:1])
                    if n % 8 in share[0]:
                        th = None
                        k.rel = [t32]
                    else:
                        th = act(eh.ap, kv, ACT.Exp, tok, eh.rel, scale=0.25, bias=ebias[:, 0:1])
                        k.rel = [th]
                    parts.append((n, e32, eh, el, t32, th, h, kp))
                    yield
                    if len(parts) > 1:
                        split(*parts.pop(0))
                    if len(pend) > LAG - 1:
                        av(*pend.pop(0))
                    if late and late[0][0] + 2 <= n:
                        norm(*late.pop(0))
                    n += 1
                    box["n"] = n
                    yield
                if h % 8 == 7:
                    qrel[b % 2, h // 8] = krel[b % 2, h // 8] = [tok]
            while parts:
                split(*parts.pop(0))
            ring = bX
            if b == NB - 1:
                ring = box["ring"] = banks([0, 4, 5, 6, 7])
                for i, r in enumerate(ring.bufs):
                    r.rel = [bX.bufs[0].rel, bS.bufs[0].rel, bS.bufs[1].rel][(i + 1) // 2]
            s["tail"] = tail(b, pend, late, av, norm, ring)

        def tail(b, pend, late, av, norm, ring):
            s = st3[b]
            while pend:
                av(*pend.pop(0))
                yield
            VA[b % 2].rel = [T.last()]
            yield from pause(2)
            while late:
                tx_ = norm(*late.pop(0))
            yield from pause(GAP + 1)
            cx = CX.ap.rearrange("p a n -> p (a n)").rearrange("p (t d) -> p t d", t=4)
            ct, evs = XTR.take(), []
            for c2 in range(2):
                ev = transpose4(ring, [cx[:, t, c2 * 128:(c2 + 1) * 128] for t in range(4)],
                                lambda k, tok: (vcopy if c2 and ring is not bX else acopy)(ct.ap[:, c2, :], k, tok, ct.rel), tx_)
                evs.append(ev)
                yield from pause(GAP)
            CX.rel = [T.last()]
            for t in range(4):
                k = ring.take()
                for c2 in range(2):
                    tok = mm(k.ap[:, 0:D], ct.ap[:, c2, t * 128:(t + 1) * 128], Wqkv[:, 3, c2, :], c2 == 0, c2 == 1, evs[c2], t_wd,
                             k.rel, inc=c2 == 1)
                tx2 = vtt(X[:, 4 * b + t, :], k.ap[:, 0:D], X[:, 4 * b + t, :], ALU.add, tok, s["txb"])
                k.rel = [tx2]
                s.setdefault("x", []).append(tx2)
                yield from pause(2)
            ct.rel = [tok]

        MZ.reset()
        QS = [MZ(128, 8, S, dt=F32R) for _ in range(2)]
        KS = [MZ(128, NH, S, dt=F32R) for _ in range(2)]
        VA = [Buf(MZ(128, 4, NH, 64, dt=F16), bar) for _ in range(2)]
        EZ = Zones(Zone(WA.start, 18 * K), Zone(SZ.start, 16 * K))
        E32 = Ring([EZ(128, 2, S) for _ in range(3)])
        EH = Ring([EZ(128, 2, S, dt=F16) for _ in range(LAG + 2)])
        EL = Ring([EZ(128, 2, S, dt=F16) for _ in range(LAG + 1)])
        LZ = Zone(bin_off, K)
        MT_off, QHL_off, CX_off = WA.start + 18 * K, MZ.at, MZ.at + 4 * K
        QHL = [Buf(MZ(128, 2, S, dt=F32R), bar)]
        CX = Buf(MZ(128, 4, D), bar)
        QHL.append(Buf(at(MZ.at, [128, 2, S], F32R), bar))
        XN_ = Buf(MZ(128, 4, D), bar)
        XTR = Ring([MZ(128, 2, S) for _ in range(1)])
        MT_ = Buf(at(MT_off, [128, S], F32R), bar)
        AZ = Zone(SZ.start + 16 * K, 3 * K)
        MXB = [AZ(128, 4, NH) for _ in range(2)]
        RC, RD = Ring([AZ(128, 4, 2, 1) for _ in range(2)]), Ring([AZ(128, 4, 2, 16) for _ in range(2)])
        ebias, zero = AZ(128, 1), AZ(128, 32)
        OS = Ring([at(Win_off, [128, S]), at(Wout_off, [128, S])])
        held((XTR, RC, RD), bar)
        krel, qrel = {}, {}
        tz0 = V(lambda e: e.memset(zero[:, :], 0.0), bar)
        tz = V(lambda e: e.memset(MT_.ap[32:33, :].bitcast(F32), 0.0), bar)
        t1row = V(lambda e: e.memset(MT_.ap[64:65, :].bitcast(F32), 1.0), bar)
        t_ln = V(lambda e: e.memset(ebias[:, :], LNES), bar)

        def clear(i, q, *w):
            qrel[i, 0] = qrel[i, 1] = [q(lambda e: e.memset(QS[i][:, :, :].bitcast(F32), 0.0), *w)]
            t0 = acopy(KS[i][:, :, :].rearrange("p h (a n) -> p (h a) n", n=32), zero[:, :].unsqueeze(1).to_broadcast([128, NH * 16, 32]), tz0, *w)
            for j in range(2):
                t0_ = dma(Y, f"one{i}", KS[i][64 * j + 48:64 * j + 49, :, :].bitcast(F32).rearrange(
                    "o (p j) n -> o p j n", j=2)[:, :, j, :],
                    MT_.ap[64:65, :].bitcast(F32).unsqueeze(1).to_broadcast([1, 8, S]), t0, t1row)
            krel[i, 0] = krel[i, 1] = [t0_]
            load_qk(i, "k")
            weave(load_v(i))

        bX, bM = banks([0]), banks([1, 2, 3])
        held((bX, bM), bar)
        st3 = {b: {} for b in range(NB)}
        nothing = lambda: iter(())

        def load_half(b, half):
            load_qk(b, "q", half)
            load_qk(b, "k", half)

        mix = [combine(b) for b in range(NB)]
        for g in mix:
            next(g)
        clear(0, V, bar)
        weave(mix[0])
        norms([0])
        beside(chain(*mix[1:]), (qprep(0), QR))
        norms([1, 2, 3])
        load_qk(0, "q")

        clear(1, G, [b.rel for b in GB.bufs])
        m0 = maxima(0)
        weave(islice(m0, 33))

        def second_q():
            yield from qprep(1)
            load_qk(1, "q")

        EZ1 = Zones(Zone(WA.start, 18 * K), Zone(SZ.start, 16 * K))
        KS_off, VA_off = MZ.start + 32 * K, MZ.start + 96 * K
        BZ = Zone(bc_off, 5 * K)
        rz = Zone(CX_off, 4 * K)
        b1m1, wgT, wgt = BZ(128, 32), BZ(16, E), BZ(E, 64)
        lgz1, top1, idxu1, idxf1 = BZ(128, NT, E), BZ(128, NT, 8), BZ(128, NT, 8), BZ(128, 1, NT)
        scr, pi_keep1, tei_keep1 = BZ(128, NT), BZ(128, 1, NT), [BZ(1, N1) for _ in range(3)]
        exz = BZ(128, NT, E)
        HL1 = at(MZ.start, [128, NT, 2 * D], F16)
        WZ = Zone(KS_off, 64 * K)
        W1 = Weights(WZ, E * 2 * H1, E * 2 * H1)
        SR1 = Ring([at(VA_off + 4 * K * i, [128, CH]) for i in range(2)])
        XT1, XR1 = Buf(at(QHL_off, [128, 2, S])), Buf(at(MT_off, [16, S]))
        dma(Y, "we", b1m1[:, :], a["b1m1"], txo)
        dma(Y, "we", wred[:, :, :], a["wred"])
        t_we = dma(Y, "we", wg8[:, :], a["L1_ffn_wg"])

        def wg_norm():
            c = V(lambda e: e.tensor_tensor(wgt[:, 0:16], wg8[:, :], wg8[:, :], ALU.mult), t_we, txo)
            c = V(lambda e: e.tensor_reduce(wgt[:, 16:17], wgt[:, 0:16], AX.X, ALU.add), c)
            y, c = rsqrt(wgt[:, 16:17], 1, wgt[:, 20:24], c, parts=E)
            c = vtt(wgt[:, 17:18], wgt[:, 16:17], y, ALU.mult, c)
            c = vts(wgt[:, 17:18], wgt[:, 17:18], 1e-4, None, ALU.max, ALU.bypass, c)
            c = V(lambda e: e.reciprocal(wgt[:, 18:19], wgt[:, 17:18]), c)
            c = vts(wgt[:, 32:48], wg8[:, :], wgt[:, 18:19], None, ALU.mult, ALU.bypass, c)
            k = bM.take()
            tok = tr(k.ap[0:16, 0:E], wgt[:, 32:48], ident[0:E, 0:E], c, k.rel, inc=True)
            t_wg = vcopy(wgT[:, :], k.ap[0:16, 0:E], tok)
            k.rel = [t_wg]
            return t_wg

        def gate(b):
            xn, xt, xr = XN_, XT1, XR1
            sc, tk = ln_stats([X[:, 4 * b + t, :] for t in range(4)], BZ, st3[b]["x"])
            for t in range(4):
                c = vts(xn.ap[:, t, :], X[:, 4 * b + t, :], *sc[t], ALU.subtract, ALU.mult, tk, xn.rel)
            yield from pause(GAP)
            hs = HL1[:, 4 * b:4 * b + 4, :]
            for c2 in range(2):
                ev = transpose4(bM, [xn.ap[:, t, c2 * 128:(c2 + 1) * 128] for t in range(4)],
                                lambda k, tok: acopy(xt.ap[:, c2, :], k, tok, xt.rel), c)
                yield from pause(GAP)
            tc_ = acopy(hs[:, :, 0:D], xn.ap, c, bar3)
            tl = vtt(hs[:, :, D:2 * D], xn.ap, hs[:, :, 0:D], ALU.subtract, tc_, q=G)
            xn.rel = [T.last(), tl]
            k = bM.take()
            for c2 in range(2):
                tok = mm(k.ap[0:16, :], wred[:, c2, :], xt.ap[:, c2, :], c2 == 0, c2 == 1, ev, t_we, k.rel, inc=c2 == 1)
            xt.rel = [tok]
            yield
            ex = acopy(xr.ap, k.ap[0:16, :], tok, xr.rel)
            k.rel = [ex]
            yield from pause(GAP)
            k = bM.take()
            for t in range(4):
                tok = mm(k.ap[:, t * E:(t + 1) * E], xr.ap[:, t * 128:(t + 1) * 128], wgT[:, :], True, True, ex, t_wg, k.rel, inc=t == 3)
            xr.rel = [tok]
            yield
            c = vcopy(lgz1[:, 4 * b:4 * b + 4, :], k.ap[:, 0:4 * E].rearrange("p (t e) -> p t e", e=E), tok)
            k.rel = [c]
            for t in range(4):
                tt = 4 * b + t
                cm = V(lambda e, tt=tt: e.max(top1[:, tt, :], lgz1[:, tt, :]), c)
            for t in range(4):
                tt = 4 * b + t
                ci = V(lambda e, tt=tt: e.max_index(idxu1[:, tt, :].bitcast(U32), top1[:, tt, :], lgz1[:, tt, :]), cm)
            st[b]["i"], st[b]["hl"] = ci, tl
            yield from pause(GAP)

        def gates(bs):
            for b in bs:
                yield from gate(b)

        def up_weights():
            SR1.bufs[0].rel = SR1.bufs[1].rel = VA[0].rel
            yield from keep(split_weights(a["w1m1"], W1.w1h, W1.w1l, E * 2 * H1, SR1, "wn", bar3), W1.t1)

        bO = [Ring([PB[0][64 * j:64 * j + 64, 512:1024]]) for j in range(2)]
        bM, bS = banks([2, 3]), pairs([2, 3])
        held((*bO, bM, bS, E32, EH, EL, OS), everyone())
        for b in range(NB):
            if 1 <= b < NB - 1:
                load_half(b + 1, 1)
            last = b + 1 == NB and stop > 3
            if b + 1 == NB:
                bar3 = everyone()
                held((SR1,), bar3)
                XT1.rel = XR1.rel = bar3
                t_wg = wg_norm()
            beside(attend(b, SH if b + 1 < NB else SH3),
                   (chain(st3[b - 1]["tail"] if b else nothing(), load_v(b + 1) if 1 <= b < NB - 1 else nothing(),
                          second_q() if b == 0 else nothing(),
                          qprep(b + 2) if b + 2 < NB else nothing(),
                          up_weights() if last else nothing()), 1.0 if b else R0),
                   (gates(range(NB - 1)) if last else chain(nothing() if b else m0, maxima(b + 1, b + 2 if b + 2 < NB else None))
                    if b + 1 < NB else nothing(), RATE if b else RATE0))
        if stop == 3:
            weave(st3[NB - 1]["tail"])
            finish()
            emit()
            return

        b2m1 = EZ1(128, E * D)
        bar = everyone()
        t_b2 = dma(Y, "wf", b2m1[:, :], a["L1_ffn_b2"].rearrange("e d -> (e d)").partition_broadcast(128), bar)
        SR2 = Ring([at(VA_off + 4 * K * i, [128, CH]) for i in range(4)])
        down = keep(split_weights(a["w2m1"], W1.w2h, W1.w2l, E * 2 * H1, SR2, "wo", bar), W1.t2)
        flush = st3[NB - 1]["tail"]
        for _ in range(LAG):
            next(flush)
        held((SR2,), [*bar, T.last(), V.last()])
        next(down)
        weave(chain(flush, gates([NB - 1])))
        bY = banks([4, 5, 6, 7])
        held((bY,), bar)
        cis, hls = [st[b]["i"] for b in range(NB)], [st[b]["hl"] for b in range(NB)]
        c = vcopy(idxf1[:, :, :], idxu1[:, :, 0:1].bitcast(U32).rearrange("p t s -> p s t"), cis)
        c1 = vtt(exz[:, :, :], lgz1[:, :, :], top1[:, :, 0:1].to_broadcast([128, NT, E]), ALU.subtract, cis)
        c1 = act(exz[:, :, :], exz[:, :, :], ACT.Exp, c1)
        c1 = V(lambda e: e.tensor_reduce(scr[:, :], exz[:, :, :], AX.X, ALU.add), c1)
        tsc1 = V(lambda e: e.reciprocal(scr[:, :], scr[:, :]), c1)
        rr = list(routing(1, idxf1, N1, rz, c, t_wb))
        rr[10], rr[12] = tei_keep1, pi_keep1
        pi1, tei1, te1, tpos = positions(1, rr, 4)
        tsc = scatter(buf1, HL1, pi1, 1, "sc1", tpos, hls, tzero1)
        weave(down)
        tout = experts(EZ1, buf1, obuf1, N1, 4, W1, ACT.Gelu, b1m1, b2m1, tei1, "e1", tsc, te1, tpos, tsc1, t_we, t_b2, W1.t1, W1.t2, deep=True)
        GB = Ring([at(MZ.start + 16 * K + K * i, [128, D]) for i in range(NT)])
        ov = out.rearrange("b (t p) d -> p (b t) d", p=128)
        for t in range(NT):
            g = GB.take()
            tg = gather(obuf1, pi1, 0, t, g.ap, f"g1{GB.at % NT}", tout, g.rel)
            c = vstt(X[:, t, :], g.ap, scr[:, t:t + 1], X[:, t, :], ALU.mult, ALU.add, tg, tsc1)
            g.rel = [c]
            if t % 4 == 3:
                to = dma(Y, "out", ov[:, t - 3:t + 1, :], X[:, t - 3:t + 1, :], c)
        Y(lambda e: e.wait_ge(*to), inc=False)
        emit()


def layouts(v):
    f = np.float32
    c = np.ascontiguousarray

    def kmaj(w, k):
        return c(w.reshape(k, 128, w.shape[-1]).transpose(1, 0, 2))

    def heads(w):
        return w.reshape(-1, 4, 2, 2, 16).transpose(0, 2, 3, 4, 1).reshape(w.shape)

    d = {}
    for n in ("x", "ctx_1024", "L0_xattn_ln_g", "L0_xattn_ln_b", "L0_xattn_b_diff", "L0_xattn_b2", "L0_ffn_b_out",
              "L1_xattn_bo", "L1_xattn_bv", "L0_ffn_b_in", "L0_ffn_b_gate"):
        d[n] = c(v[n])
    d["ident"] = np.eye(128, dtype=f)
    d["U"] = np.triu(np.ones((128, 128), f), 1)
    d["io8"] = np.broadcast_to(np.arange(8, dtype=f), (128, 8)).copy()
    d["ioj"] = np.broadcast_to(np.arange(32, dtype=f), (128, 32)).copy()
    d["WdT"] = kmaj(v["L0_xattn_W_diff"].T, 2)
    d["W1T"] = kmaj(v["L0_xattn_W1"].T, 2)
    d["W2T"] = kmaj(v["L0_xattn_W2"].T, 8)
    pp = np.zeros((128, 16), f)
    pp[:, 0:2] = v["L0_xattn_ln_g"].reshape(2, 128).T
    pp[:, 2:4] = v["L0_xattn_ln_b"].reshape(2, 128).T
    pp[:, 4:12] = v["L0_xattn_b1"].reshape(8, 128).T
    pp[:, 12:14] = heads(v["L1_xattn_bq"]).reshape(2, 128).T
    pp[:, 14:16] = heads(v["L1_xattn_bk"]).reshape(2, 128).T
    d["pp"] = pp
    d["Win"] = kmaj(v["L0_ffn_W_in"], 2)
    d["Wg"] = kmaj(v["L0_ffn_W_gate"], 2)
    d["Wout"] = kmaj(v["L0_ffn_W_out"], 2)
    d["L0_ffn_b2"] = c(v["L0_ffn_b2"])
    d["w1m0"] = c(v["L0_ffn_W1"].reshape(8, 2, 128, H0).transpose(2, 0, 1, 3).reshape(128, -1))
    d["w2m0"] = c(v["L0_ffn_W2"].reshape(8, 8, 128, D).transpose(2, 0, 1, 3).reshape(128, -1))
    d["ctxT"] = c(v["ctx_1024"].reshape(NB, S, 2, 128).transpose(0, 3, 2, 1))
    d["Wqkv"] = c(np.stack([kmaj(w, 2) for w in (heads(v["L1_xattn_Wq"]), heads(v["L1_xattn_Wk"]), v["L1_xattn_Wv"],
                                                  v["L1_xattn_Wo"])], 1))
    d["wred"] = kmaj(v["L1_ffn_w_red"], 2)
    d["L1_ffn_wg"], d["L1_ffn_b2"] = c(v["L1_ffn_wg"]), c(v["L1_ffn_b2"])
    d["w1m1"] = c(v["L1_ffn_W1"].reshape(8, 2, 128, H1).transpose(2, 0, 1, 3).reshape(128, -1))
    d["w2m1"] = c(v["L1_ffn_W2"].reshape(8, 4, 128, D).transpose(2, 0, 1, 3).reshape(128, -1))
    d["b1m1"] = c(v["L1_ffn_b1"].reshape(32, 128).T)
    d["b1m0"] = c(v["L0_ffn_b1"].reshape(64, 128).T)
    return d


def kernel(**inputs):
    import concourse.bacc as bacc
    from concourse.bass_utils import run_bass_kernel_spmd

    arrays = layouts({n: np.asarray(x) for n, x in inputs.items()})
    nc = bacc.Bacc("TRN2", target_bir_lowering=False, num_devices=1)
    aps = {n: nc.dram_tensor("in_" + n, x.shape, mybir.dt.from_np(x.dtype), kind="ExternalInput").ap()
           for n, x in arrays.items()}
    out = nc.dram_tensor("out_0", (NB, S, D), F32, kind="ExternalOutput").ap()
    build(nc, aps, out)
    r = run_bass_kernel_spmd(nc, [{"in_" + n: x for n, x in arrays.items()}], core_ids=[0])
    return r.results[0]["out_0"]
```
